# Optimizing a Trainium2 kernel written in Bass

```python
import numpy as np
import jax
import jax.numpy as jnp

def _softmax(x, axis=-1):
    return jax.nn.softmax(x, axis=axis)

def _gelu(x):
    return jax.nn.gelu(x, approximate=True)

def _silu(x):
    return jax.nn.silu(x)

def _sigmoid(x):
    return jax.nn.sigmoid(x)

def _layernorm(x, axis=-1, eps=1e-05):
    m = jnp.mean(x, axis=axis, keepdims=True)
    v = jnp.var(x, axis=axis, keepdims=True)
    return (x - m) / jnp.sqrt(v + eps)

def _scatter_add(tgt, idx, src, axis=0):
    return tgt.at[idx].add(src)

def _segment_sum(src, seg, n):
    return jax.ops.segment_sum(src, seg, n)
kernel_name = 'mk_gps_d1_gnn_r8_1a441d'

def setup_inputs(seed: int=0):
    np.random.seed(seed)
    _w = jnp.asarray

    def _rec_inputs():
        import jax
        import jax.numpy as jnp
        _gk = jax.random.key(seed)
        x = -0.0003713 + 1 * jax.random.normal(jax.random.fold_in(_gk, 1), (6250, 256), jnp.float32)
        src = jax.random.randint(jax.random.fold_in(_gk, 2), (100000,), 0, 6250, jnp.int32)
        dst = jnp.minimum((6250 * jax.random.uniform(jax.random.fold_in(_gk, 3), (100000,)) ** 2.0).astype(jnp.int32), 49999)
        _o = jnp.argsort(dst, stable=True)
        src = src[_o]
        dst = dst[_o]
        return (x, src, dst)
    x, src, dst = _rec_inputs()

    def _L0_gnn_setup():
        import jax, jax.numpy as jnp
        import numpy as np
        N, IN_CH, HEADS, OUT_CH, E = (6250, 256, 4, 64, 100000)
        key = jax.random.key(seed)
        k1, k2, k3, k4, k5 = jax.random.split(key, 5)
        x = jax.random.normal(k1, (N, IN_CH), dtype=jnp.float32)
        edge_index = jax.random.randint(k2, (2, E), 0, N, dtype=jnp.int64)
        bw = float(np.sqrt(6.0 / (IN_CH + HEADS * OUT_CH)))
        ba = float(np.sqrt(6.0 / (HEADS + OUT_CH)))
        weight = jax.random.uniform(k3, (IN_CH, HEADS * OUT_CH), jnp.float32, -bw, bw)
        attn_l = jax.random.uniform(k4, (HEADS, OUT_CH), jnp.float32, -ba, ba)
        attn_r = jax.random.uniform(k5, (HEADS, OUT_CH), jnp.float32, -ba, ba)
        return {'x': x, 'edge_index': edge_index, 'weight': weight, 'attn_l': attn_l, 'attn_r': attn_r}
    _L0_gnn_all = _L0_gnn_setup()
    _L0_gnn_in = {k: v for k, v in _L0_gnn_all.items() if k in ('weight', 'attn_l', 'attn_r')}
    del _L0_gnn_all

    def _L0_mix_setup():
        import jax, jax.numpy as jnp
        import numpy as np
        HEADS, DIM_HEAD = (8, 64)
        EPS = 1e-05

        def instance_norm(t):
            mu = jnp.mean(t, axis=-1, keepdims=True)
            var = jnp.mean((t - mu) ** 2, axis=-1, keepdims=True)
            return (t - mu) * jax.lax.rsqrt(var + EPS)
        key = jax.random.key(seed)
        k1, k2, k3, k4 = jax.random.split(key, 4)
        B, N, D = (8, 1024, 256)
        inner = HEADS * DIM_HEAD
        x = jax.random.normal(k1, (B, N, D), jnp.float32)
        w_qkv = jax.random.normal(k2, (3 * inner, D), jnp.float32) / np.sqrt(D).astype(np.float32)
        w_out = jax.random.normal(k3, (D, inner), jnp.float32) / np.sqrt(inner).astype(np.float32)
        b_out = 0.01 * jax.random.normal(k4, (D,), jnp.float32)
        return {'x': x, 'w_qkv': w_qkv, 'w_out': w_out, 'b_out': b_out}
    _L0_mix_all = _L0_mix_setup()
    _L0_mix_in = {k: v for k, v in _L0_mix_all.items() if k in ('w_qkv', 'w_out', 'b_out')}
    del _L0_mix_all

    def _L0_ffn_setup():
        import jax, jax.numpy as jnp
        import numpy as np
        E, D, H, TOP_K = (6, 256, 256, 2)
        ROUTER_H = D // 2
        key = jax.random.key(seed)
        ks = jax.random.split(key, 12)
        s = 1.0 / np.sqrt(D)
        sh = 1.0 / np.sqrt(H)
        sr = 1.0 / np.sqrt(ROUTER_H)
        return {'features': jax.random.normal(ks[0], (8, 512, D), dtype=jnp.float32), 'router_w1': jax.random.uniform(ks[1], (D, ROUTER_H), jnp.float32, -s, s), 'router_b1': jnp.zeros((ROUTER_H,), jnp.float32), 'router_w2': jax.random.uniform(ks[2], (ROUTER_H, E), jnp.float32, -sr, sr), 'router_b2': jnp.zeros((E,), jnp.float32), 'expert_w1': jax.random.uniform(ks[3], (E, D, H), jnp.float32, -s, s), 'expert_b1': jnp.zeros((E, H), jnp.float32), 'expert_w2': jax.random.uniform(ks[4], (E, H, H), jnp.float32, -sh, sh), 'expert_b2': jnp.zeros((E, H), jnp.float32), 'expert_w3': jax.random.uniform(ks[5], (E, H, D), jnp.float32, -sh, sh), 'expert_b3': jnp.zeros((E, D), jnp.float32)}
    _L0_ffn_all = _L0_ffn_setup()
    _L0_ffn_in = {k: v for k, v in _L0_ffn_all.items() if k in ('router_w1', 'router_b1', 'router_w2', 'router_b2', 'expert_w1', 'expert_b1', 'expert_w2', 'expert_b2', 'expert_w3', 'expert_b3')}
    del _L0_ffn_all
    return {'x': x, 'src': src, 'dst': dst, 'L0_gnn_weight': _L0_gnn_in['weight'], 'L0_gnn_attn_l': _L0_gnn_in['attn_l'], 'L0_gnn_attn_r': _L0_gnn_in['attn_r'], 'L0_mix_w_qkv': _L0_mix_in['w_qkv'], 'L0_mix_w_out': _L0_mix_in['w_out'], 'L0_mix_b_out': _L0_mix_in['b_out'], 'L0_ffn_router_w1': _L0_ffn_in['router_w1'], 'L0_ffn_router_b1': _L0_ffn_in['router_b1'], 'L0_ffn_router_w2': _L0_ffn_in['router_w2'], 'L0_ffn_router_b2': _L0_ffn_in['router_b2'], 'L0_ffn_expert_w1': _L0_ffn_in['expert_w1'], 'L0_ffn_expert_b1': _L0_ffn_in['expert_b1'], 'L0_ffn_expert_w2': _L0_ffn_in['expert_w2'], 'L0_ffn_expert_b2': _L0_ffn_in['expert_b2'], 'L0_ffn_expert_w3': _L0_ffn_in['expert_w3'], 'L0_ffn_expert_b3': _L0_ffn_in['expert_b3']}

def reference(x, src, dst, L0_gnn_weight, L0_gnn_attn_l, L0_gnn_attn_r, L0_mix_w_qkv, L0_mix_w_out, L0_mix_b_out, L0_ffn_router_w1, L0_ffn_router_b1, L0_ffn_router_w2, L0_ffn_router_b2, L0_ffn_expert_w1, L0_ffn_expert_b1, L0_ffn_expert_w2, L0_ffn_expert_b2, L0_ffn_expert_w3, L0_ffn_expert_b3):
    import jax
    import jax.numpy as jnp

    def _L0_gnn_ref(x, edge_index, weight, attn_l, attn_r):
        import jax, jax.numpy as jnp
        import numpy as np
        N, IN_CH, HEADS, OUT_CH, E = (6250, 256, 4, 64, 100000)
        heads, out_ch = attn_l.shape
        n = x.shape[0]
        xt = jnp.matmul(x, weight).reshape(-1, heads, out_ch)
        row, col = (edge_index[0], edge_index[1])
        alpha_l = jnp.einsum('ehd,hd->eh', xt[row], attn_l)
        alpha_r = jnp.einsum('ehd,hd->eh', xt[col], attn_r)
        alpha = jax.nn.softmax(jax.nn.leaky_relu(alpha_l + alpha_r, 0.01), axis=1)
        tmp = jnp.einsum('nh,nhd->nd', alpha[:n], xt[col[:n]])
        out = jnp.broadcast_to(tmp[:, None, :], (n, heads, out_ch))
        return out.reshape(n, heads * out_ch)

    def _L0_mix_ref(x, w_qkv, w_out, b_out):
        import jax, jax.numpy as jnp
        import numpy as np
        HEADS, DIM_HEAD = (8, 64)
        EPS = 1e-05

        def instance_norm(t):
            mu = jnp.mean(t, axis=-1, keepdims=True)
            var = jnp.mean((t - mu) ** 2, axis=-1, keepdims=True)
            return (t - mu) * jax.lax.rsqrt(var + EPS)
        B, N, _ = x.shape
        H, Dh = (HEADS, DIM_HEAD)
        qkv = jnp.einsum('bnd,ed->bne', x, w_qkv)
        q, k, v = jnp.split(qkv, 3, axis=-1)

        def to_heads(t):
            return t.reshape(B, N, H, Dh).transpose(0, 2, 1, 3)
        q, k, v = (to_heads(q), to_heads(k), to_heads(v))
        k = instance_norm(k)
        v = instance_norm(v)
        dots = jnp.einsum('bhnd,bhne->bhde', k, v)
        out = jnp.einsum('bhnd,bhde->bhne', q, dots) / N
        out = out.transpose(0, 2, 1, 3).reshape(B, N, H * Dh)
        return jnp.einsum('bne,de->bnd', out, w_out) + b_out

    def _L0_ffn_ref(features, router_w1, router_b1, router_w2, router_b2, expert_w1, expert_b1, expert_w2, expert_b2, expert_w3, expert_b3):
        import jax, jax.numpy as jnp
        import numpy as np
        E, D, H, TOP_K = (6, 256, 256, 2)
        ROUTER_H = D // 2
        rh = jax.nn.relu(features @ router_w1 + router_b1)
        expert_logits = jax.nn.softmax(rh @ router_w2 + router_b2, axis=-1)
        top_w, top_i = jax.lax.top_k(expert_logits, TOP_K)
        routing_weights = jax.nn.softmax(top_w, axis=-1)
        h1 = jax.nn.relu(jnp.einsum('bsd,edh->bseh', features, expert_w1) + expert_b1)
        h2 = jax.nn.relu(jnp.einsum('bseh,ehf->bsef', h1, expert_w2) + expert_b2)
        expert_out = jnp.einsum('bsef,efo->bseo', h2, expert_w3) + expert_b3
        sel = jnp.take_along_axis(expert_out, top_i[:, :, :, None], axis=2)
        combined = jnp.sum(sel * routing_weights[..., None], axis=2)
        return combined
    edge_index = jnp.stack([src, dst])
    xn = _layernorm(x, axis=-1)
    x = x + _L0_gnn_ref(xn, edge_index, L0_gnn_weight, L0_gnn_attn_l, L0_gnn_attn_r) + _L0_mix_ref(xn[None], L0_mix_w_qkv, L0_mix_w_out, L0_mix_b_out)[0]
    x = x + _L0_ffn_ref(_layernorm(x, axis=-1)[None], L0_ffn_router_w1, L0_ffn_router_b1, L0_ffn_router_w2, L0_ffn_router_b2, L0_ffn_expert_w1, L0_ffn_expert_b1, L0_ffn_expert_w2, L0_ffn_expert_b2, L0_ffn_expert_w3, L0_ffn_expert_b3)[0]
    return x

_drawn_inputs = setup_inputs


def setup_inputs(seed=0):
    import zlib

    import numpy as np

    out = dict(_drawn_inputs(seed))
    spreads = {'L0_ffn_router_b1': (0.0, 0.27),
     'L0_ffn_router_b2': (0.0, 0.1),
     'L0_ffn_expert_b1': (0.0, 0.8),
     'L0_ffn_expert_b2': (0.0, 0.373),
     'L0_ffn_expert_b3': (0.0, 0.1)}
    factors = {'L0_mix_b_out': 5.998}
    for name, (base, spread) in spreads.items():
        noise = np.random.default_rng([zlib.crc32(name.encode()), seed]).standard_normal(out[name].shape)
        drawn = base * np.exp(spread * noise) if base else spread * noise
        out[name] = jnp.asarray(drawn.astype(out[name].dtype))
    for name, factor in factors.items():
        out[name] = (out[name] * factor).astype(out[name].dtype)
    return out
```

```python
import concourse.bass as bass
from concourse import mybir
from contextlib import ExitStack

FP32 = mybir.dt.float32
FP32R = mybir.dt.float32r
I32 = mybir.dt.int32
ALU = mybir.AluOpType
ACT = mybir.ActivationFunctionType
AX = mybir.AxisListType

N, D = 6250, 256
GH, GC = 4, 64
MH, MC = 8, 64
MI = MH * MC
E, F, RH = 6, 256, 128
EPS = 1e-5

P = 125
T = N // P
G = 10
ITERS = T // G
KC = D // 128
AHEAD = 7
HALF = G // 2
XTW = D + GH
GW = D + 2 * GH

S = 128
REG = N + S
EP = 8
NT = (N + E * (S - 1)) // S
LEAD = 3
U = 9
ROW = D + 6
C_NMR, C_R, C_W, C_TOK, C_POS = D, D + 1, D + 2, D + 4, D + 5
ROW1 = D + ROW
SKIP = 1 << 20
LW = KC * F
EW = 3 * LW

ORDER = [("product", 1, 0), ("transpose", 0, 2), ("product", 1, 1), ("transpose", 1, 0),
         ("product", 1, 2), ("transpose", 1, 1), ("product", 2, 0), ("transpose", 1, 2),
         ("product", 2, 1), ("transpose", 2, 0), ("product", 2, 2), ("transpose", 2, 1),
         ("product", 3, 0), ("transpose", 2, 2), ("product", 3, 1), ("transpose", 0, 0),
         ("product", 3, 2), ("transpose", 0, 1)]

PREP_EPS, PREP_X, PREP_ALL = 1, 3, 27


def gps_layer(nc, x, src, dst, w_kv, w_q, w_oT, b_out, w_g, a_l, a_r, rw1, rb1, rw2, rb2,
              ew1, eb1, ew2, eb2, ew3, eb3, out):
    ctx = ExitStack()
    with ctx:
        def sb(name, shape, dt=FP32):
            return ctx.enter_context(nc.sbuf_tensor(name, shape, dt))

        def sem(name):
            return ctx.enter_context(nc.semaphore(name))

        xt_tab = nc.dram_tensor("xt_tab", (N, XTW), FP32, kind="Internal").ap()
        al_tab = nc.dram_tensor("al_tab", (N, GH), FP32, kind="Internal").ap()
        tab0 = nc.dram_tensor("tab0", (E * REG + S, ROW), FP32, kind="Internal").ap()
        tab1 = nc.dram_tensor("tab1", (E * REG + S, ROW1), FP32, kind="Internal").ap()

        ident = sb("ident", [128, 128])
        tri = sb("tri", [P, P])
        ones = sb("ones", [P, P])
        ebase = sb("ebase", [P, 2, EP])
        desc = sb("desc", [P, EP])
        tok_all = sb("tok_all", [P, T], I32)
        wkv_h, wkv_l = sb("wkv_h", [128, KC, 2 * MI], FP32R), sb("wkv_l", [128, KC, 2 * MI], FP32R)
        wg_h, wg_l = sb("wg_h", [128, KC, GW], FP32R), sb("wg_l", [128, KC, GW], FP32R)
        wq_sb = sb("wq_sb", [128, MI // 128, D])
        woT_sb = sb("woT_sb", [128, MI // 128, D])
        mix_w = sb("mix_w", [128, KC, D])
        bo_sb = sb("bo_sb", [P, D])
        rw1_sb = sb("rw1_sb", [128, KC, RH])
        rb1_sb = sb("rb1_sb", [RH, 1])
        rw2_sb = sb("rw2_sb", [RH, EP])
        rb2_sb = sb("rb2_sb", [P, EP])
        we_h, we_l = sb("we_h", [128, E * EW], FP32R), sb("we_l", [128, E * EW], FP32R)
        be_sb = sb("be_sb", [128, E * 2 * F])
        b3_hl = sb("b3_hl", [128, E * D], FP32R)
        sel_hl = sb("sel_hl", [128, S], FP32R)
        src_all, dst_all = sb("src_all", [P, T], I32), sb("dst_all", [P, T], I32)
        raw_e = sb("raw_e", [128, EW])
        skip_rows = sb("skip_rows", [S, ROW1])
        eps_sb = sb("eps_sb", [128, 1])

        arena = sb("arena", [128, U * ROW1])
        xring = sb("xring", [P, G, D])
        xn = sb("xn", [P, 2, D])
        x_h, x_l = sb("x_h", [128, 3, KC, 128], FP32R), sb("x_l", [128, 3, KC, 128], FP32R)
        st = sb("st", [P, G, 6])
        mv = sb("mv", [P, G, 2])
        sd = sb("sd", [P, G])
        rs = sb("rs", [P, G])
        nmr = sb("nmr", [P, G])
        rs_all, nmr_all = sb("rs_all", [P, T + G]), sb("nmr_all", [P, T + G])
        work = sb("work", [128, 6 * MI])

        kv_raw = arena[:, 0:KC * 2 * MI].rearrange("p (c n) -> p c n", c=KC)
        g_at = KC * 2 * MI
        wg_raw = arena[:, g_at:g_at + KC * GW].rearrange("p (c n) -> p c n", c=KC)
        att_bc = arena[:, g_at + KC * GW:g_at + KC * GW + 2 * D].rearrange("p (s n) -> p s n", s=2)
        att_pr = work[:, 0:KC * D].rearrange("p (c n) -> p c n", c=KC)
        kv_mean = work[:, 2 * MI:2 * MI + KC * 2 * MH].rearrange("p (c h) -> p c h", c=KC)
        b3_raw = work[:, 2 * MI + 64:2 * MI + 64 + E * D]
        xts = arena[0:P, 0:G * GW].rearrange("p (g n) -> p g n", g=G)
        sq = work[0:P, 0:2 * MI]
        ks = work[0:P, 2 * MI:4 * MI].rearrange("p (b n) -> p b n", b=2)
        vs = work[0:P, 4 * MI:6 * MI].rearrange("p (b n) -> p b n", b=2)
        ss = sb("ss", [P, 2 * MH])
        sse = sb("sse", [P, 2 * MH])
        pr = sb("pr", [P, MH])
        sr = sb("sr", [P, MH])
        rkv = sb("rkv", [P, MH])

        dotsT = sb("dotsT", [128, MI // 128, 128])
        a_sb = work[:, 0:(MI // 128) * D].rearrange("p (b n) -> p b n", b=MI // 128)

        xtg = arena[0:P, 0:G * XTW].rearrange("p (g n) -> p g n", g=G)
        gp = arena[0:P, G * XTW:G * XTW + 2 * D].rearrange("p (b n) -> p b n", b=2)
        gt = arena[0:P, G * XTW + 2 * D:G * XTW + 2 * D + 2 * GC].rearrange("p (b n) -> p b n", b=2)
        y1 = arena[0:P, G * XTW + 3 * D:G * XTW + 5 * D].rearrange("p (b n) -> p b n", b=2)
        y2 = arena[0:P, G * XTW + 5 * D:G * XTW + 7 * D].rearrange("p (b n) -> p b n", b=2)
        xr = work[0:P, 0:G * ROW].rearrange("p (g n) -> p g n", g=G)
        xT = sb("xT", [128, 2, KC, 128])
        rhT = sb("rhT", [RH, 2, P])
        alg = sb("alg", [P, G, GH])
        al = sb("al", [P, 4, G, GH])
        am = sb("am", [P, 3, G])
        idx_s, idx_d = sb("idx_s", [P, G], I32), sb("idx_d", [P, G], I32)
        lg = sb("lg", [P, 4, G, EP])
        oh = sb("oh", [P, G, 2, EP])
        rk = sb("rk", [P, G, 2, EP])
        tw = sb("tw", [P, 10, G])
        posf = sb("posf", [P, G, 2])
        pos0 = sb("pos0", [P, G], I32)
        base = sb("base", [P, 2, EP])
        bsum = sb("bsum", [P, 2, EP])

        NTT = NT + LEAD
        NM = -(-N // S)
        cnt = sb("cnt", [1, 2, EP])
        nmul = sb("nmul", [1, NM])
        ntl = sb("ntl", [1, 2, EP])
        ncmp = arena[0:1, 0:2 * EP * NM].rearrange("p (k e m) -> p k e m", k=2, e=EP)
        ends = sb("ends", [1, 2, EP])
        jj = sb("jj", [1, NTT])
        ge = arena[0:1, 1024:1024 + 2 * NTT * E].rearrange("p (k j e) -> p k j e", k=2, j=NTT)
        gn = arena[0:1, 2048:2048 + 2 * NTT * E].rearrange("p (k j e) -> p k j e", k=2, j=NTT)
        tf = sb("tf", [1, 8, 2, NTT])
        tab_row, tab_e = sb("tab_row", [1, 2, NTT], I32), sb("tab_e", [1, 2, NTT], I32)
        fillf = sb("fillf", [1, 2, EP])
        fill = sb("fill", [1, 2, EP], I32)

        rb = arena[:, :].rearrange("p (u n) -> p u n", u=U)
        xe = sb("xe", [S, 3, D])
        hs = sb("hs", [S, 3, D])

        kv_ps = [ctx.enter_context(nc.psum_tensor(f"kv_ps{b}", [128, 2 * MI], FP32)) for b in range(2)]
        pt = [ctx.enter_context(nc.psum_tensor(f"pt{b}", [128, 512], FP32)) for b in range(2)]
        xt_ps = ctx.enter_context(nc.psum_tensor("xt_ps", [128, 512], FP32))
        d_ps = ctx.enter_context(nc.psum_tensor("d_ps", [128, 512], FP32))

        def half_t(bank):
            return bank[:, 0:KC * 128].rearrange("p (c n) -> p c n", c=KC)

        ma_ps = [kv_ps[0][:, 0:512], kv_ps[0][:, 512:1024]]
        rh_ps = [kv_ps[1][:, 0:512], kv_ps[1][:, 512:1024]]
        lg_ps = xt_ps[0:P, 0:G * EP].rearrange("p (g e) -> p g e", g=G)
        rk_ps = d_ps[0:P, 0:G * 2 * EP].rearrange("p (g k e) -> p g k e", g=G, k=2)
        t_ps = [pt[0], pt[1], xt_ps]
        l_ps = [kv_ps[0][:, 0:512], kv_ps[0][:, 512:1024], kv_ps[1][:, 0:512]]

        x_in = [sem(f"x_in{g}") for g in range(G)]
        w1_in, w2_in, b3_in, raw_in = sem("w1_in"), sem("w2_in"), sem("b3_in"), sem("raw_in")
        pool_c, prep = sem("pool_c"), sem("prep")
        split_h, split_l = sem("split_h"), sem("split_l")
        bs_done, ag_done, sd_done, fin_done = sem("bs_done"), sem("ag_done"), sem("sd_done"), sem("fin_done")
        xn_ready, pt_ready, xh_ready, xl_ready = sem("xn_ready"), sem("pt_ready"), sem("xh_ready"), sem("xl_ready")
        k_ready, v_ready, xt_ready = sem("k_ready"), sem("v_ready"), sem("xt_ready")
        sqk_done, sqv_done, red_done, sse_done = sem("sqk_done"), sem("sqv_done"), sem("red_done"), sem("sse_done")
        pr_done, sr_done, rc_done = sem("pr_done"), sem("sr_done"), sem("rc_done")
        ks_ready, xts_done, dots_done = sem("ks_ready"), sem("xts_done"), sem("dots_done")
        xt_out = [sem(f"xt_out{h}") for h in range(2)]
        dT_done, a_done, as_done, m_done, mw_done = (sem("dT_done"), sem("a_done"), sem("as_done"),
                                                     sem("m_done"), sem("mw_done"))
        idx_done = sem("idx_done")
        g_in = [sem(f"g_in{g}") for g in range(G)]
        rs2_done, al_step, al_ready, ex_done = sem("rs2_done"), sem("al_step"), sem("al_ready"), sem("ex_done")
        xn1_done, t1_done, xT1_done, ma_done = sem("xn1_done"), sem("t1_done"), sem("xT1_done"), sem("ma_done")
        gp_done, gt_done, y1_done, y2_done, x2_done = (sem("gp_done"), sem("gt_done"), sem("y1_done"),
                                                       sem("y2_done"), sem("x2_done"))
        bs2_done, ag2_done, sd2_done, fin2_done = sem("bs2_done"), sem("ag2_done"), sem("sd2_done"), sem("fin2_done")
        xn2_done, t2_done, xT2_done = sem("xn2_done"), sem("t2_done"), sem("xT2_done")
        rh_done, rhT_done, lg_done = sem("rh_done"), sem("rhT_done"), sem("lg_done")
        step, lgx_ready, ex2_done, d_ready, ex3_done = (sem("step"), sem("lgx_ready"), sem("ex2_done"),
                                                        sem("d_ready"), sem("ex3_done"))
        oh_ready, rk_done, row_ready = sem("oh_ready"), sem("rk_done"), sem("row_ready")
        sc_out = [sem(f"sc_out{g}") for g in range(G)]
        cnt_done, tstep, tab_done, fill_out = sem("cnt_done"), sem("tstep"), sem("tab_done"), sem("fill_out")
        r_in = [sem(f"r_in{u}") for u in range(U)]
        xe_done, et_done, eh_done, el_done = sem("xe_done"), sem("et_done"), sem("eh_done"), sem("el_done")
        l_done, hs_done, z_done = sem("l_done"), sem("hs_done"), sem("z_done")
        z_out = [sem(f"z_out{u}") for u in range(U)]

        x_t = x.rearrange("(p t) n -> p t n", t=T)
        xt_t = xt_tab.rearrange("(p t) n -> p t n", t=T)
        al_t = al_tab.rearrange("(p t) n -> p t n", t=T)
        W1, W2, RAW = 16 * 4, 16 * 11, 16 * 3

        block = ctx.enter_context(nc.Block())

        @block.sync
        def _(sp):
            def chunks(w):
                return w.rearrange("(c p) n -> p c n", p=128)

            def row(w):
                return w.rearrange("(a n) -> a n", a=1)

            ev = [w.rearrange("e (c p) n -> e p c n", p=128) for w in (ew1, ew2, ew3)]

            def expert(at):
                for layer in range(3):
                    wide = raw_e[:, layer * LW:(layer + 1) * LW].rearrange("p (c n) -> p c n", c=KC)
                    sp.dma_start(wide, ev[layer][at, :, :, :].rearrange("a p c n -> (a p) c n")).then_inc(raw_in, 16)

            for g in range(G):
                if g == 2:
                    sp.dma_start(kv_raw, chunks(w_kv)).then_inc(w1_in, 16)
                    sp.dma_start(wg_raw[:, :, 0:D], chunks(w_g)).then_inc(w1_in, 16)
                    for s, a in enumerate((a_r, a_l)):
                        sp.dma_start(att_bc[:, s, :], a.rearrange("h c -> (h c)").partition_broadcast(128)).then_inc(w1_in, 16)
                    for q in (0, 32):
                        sp.dma_start(b3_raw[q:q + 1, :], row(eb3.rearrange("e n -> (e n)"))).then_inc(b3_in, 16)
                sp.dma_start(xring[:, g, :], x_t[:, g, :]).then_inc(x_in[g], 16)
            expert(slice(0, 1))
            sp.dma_start(src_all[:, :], src[0:N].rearrange("(p t) -> p t", t=T)).then_inc(w2_in, 16)
            sp.dma_start(dst_all[:, :], dst[0:N].rearrange("(p t) -> p t", t=T)).then_inc(w2_in, 16)
            sp.dma_start(wq_sb[:, :, :], chunks(w_q)).then_inc(w2_in, 16)
            sp.dma_start(woT_sb[:, :, :], chunks(w_oT)).then_inc(w2_in, 16)
            sp.dma_start(bo_sb[:, :], b_out.partition_broadcast(P)).then_inc(w2_in, 16)
            sp.dma_start(rw1_sb[:, :, :], chunks(rw1)).then_inc(w2_in, 16)
            sp.dma_start(rb1_sb[:, :], rb1.rearrange("(p a) -> p a", a=1)).then_inc(w2_in, 16)
            sp.dma_start(rw2_sb[:, 0:E], rw2).then_inc(w2_in, 16)
            sp.dma_start(rb2_sb[:, 0:E], rb2.partition_broadcast(P)).then_inc(w2_in, 16)
            be_v = be_sb[:, :].rearrange("p (e l n) -> p e l n", e=E, l=2)
            for layer, b in enumerate((eb1, eb2)):
                sp.dma_start(be_v[:, :, layer, :], b.partition_broadcast(128)).then_inc(w2_in, 16)

            def reload(it, at):
                for g in range(G):
                    sp.wait_ge(xn_ready, it * G + (g + 1))
                    sp.dma_start(xring[:, g, :], x_t[:, at(g), :].rearrange("p a n -> p (a n)")).then_inc(x_in[g], 16)
                    if g == 6:
                        store(it, 0)
                store(it, 1)

            def store(it, h):
                lo = HALF * h
                sp.wait_ge(xts_done, it * G + (1 + lo + HALF))
                sp.dma_start(xt_t[:, bass.ds(it * G + lo, HALF), :], xts[:, lo:lo + HALF, 0:XTW]).then_inc(xt_out[h], 16)
                sp.dma_start(al_t[:, bass.ds(it * G + lo, HALF), :], xts[:, lo:lo + HALF, XTW:GW]).then_inc(xt_out[h], 16)

            with sp.Fori(0, ITERS - 1) as it:
                reload(it, lambda g: bass.ds(it * G + (G + g), 1))
                sp.wait_ge(split_l, it + 1)
                expert(bass.ds(it + 1, 1))
            reload(ITERS - 1, lambda g: slice(g, g + 1))
            sp.wait_ge(split_l, E - 1)
            expert(slice(E - 1, E))

            with sp.Fori(0, ITERS - 1) as it:
                for g in range(G):
                    sp.wait_ge(y1_done, it * G + (g + 1))
                    sp.dma_start(xring[:, g, :], x_t[:, bass.ds(it * G + (G + g), 1), :].rearrange("p a n -> p (a n)")).then_inc(x_in[g], 16)

            sp.wait_ge(tab_done, 1)
            for g in range(G):
                sp.wait_ge(sc_out[g], 16 * (ITERS + 1))
            sp.dma_start(tab1[E * REG:E * REG + S, :], skip_rows[:, :]).then_inc(fill_out, 16)
            for k, tab in enumerate((tab0, tab1)):
                for e in range(E):
                    end = sp.value_load(fill[0:1, k, e:e + 1], min_val=0, max_val=(E - 1) * REG + N)
                    sp.dma_start(tab[bass.ds(end, S), :], skip_rows[:, ROW1 - tab.shape[1]:ROW1]).then_inc(fill_out, 16)
            sp.wait_ge(fill_out, 16 * (2 * E + 1))

            def load(k, u, at, turn=None):
                tab = (tab0, tab1)[k]
                first = sp.value_load(tab_row[0:1, k, at], min_val=0, max_val=E * REG)
                if turn is not None:
                    sp.wait_ge(z_out[u], turn * 16 + 16 * (k * (NT // U) + 1))
                sp.dma_start(rb[:, u, ROW1 - tab.shape[1]:ROW1], tab[bass.ds(first, S), :]).then_inc(r_in[u], 16)

            for k in range(2):
                if k == 1:
                    for u in range(U):
                        sp.wait_ge(z_out[u], 16 * (NT // U))
                    sp.wait_ge(xe_done, NT + LEAD)
                for u in range(U):
                    load(k, u, slice(u, u + 1))
                with sp.Fori(0, NT // U - 1) as it:
                    for u in range(U):
                        load(k, u, bass.ds(it * U + (U + u), 1), it)
                for u in range(LEAD):
                    load(k, u, slice(NT + u, NT + u + 1), NT // U - 1)
            for u in range(U):
                sp.wait_ge(z_out[u], 16 * 2 * (NT // U))

        @block.gpsimd
        def _(pool):
            pool.memset(ident[:, :], 0.0).then_inc(pool_c, 1)
            pool.memset(tri[:, :], 0.0).then_inc(pool_c, 1)
            pool.memset(ones[:, :], 1.0).then_inc(pool_c, 1)
            pool.wait_ge(pool_c, 3)
            pool.affine_select(out=ident[:, :], in_=ident[:, :], compare_op=ALU.not_equal, fill=1.0, base=0,
                               pattern=[[-1, 128]], channel_multiplier=1).then_inc(pool_c, 1)
            pool.affine_select(out=tri[:, :], in_=tri[:, :], compare_op=ALU.is_ge, fill=1.0, base=0,
                               pattern=[[-1, P]], channel_multiplier=1).then_inc(pool_c, 1)
            pool.iota(ebase[:, :, :], pattern=[[0, 2], [REG, EP]], base=0, channel_multiplier=0,
                      allow_small_or_imprecise_dtypes=True).then_inc(pool_c, 1)
            pool.iota(desc[:, :], pattern=[[-1, EP]], base=EP, channel_multiplier=0,
                      allow_small_or_imprecise_dtypes=True).then_inc(pool_c, 1)
            pool.iota(tok_all[:, :], pattern=[[1, T]], base=0, channel_multiplier=T).then_inc(pool_c, 1)
            pool.iota(nmul[:, :], pattern=[[S, NM]], base=0, channel_multiplier=0,
                      allow_small_or_imprecise_dtypes=True).then_inc(pool_c, 1)
            pool.iota(jj[:, :], pattern=[[1, NTT]], base=0, channel_multiplier=0,
                      allow_small_or_imprecise_dtypes=True).then_inc(pool_c, 1)
            pool.memset(skip_rows[:, 0:D + C_TOK], 0.0).then_inc(pool_c, 1)
            pool.iota(skip_rows[:, D + C_TOK:ROW1].bitcast(I32), pattern=[[0, 2]], base=SKIP,
                      channel_multiplier=0).then_inc(pool_c, 1)
            part = -(-S // G)
            for g in range(G):
                lo, hi = g * part, min(g * part + part, S)
                pool.wait_ge(pool_c, 12)
                pool.dma_start(tab0[E * REG + lo:E * REG + hi, :], skip_rows[lo:hi, D:ROW1]).then_inc(sc_out[g], 16)

            def wait_alone(semaphore, value):
                value = pool.to_reg(value)
                pool.wait_ge(pool_c, 1)
                pool.wait_ge(semaphore, value)

            with pool.Fori(0, E) as e:
                wait_alone(raw_in, e * RAW + RAW)
                pool.tensor_copy(we_h[:, bass.ds(e * EW, EW)], raw_e[:, :]).then_inc(split_h, 1)
                wait_alone(split_h, e + 1)
                pool.tensor_tensor(we_l[:, bass.ds(e * EW, EW)], raw_e[:, :],
                                   we_h[:, bass.ds(e * EW, EW)].bitcast(FP32), ALU.subtract).then_inc(split_l, 1)

            def gathers(it, at):
                if it is not None:
                    for g in range(G):
                        pool.wait_ge(g_in[g], it * 32 + 32)
                pool.wait_ge(w2_in, W2)
                pool.tensor_copy(idx_s[:, :], src_all[:, at]).then_inc(idx_done, 1)
                pool.tensor_copy(idx_d[:, :], dst_all[:, at]).then_inc(idx_done, 1)
                pool.wait_ge(idx_done, 2 if it is None else it * 2 + 4)
                for g in range(G):
                    if it is not None:
                        wait_alone(gp_done, it * G + (g + 1))
                    pool.indirect_dma_start(out=alg[:, g, :], out_offset=None, in_=al_tab,
                                            in_offset=bass.IndirectOffsetOnAxis(ap=idx_s[:, g:g + 1], axis=0)
                                            ).then_inc(g_in[g], 16)
                    pool.indirect_dma_start(out=xtg[:, g, :], out_offset=None, in_=xt_tab,
                                            in_offset=bass.IndirectOffsetOnAxis(ap=idx_d[:, g:g + 1], axis=0)
                                            ).then_inc(g_in[g], 16)

            def scatters(it):
                wait_alone(row_ready, it + 1)
                for g in range(G):
                    pool.indirect_dma_start(out=tab0, out_offset=bass.IndirectOffsetOnAxis(ap=pos0[:, g:g + 1], axis=0),
                                            in_=xr[:, g, :], in_offset=None).then_inc(sc_out[g], 16)

            for h in range(2):
                pool.wait_ge(xt_out[h], 16 + 32 * ITERS)
            gathers(None, slice(0, G))
            with pool.Fori(0, ITERS - 1) as it:
                gathers(it, bass.ds(it * G + G, G))
                scatters(it)
            scatters(ITERS - 1)

            for k in range(2):
                with pool.Fori(0, NT // U) as it:
                    for u in range(U):
                        wait_alone(z_done, it * U + (k * NT + u + 1))
                        if k == 0:
                            pool.indirect_dma_start(
                                out=tab1, out_offset=bass.IndirectOffsetOnAxis(
                                    ap=rb[:, u, D + C_POS:D + C_POS + 1].bitcast(I32), axis=0),
                                in_=rb[:, u, :], in_offset=None, bounds_check=E * REG - 1, oob_is_err=False
                            ).then_inc(z_out[u], 16)
                        else:
                            pool.indirect_dma_start(
                                out=out, out_offset=bass.IndirectOffsetOnAxis(
                                    ap=rb[:, u, D + C_TOK:D + C_TOK + 1].bitcast(I32), axis=0),
                                in_=rb[:, u, 0:D], in_offset=None, bounds_check=N - 1, oob_is_err=False
                            ).then_inc(z_out[u], 16)

        @block.scalar
        def _(act):
            def stdev(h, value):
                lo = HALF * h
                act.wait_ge(ag_done, value)
                act.activation(sd[:, lo:lo + HALF], mv[:, lo:lo + HALF, 1], ACT.Sqrt, bias=eps_sb[0:P, 0:1]).then_inc(sd_done, 1)

            def upper(b):
                act.activation(x_h[:, b, :, 0:P], half_t(pt[b])[:, :, 0:P], ACT.Copy).then_inc(xh_ready, 1)

            act.sem_inc(xts_done, 1)
            for h in range(2):
                act.sem_inc(xt_out[h], 16)
            act.wait_ge(prep, PREP_EPS)
            stdev(0, AHEAD)
            act.wait_ge(prep, PREP_X)
            act.wait_ge(pt_ready, 1)
            upper(0)
            with act.Fori(0, ITERS) as it:
                for g in range(G):
                    b = g % 2
                    t = it * G + g
                    act.wait_ge(k_ready, t + 1)
                    act.activation(sq[:, 0:MI], kv_ps[b][0:P, 0:MI], ACT.Square).then_inc(sqk_done, 1)
                    act.wait_ge(pt_ready, t + 2)
                    upper(1 - b)
                    act.wait_ge(v_ready, t + 1)
                    act.activation(sq[:, MI:2 * MI], kv_ps[b][0:P, MI:2 * MI], ACT.Square).then_inc(sqv_done, 1)
                    act.activation(vs[:, b, :], kv_ps[b][0:P, MI:2 * MI], ACT.Copy)
                    if g % HALF == 0:
                        act.wait_ge(xt_out[g // HALF], it * 32 + 16)
                    act.wait_ge(xt_ready, t + 1)
                    act.activation(xts[:, g, :], xt_ps[0:P, 0:GW], ACT.Copy).then_inc(xts_done, 1)
                    act.wait_ge(pr_done, t + 1)
                    act.activation(sr[:, :], pr[:, :], ACT.Sqrt).then_inc(sr_done, 1)
                    if g in (2, 7):
                        stdev(1 if g == 2 else 0, it * G + (AHEAD + g + 1))

            act.wait_ge(a_done, 1)
            act.activation(a_sb, kv_ps[0][:, :].rearrange("p (b n) -> p b n", b=MI // 128), ACT.Copy,
                           scale=1.0 / N).then_inc(as_done, 1)
            act.wait_ge(m_done, 1)
            act.activation(mix_w[:, :, :], pt[0][:, :].rearrange("p (c n) -> p c n", c=KC), ACT.Copy).then_inc(mw_done, 1)

            with act.Fori(0, ITERS) as it:
                act.wait_ge(al_ready, it + 1)
                act.activation(al[:, 2, :, :], al[:, 1, :, :], ACT.Exp).then_inc(ex_done, 1)
                for g in range(G):
                    b = g % 2
                    act.wait_ge(t1_done, it * G + (g + 1))
                    act.activation(xT[:, b, :, 0:P], half_t(pt[b])[:, :, 0:P], ACT.Copy).then_inc(xT1_done, 1)
                act.wait_ge(ag2_done, it * G + G)
                act.activation(sd[:, :], mv[:, :, 1], ACT.Sqrt, bias=eps_sb[0:P, 0:1]).then_inc(sd2_done, 1)
                for g in range(G):
                    b = g % 2
                    act.wait_ge(t2_done, it * G + (g + 1))
                    act.activation(xT[:, b, :, 0:P], half_t(pt[b])[:, :, 0:P], ACT.Copy).then_inc(xT2_done, 1)
                    act.wait_ge(rh_done, it * G + (g + 1))
                    act.activation(rhT[:, b, :], rh_ps[b][:, 0:P], ACT.Relu, bias=rb1_sb[:, 0:1]).then_inc(rhT_done, 1)
                act.wait_ge(lgx_ready, it + 1)
                act.activation(lg[:, 2, :, :], lg[:, 1, :, :], ACT.Exp).then_inc(ex2_done, 1)
                act.wait_ge(d_ready, it + 1)
                act.activation(tw[:, 5, :], tw[:, 4, :], ACT.Exp).then_inc(ex3_done, 1)

            def normal(k, j, it):
                u, turn = j % U, j // U
                loads = NT // U + (1 if u < LEAD else 0)
                act.wait_ge(r_in[u], it * 16 + 16 * (k * loads + turn + 1))
                act.activation(xe[:, j % 3, :], rb[:, u, D:2 * D], ACT.Identity,
                               bias=rb[:, u, D + C_NMR:D + C_NMR + 1],
                               scale=rb[:, u, D + C_R:D + C_R + 1]).then_inc(xe_done, 1)

            def upper3(layer, lane, n):
                act.wait_ge(et_done, n)
                act.activation(x_h[:, lane, :, :], half_t(t_ps[lane]), ACT.Relu if layer else ACT.Copy).then_inc(eh_done, 1)

            for k in range(2):
                nt = k * (NT * 3 + 2)
                for j in range(LEAD):
                    normal(k, j, 0)
                for j in range(2):
                    upper3(0, j, nt + j + 1)
                with act.Fori(0, NT // U) as it:
                    n, j = 2, 3
                    for _ in range(U // 3):
                        for kind, layer, lane in ORDER:
                            if kind == "transpose":
                                if layer == 0:
                                    normal(k, j, it)
                                    j += 1
                                n += 1
                                upper3(layer, lane, it * (3 * U) + (nt + n))

        @block.vector
        def _(dve):
            done = [0]

            def link(ins):
                done[0] += 1
                ins.then_inc(prep, 1)
                dve.wait_ge(prep, done[0])

            def stats(j, value):
                dve.wait_ge(x_in[j], value)
                dve.bn_stats(st[:, j, :], xring[:, j, :]).then_inc(bs_done, 1)

            def aggregate(j, value):
                value = dve.to_reg(value)
                dve.wait_ge(prep, 1)
                dve.wait_ge(bs_done, value)
                dve.bn_aggr(mv[:, j, :], st[:, j, :]).then_inc(ag_done, 1)

            def finish(h, n, at):
                lo = HALF * h
                part = slice(lo, lo + HALF)
                dve.wait_ge(sd_done, n + 1)
                dve.reciprocal(rs[:, part], sd[:, part]).then_inc(fin_done, 1)
                dve.wait_ge(fin_done, n * 4 + 1)
                dve.scalar_tensor_tensor(nmr[:, part], mv[:, part, 0], -1.0, rs[:, part], ALU.mult, ALU.mult).then_inc(fin_done, 1)
                dve.wait_ge(fin_done, n * 4 + 2)
                dve.tensor_copy(rs_all[:, at], rs[:, part]).then_inc(fin_done, 1)
                dve.tensor_copy(nmr_all[:, at], nmr[:, part]).then_inc(fin_done, 1)

            def normal(j, b):
                dve.tensor_scalar(xn[:, b, :], xring[:, j, :], rs[:, j:j + 1], nmr[:, j:j + 1],
                                  ALU.mult, ALU.add).then_inc(xn_ready, 1)

            def lower(b):
                dve.tensor_tensor(x_l[:, b, :, 0:P], half_t(pt[b])[:, :, 0:P], x_h[:, b, :, 0:P].bitcast(FP32),
                                  ALU.subtract).then_inc(xl_ready, 1)

            link(dve.memset(eps_sb[:, :], EPS))
            assert done[0] == PREP_EPS
            for j in range(AHEAD):
                stats(j, 16)
            for j in range(AHEAD):
                aggregate(j, j + 1)
            for buf in (x_h, x_l):
                dve.memset(buf[:, :, :, :].bitcast(FP32), 0.0).then_inc(prep, 1)
                done[0] += 1
            assert done[0] == PREP_X
            dve.wait_ge(prep, PREP_X)
            finish(0, 0, slice(0, HALF))
            for j in range(2):
                normal(j, j)

            dve.wait_ge(w1_in, W1)
            kv_v = kv_raw.rearrange("p c (h n) -> p (c h) n", n=MC)
            mean_v = kv_mean.rearrange("p c h -> p (c h)")
            link(dve.reduce_sum(mean_v, kv_v, axis=AX.X))
            link(dve.tensor_scalar(mean_v, mean_v, -1.0 / MC, None, ALU.mult))
            link(dve.tensor_tensor(kv_v, kv_v, mean_v.unsqueeze(2).to_broadcast([128, KC * 2 * MH, MC]), ALU.add))
            link(dve.tensor_copy(wkv_h[:, :, :], kv_raw))
            dve.tensor_tensor(wkv_l[:, :, :], kv_raw, wkv_h[:, :, :].bitcast(FP32), ALU.subtract).then_inc(prep, 1)
            done[0] += 1
            for s in range(2):
                link(dve.tensor_tensor(att_pr, wg_raw[:, :, 0:D], att_bc[:, s, :].unsqueeze(1).to_broadcast([128, KC, D]), ALU.mult))
                link(dve.reduce_sum(wg_raw[:, :, D + GH * s:D + GH * (s + 1)], att_pr.rearrange("p c (h n) -> p c h n", n=GC), axis=AX.X))
            link(dve.tensor_copy(wg_h[:, :, :], wg_raw))
            link(dve.tensor_tensor(wg_l[:, :, :], wg_raw, wg_h[:, :, :].bitcast(FP32), ALU.subtract))
            dve.wait_ge(b3_in, 32)
            link(dve.memset(b3_hl[:, :].bitcast(FP32), 0.0))
            link(dve.memset(sel_hl[:, :].bitcast(FP32), 0.0))
            link(dve.tensor_copy(b3_hl[0:1, :], b3_raw[0:1, :]))
            link(dve.tensor_copy(b3_hl[32:33, :], b3_raw[32:33, :]))
            link(dve.tensor_tensor(b3_hl[32:33, :], b3_raw[32:33, :], b3_hl[32:33, :].bitcast(FP32), ALU.subtract))
            for q in (0, 32):
                link(dve.memset(sel_hl[q:q + 1, :].bitcast(FP32), 1.0))
            link(dve.memset(rw2_sb[:, E:EP], 0.0))
            link(dve.memset(rb2_sb[:, E:EP], -1e30))
            link(dve.memset(base[:, :, :], 0.0))
            link(dve.memset(dotsT[:, :, :], 0.0))
            link(dve.memset(xT[:, :, :, :], 0.0))
            link(dve.memset(vs[:, 1, :], 0.0))
            dve.memset(ks[:, 1, :], 0.0).then_inc(ks_ready, 1)
            assert done[0] == PREP_ALL, done[0]
            dve.wait_ge(xh_ready, 1)
            lower(0)

            with dve.Fori(0, ITERS) as it:
                for g in range(G):
                    b = g % 2
                    t = it * G + g
                    j = (g + AHEAD) % G
                    stats(j, it * 16 + 16 * (1 + (g + AHEAD) // G))
                    dve.wait_ge(sqk_done, t + 1)
                    dve.reduce_sum(ss[:, 0:MH], sq[:, 0:MI].rearrange("p (h n) -> p h n", n=MC), axis=AX.X).then_inc(red_done, 1)
                    aggregate(j, t + (AHEAD + 1))
                    dve.wait_ge(xh_ready, t + 2)
                    lower(1 - b)
                    dve.wait_ge(sqv_done, t + 1)
                    dve.reduce_sum(ss[:, MH:2 * MH], sq[:, MI:2 * MI].rearrange("p (h n) -> p h n", n=MC), axis=AX.X).then_inc(red_done, 1)
                    dve.wait_ge(red_done, t * 2 + 2)
                    dve.tensor_scalar(sse[:, :], ss[:, :], 1.0 / MC, EPS, ALU.mult, ALU.add).then_inc(sse_done, 1)
                    dve.wait_ge(sse_done, t + 1)
                    dve.tensor_tensor(pr[:, :], sse[:, 0:MH], sse[:, MH:2 * MH], ALU.mult).then_inc(pr_done, 1)
                    if g in (3, 8):
                        h = 1 if g == 3 else 0
                        finish(h, it * 2 + (1 if g == 3 else 2), bass.ds(it * G + (HALF if g == 3 else G), HALF))
                        dve.wait_ge(fin_done, it * 8 + (8 if g == 3 else 12))
                    dve.wait_ge(pt_ready, t + 1)
                    normal((g + 2) % G, b)
                    dve.wait_ge(sr_done, t + 1)
                    dve.reciprocal(rkv[:, :], sr[:, :]).then_inc(rc_done, 1)
                    dve.wait_ge(rc_done, t + 1)
                    dve.tensor_tensor(ks[:, b, :].rearrange("p (h n) -> p h n", n=MC),
                                      kv_ps[b][0:P, 0:MI].rearrange("p (h n) -> p h n", n=MC),
                                      rkv[:, :].unsqueeze(2).to_broadcast([P, MH, MC]), ALU.mult).then_inc(ks_ready, 1)

            dve.wait_ge(dots_done, 1)
            d_v = d_ps[:, :].rearrange("p (b n) -> p b n", b=MI // 128)
            for q in range(2):
                dve.tensor_copy(dotsT[MC * q:MC * (q + 1), :, MC * q:MC * (q + 1)],
                                d_v[MC * q:MC * (q + 1), :, MC * q:MC * (q + 1)]).then_inc(dT_done, 1)

            def bc(ap, n):
                return ap.unsqueeze(len(ap.shape)).to_broadcast([*ap.shape, n])

            AL_STEPS = 5
            R_STEPS = 24
            for g in range(G):
                dve.wait_ge(xt_out[g // HALF], 16 + 32 * ITERS)
            with dve.Fori(0, ITERS) as it:
                for g in range(G):
                    dve.wait_ge(g_in[g], it * 32 + 32)
                n = [0]

                def al_link(ins):
                    n[0] += 1
                    ins.then_inc(al_step, 1)
                    dve.wait_ge(al_step, it * AL_STEPS + n[0])

                dve.tensor_copy(rs[:, :], rs_all[:, bass.ds(it * G, G)]).then_inc(rs2_done, 1)
                dve.tensor_copy(nmr[:, :], nmr_all[:, bass.ds(it * G, G)]).then_inc(rs2_done, 1)
                al_link(dve.tensor_tensor(al[:, 0, :, :], alg[:, :, :], xtg[:, :, D:XTW], ALU.add))
                al_link(dve.scalar_tensor_tensor(al[:, 1, :, :], al[:, 0, :, :], 0.01, al[:, 0, :, :], ALU.mult, ALU.max))
                al_link(dve.reduce_max(am[:, 0, :], al[:, 1, :, :], axis=AX.X))
                dve.tensor_tensor(al[:, 1, :, :], al[:, 1, :, :], bc(am[:, 0, :], GH), ALU.subtract).then_inc(al_ready, 1)
                dve.wait_ge(rs2_done, it * 2 + 2)

                def normal1(g):
                    if g >= 2:
                        dve.wait_ge(t1_done, it * G + (g - 1))
                    dve.tensor_scalar(xn[:, g % 2, :], xring[:, g, :], rs[:, g:g + 1], nmr[:, g:g + 1],
                                      ALU.mult, ALU.add).then_inc(xn1_done, 1)

                for g in range(2):
                    dve.wait_ge(x_in[g], it * 16 + 16 * (ITERS + 1))
                    normal1(g)
                dve.wait_ge(ex_done, it + 1)
                al_link(dve.reduce_sum(am[:, 1, :], al[:, 2, :, :], axis=AX.X))
                al_link(dve.reciprocal(am[:, 2, :], am[:, 1, :]))
                assert n[0] == AL_STEPS
                dve.tensor_tensor(al[:, 3, :, :], al[:, 2, :, :], bc(am[:, 2, :], GH), ALU.mult).then_inc(step, 1)
                dve.wait_ge(step, it * R_STEPS + 1)

                def graph(g):
                    b = g % 2
                    dve.tensor_tensor(gp[:, b, :].rearrange("p (h n) -> p h n", n=GC),
                                      xtg[:, g, 0:D].rearrange("p (h n) -> p h n", n=GC),
                                      bc(al[:, 3, g, :], GC), ALU.mult).then_inc(gp_done, 1)
                    dve.tensor_tensor(y1[:, b, :], xring[:, g, :], bo_sb[:, :], ALU.add).then_inc(y1_done, 1)

                def graph_sum(g):
                    b = g % 2
                    dve.wait_ge(gp_done, it * G + (g + 1))
                    dve.reduce_sum(gt[:, b, :], gp[:, b, :].rearrange("p (h n) -> p n h", n=GC), axis=AX.X).then_inc(gt_done, 1)

                def plus_graph(g):
                    b = g % 2
                    dve.wait_ge(gt_done, it * G + (g + 1))
                    dve.tensor_tensor(y2[:, b, :].rearrange("p (h n) -> p h n", n=GC),
                                      y1[:, b, :].rearrange("p (h n) -> p h n", n=GC),
                                      gt[:, b, :].unsqueeze(1).to_broadcast([P, GH, GC]), ALU.add).then_inc(y2_done, 1)

                def plus_mix(g):
                    dve.wait_ge(y2_done, it * G + (g + 1))
                    dve.wait_ge(sc_out[g], it * 16 + 16)
                    dve.wait_ge(ma_done, it * G + (g + 1))
                    dve.tensor_tensor(xr[:, g, 0:D], ma_ps[g % 2][0:P, 0:D], y2[:, g % 2, :], ALU.add).then_inc(x2_done, 1)

                def stats2(g):
                    dve.wait_ge(x2_done, it * G + (g + 1))
                    dve.bn_stats(st[:, g, :], xr[:, g, 0:D]).then_inc(bs2_done, 1)

                def aggregate2(g):
                    value = dve.to_reg(it * G + (g + 1))
                    dve.wait_ge(prep, 1)
                    dve.wait_ge(bs2_done, value)
                    dve.bn_aggr(mv[:, g, :], st[:, g, :]).then_inc(ag2_done, 1)

                dve.wait_ge(w2_in, W2)
                for g in range(G + 1):
                    if g < G:
                        if g + 2 < G:
                            dve.wait_ge(x_in[g + 2], it * 16 + 16 * (ITERS + 1))
                            normal1(g + 2)
                        graph(g)
                    if g > 0:
                        plus_mix(g - 1)
                    if g < G:
                        graph_sum(g)
                    if g > 0:
                        stats2(g - 1)
                    if g < G:
                        plus_graph(g)
                    if g > 0:
                        aggregate2(g - 1)

                dve.wait_ge(sd2_done, it + 1)
                dve.reciprocal(xr[:, :, C_R], sd[:, :]).then_inc(fin2_done, 1)
                dve.wait_ge(fin2_done, it * 2 + 1)
                dve.scalar_tensor_tensor(xr[:, :, C_NMR], mv[:, :, 0], -1.0, xr[:, :, C_R], ALU.mult, ALU.mult).then_inc(fin2_done, 1)
                dve.wait_ge(fin2_done, it * 2 + 2)
                for g in range(G):
                    if g >= 2:
                        dve.wait_ge(t2_done, it * G + (g - 1))
                    else:
                        dve.wait_ge(t1_done, it * G + G)
                    dve.tensor_scalar(xn[:, g % 2, :], xr[:, g, 0:D], xr[:, g, C_R:C_R + 1], xr[:, g, C_NMR:C_NMR + 1],
                                      ALU.mult, ALU.add).then_inc(xn2_done, 1)

                n2 = [1]

                def link2(ins):
                    n2[0] += 1
                    ins.then_inc(step, 1)
                    dve.wait_ge(step, it * R_STEPS + n2[0])

                dve.wait_ge(lg_done, it * G + G)
                link2(dve.tensor_tensor(lg[:, 0, :, :], lg_ps, rb2_sb[:, :].unsqueeze(1).to_broadcast([P, G, EP]), ALU.add))
                link2(dve.reduce_max(tw[:, 0, :], lg[:, 0, :, :], axis=AX.X))
                dve.tensor_tensor(lg[:, 1, :, :], lg[:, 0, :, :], bc(tw[:, 0, :], EP), ALU.subtract).then_inc(lgx_ready, 1)
                dve.wait_ge(ex2_done, it + 1)
                link2(dve.reduce_sum(tw[:, 1, :], lg[:, 2, :, :], axis=AX.X))
                link2(dve.reciprocal(tw[:, 1, :], tw[:, 1, :]))
                link2(dve.tensor_tensor(lg[:, 3, :, :], lg[:, 2, :, :], bc(tw[:, 1, :], EP), ALU.mult))

                def choose(k, prob):
                    link2(dve.reduce_max(tw[:, 2 + k, :], prob, axis=AX.X))
                    link2(dve.tensor_tensor(lg[:, 0, :, :], prob, bc(tw[:, 2 + k, :], EP), ALU.is_equal))
                    link2(dve.tensor_tensor(lg[:, 1, :, :], lg[:, 0, :, :], desc[:, :].unsqueeze(1).to_broadcast([P, G, EP]), ALU.mult))
                    link2(dve.reduce_max(tw[:, 6, :], lg[:, 1, :, :], axis=AX.X))
                    last = dve.tensor_tensor(oh[:, :, k, :], lg[:, 1, :, :], bc(tw[:, 6, :], EP), ALU.is_equal)
                    if k == 0:
                        link2(last)
                    else:
                        last.then_inc(oh_ready, 1)

                choose(0, lg[:, 3, :, :])
                link2(dve.scalar_tensor_tensor(lg[:, 2, :, :], oh[:, :, 0, :], -4.0, lg[:, 3, :, :], ALU.mult, ALU.add))
                choose(1, lg[:, 2, :, :])
                dve.tensor_tensor(tw[:, 4, :], tw[:, 3, :], tw[:, 2, :], ALU.subtract).then_inc(d_ready, 1)
                dve.wait_ge(ex3_done, it + 1)
                link2(dve.tensor_scalar(tw[:, 7, :], tw[:, 5, :], 1.0, None, ALU.add))
                link2(dve.reciprocal(xr[:, :, C_W], tw[:, 7, :]))
                dve.tensor_tensor(xr[:, :, C_W + 1], tw[:, 5, :], xr[:, :, C_W], ALU.mult)
                dve.tensor_copy(xr[:, :, C_TOK].bitcast(I32), tok_all[:, bass.ds(it * G, G)])
                dve.wait_ge(rk_done, it + 1)
                link2(dve.tensor_tensor(rk[:, :, :, :], rk_ps, ebase[:, :, :].unsqueeze(1).to_broadcast([P, G, 2, EP]), ALU.add))
                link2(dve.tensor_tensor(rk[:, :, :, :], rk[:, :, :, :], oh[:, :, :, :], ALU.mult))
                link2(dve.reduce_sum(posf[:, :, :], rk[:, :, :, :], axis=AX.X))
                link2(dve.tensor_copy(pos0[:, :], posf[:, :, 0]))
                dve.tensor_copy(xr[:, :, C_POS].bitcast(I32), posf[:, :, 1]).then_inc(row_ready, 1)
                link2(dve.reduce_sum(bsum[:, :, :], oh[:, :, :, :].rearrange("p g k e -> p k e g"), axis=AX.X))
                link2(dve.tensor_tensor(base[:, :, :], base[:, :, :], bsum[:, :, :], ALU.add))
                assert n2[0] == R_STEPS, n2[0]

            tn = [0]

            def tlink(ins):
                tn[0] += 1
                ins.then_inc(tstep, 1)
                dve.wait_ge(tstep, tn[0])

            dve.wait_ge(cnt_done, 1)
            tlink(dve.tensor_copy(cnt[:, :, :], d_ps[0:1, 0:2 * EP].rearrange("p (k e) -> p k e", k=2)))
            tlink(dve.tensor_tensor(fillf[:, :, :], cnt[:, :, :], ebase[0:1, :, :], ALU.add))
            tlink(dve.tensor_copy(fill[:, :, :], fillf[:, :, :]))
            ce = cnt[:, :, :].rearrange("p k e -> p (k e)")
            nc_v = ncmp.rearrange("p k e m -> p (k e) m")
            tlink(dve.tensor_tensor(nc_v, bc(ce, NM), nmul[:, :].unsqueeze(1).to_broadcast([1, 2 * EP, NM]), ALU.is_gt))
            tlink(dve.reduce_sum(ntl[:, :, :].rearrange("p k e -> p (k e)"), nc_v, axis=AX.X))
            tlink(dve.tensor_copy(ends[:, :, 0:1], ntl[:, :, 0:1]))
            for e in range(1, E):
                tlink(dve.tensor_tensor(ends[:, :, e:e + 1], ends[:, :, e - 1:e], ntl[:, :, e:e + 1], ALU.add))
            for k in range(2):
                tlink(dve.tensor_tensor(ge[:, k, :, :], bc(jj[:, :], E), ends[:, k, 0:E].unsqueeze(1).to_broadcast([1, NTT, E]), ALU.is_ge))
                tlink(dve.reduce_sum(tf[:, 0, k, :], ge[:, k, :, :], axis=AX.X))
                tlink(dve.tensor_tensor(gn[:, k, :, :], ge[:, k, :, :], ntl[:, k, 0:E].unsqueeze(1).to_broadcast([1, NTT, E]), ALU.mult))
                tlink(dve.reduce_sum(tf[:, 1, k, :], gn[:, k, :, :], axis=AX.X))
                tlink(dve.tensor_tensor(tf[:, 2, k, :], jj[:, :], tf[:, 1, k, :], ALU.subtract))
                tlink(dve.tensor_scalar(tf[:, 3, k, :], ge[:, k, :, E - 1], -1.0, 1.0, ALU.mult, ALU.add))
                tlink(dve.tensor_tensor(tf[:, 4, k, :], tf[:, 2, k, :], tf[:, 3, k, :], ALU.mult))
                tlink(dve.tensor_scalar(tf[:, 5, k, :], tf[:, 4, k, :], float(S), None, ALU.mult))
                tlink(dve.scalar_tensor_tensor(tf[:, 6, k, :], tf[:, 0, k, :], float(REG), tf[:, 5, k, :], ALU.mult, ALU.add))
                tlink(dve.tensor_scalar(tf[:, 7, k, :], tf[:, 0, k, :], float(E - 1), None, ALU.min))
                tlink(dve.tensor_copy(tab_row[:, k, :], tf[:, 6, k, :]))
                tlink(dve.tensor_copy(tab_e[:, k, :], tf[:, 7, k, :]))
            dve.sem_inc(tab_done, 1)

            def lower3(layer, lane, n):
                dve.wait_ge(eh_done, n)
                hi = x_h[:, lane, :, :].bitcast(FP32)
                if layer:
                    ins = dve.scalar_tensor_tensor(x_l[:, lane, :, :], half_t(t_ps[lane]), 0.0, hi, ALU.max, ALU.subtract)
                else:
                    ins = dve.tensor_tensor(x_l[:, lane, :, :], half_t(t_ps[lane]), hi, ALU.subtract)
                ins.then_inc(el_done, 1)

            for k in range(2):
                nt, nl = k * (NT * 3 + 2), k * NT * 3
                for j in range(2):
                    lower3(0, j, nt + j + 1)
                with dve.Fori(0, NT // U) as it:
                    n, m, j, i = 2, 0, 0, 0
                    es = [dve.value_load(tab_e[0:1, k, bass.ds(it * U + u, 1)], min_val=0, max_val=E - 1) for u in range(U)]
                    for group in range(U // 3):
                        for kind, layer, lane in ORDER:
                            if kind == "transpose":
                                n += 1
                                lower3(layer, lane, it * (3 * U) + (nt + n))
                                continue
                            m += 1
                            u = group * 3 + lane
                            dve.wait_ge(l_done, it * (3 * U) + (nl + m))
                            if layer < 3:
                                at = es[u] * (2 * F) + (layer - 1) * F
                                dve.tensor_tensor(hs[:, lane, :], l_ps[lane][:, 0:F], be_sb[:, bass.ds(at, F)], ALU.add).then_inc(hs_done, 1)
                            else:
                                before = rb[:, u, D:2 * D] if k == 0 else rb[:, u, 0:D]
                                dve.scalar_tensor_tensor(rb[:, u, 0:D], l_ps[lane][:, 0:D],
                                                         rb[:, u, D + C_W + k:D + C_W + k + 1], before,
                                                         ALU.mult, ALU.add).then_inc(z_done, 1)

        @block.tensor
        def _(pe):
            def transpose(bank, rows, p):
                for c in range(KC):
                    last = pe.transpose(half_t(bank)[:, c, 0:p], rows[:, c * 128:(c + 1) * 128], ident[0:p, 0:p])
                return last

            def product(outp, lane, w_h, w_l, xl, ready, add=None):
                first = True
                if add is not None:
                    pe.matmul(outp, add[0], add[1], start=True, stop=False)
                    first = False
                for c in range(KC):
                    pe.matmul(outp, x_h[:, lane, c, :], w_h(c), start=first, stop=False)
                    first = False
                    pe.matmul(outp, x_h[:, lane, c, :], w_l(c), start=False, stop=False)
                if ready is not None:
                    pe.wait_ge(xl, ready)
                for c in range(KC):
                    last = pe.matmul(outp, x_l[:, lane, c, :], w_h(c), start=False, stop=c == KC - 1)
                return last

            pe.wait_ge(pool_c, 5)
            pe.wait_ge(xn_ready, 1)
            transpose(pt[0], xn[:, 0, :], P).then_inc(pt_ready, 1)
            pe.wait_ge(ks_ready, 1)
            pe.wait_ge(prep, PREP_ALL)
            pe.matmul(d_ps[:, :], vs[:, 1, 0:128], ks[:, 1, :], start=True, stop=False, skip_group_check=True)

            def dots(b):
                for q in range(MI // 128):
                    at = slice(q * 128, (q + 1) * 128)
                    last = pe.matmul(d_ps[:, at], vs[:, b, at], ks[:, b, at], start=False, stop=False, skip_group_check=True)
                return last

            with pe.Fori(0, ITERS) as it:
                for g in range(G):
                    b = g % 2
                    t = it * G + g
                    pe.wait_ge(xh_ready, t + 1)
                    product(kv_ps[b][:, 0:MI], b, lambda c: wkv_h[:, c, 0:MI], lambda c: wkv_l[:, c, 0:MI],
                            xl_ready, t + 1).then_inc(k_ready, 1)
                    product(kv_ps[b][:, MI:2 * MI], b, lambda c: wkv_h[:, c, MI:2 * MI], lambda c: wkv_l[:, c, MI:2 * MI],
                            None, None).then_inc(v_ready, 1)
                    pe.wait_ge(xn_ready, t + 2)
                    transpose(pt[1 - b], xn[:, 1 - b, :], P).then_inc(pt_ready, 1)
                    pe.wait_ge(xts_done, t + 1)
                    product(xt_ps[:, 0:GW], b, lambda c: wg_h[:, c, :], lambda c: wg_l[:, c, :],
                            None, None).then_inc(xt_ready, 1)
                    pe.wait_ge(ks_ready, t + 1)
                    dots(1 - b)
            pe.wait_ge(ks_ready, T + 1)
            dots((T - 1) % 2).then_inc(dots_done, 1)

            pe.wait_ge(w2_in, W2)
            pe.wait_ge(dT_done, 2)
            for q in range(MI // 128):
                last = pe.matmul(kv_ps[0][:, q * D:(q + 1) * D], dotsT[:, q, :], woT_sb[:, q, :], start=True, stop=True)
            last.then_inc(a_done, 1)
            pe.wait_ge(as_done, 1)
            pe.wait_ge(xl_ready, T + 1)
            for c in range(KC):
                for q in range(MI // 128):
                    last = pe.matmul(pt[0][:, c * D:(c + 1) * D], wq_sb[:, q, c * 128:(c + 1) * 128], a_sb[:, q, :],
                                     start=q == 0, stop=q == MI // 128 - 1)
            last.then_inc(m_done, 1)
            pe.wait_ge(mw_done, 1)

            with pe.Fori(0, ITERS) as it:
                def t1(g):
                    b = g % 2
                    pe.wait_ge(xn1_done, it * G + (g + 1))
                    transpose(pt[b], xn[:, b, :], P).then_inc(t1_done, 1)

                def mix(g):
                    b = g % 2
                    pe.wait_ge(xT1_done, it * G + (g + 1))
                    if g >= 2:
                        pe.wait_ge(x2_done, it * G + (g - 1))
                    for c in range(KC):
                        last = pe.matmul(ma_ps[b][0:P, 0:D], xT[:, b, c, 0:P], mix_w[:, c, :], start=c == 0, stop=c == KC - 1)
                    last.then_inc(ma_done, 1)

                t1(0)
                for g in range(G):
                    if g + 1 < G:
                        t1(g + 1)
                    mix(g)

                def t2(g):
                    b = g % 2
                    pe.wait_ge(xn2_done, it * G + (g + 1))
                    transpose(pt[b], xn[:, b, :], P).then_inc(t2_done, 1)

                def hidden(g):
                    b = g % 2
                    pe.wait_ge(xT2_done, it * G + (g + 1))
                    for c in range(KC):
                        last = pe.matmul(rh_ps[b][:, 0:P], rw1_sb[:, c, :], xT[:, b, c, 0:P], start=c == 0, stop=c == KC - 1)
                    last.then_inc(rh_done, 1)

                def logits(g):
                    pe.wait_ge(rhT_done, it * G + (g + 1))
                    pe.matmul(lg_ps[:, g, :], rhT[:, g % 2, :], rw2_sb[:, :], start=True, stop=True).then_inc(lg_done, 1)

                t2(0)
                for g in range(G + 1):
                    if g + 1 < G:
                        t2(g + 1)
                    if g < G:
                        hidden(g)
                    if g > 0:
                        logits(g - 1)
                pe.wait_ge(oh_ready, it + 1)
                pe.matmul(rk_ps, tri[:, :], oh[:, :, :, :], start=True, stop=False, skip_group_check=True)
                pe.matmul(rk_ps, ones[:, :], base[:, :, :].unsqueeze(1).to_broadcast([P, G, 2, EP]), start=False, stop=False,
                          skip_group_check=True)
                for g in range(G - 1):
                    last = pe.matmul(rk_ps[:, g + 1:G, :, :], ones[:, :],
                                     oh[:, g, :, :].unsqueeze(1).to_broadcast([P, G - 1 - g, 2, EP]),
                                     start=False, stop=g == G - 2, skip_group_check=True)
                last.then_inc(rk_done, 1)
            pe.wait_ge(step, ITERS * 24)
            pe.matmul(d_ps[0:P, 0:2 * EP], ones[:, :], base[:, :, :].rearrange("p k e -> p (k e)"), start=True, stop=True).then_inc(cnt_done, 1)

            pe.wait_ge(split_l, E)
            pe.wait_ge(tab_done, 1)
            for k in range(2):
                nt, nx, nh = k * (NT * 3 + 2), k * (NT + LEAD), k * NT * 2
                if k == 1:
                    pe.wait_ge(el_done, nt)
                for j in range(2):
                    pe.wait_ge(xe_done, nx + j + 1)
                    transpose(t_ps[j], xe[:, j, :], S).then_inc(et_done, 1)
                with pe.Fori(0, NT // U) as it:
                    es = [pe.value_load(tab_e[0:1, k, bass.ds(it * U + u, 1)], min_val=0, max_val=E - 1) for u in range(U)]
                    x_n, h_n, m = 2, 0, 0
                    for group in range(U // 3):
                        for kind, layer, lane in ORDER:
                            if kind == "transpose":
                                if layer == 0:
                                    x_n += 1
                                    pe.wait_ge(xe_done, it * U + (nx + x_n))
                                    rows = xe[:, lane, :]
                                else:
                                    h_n += 1
                                    pe.wait_ge(hs_done, it * (2 * U) + (nh + h_n))
                                    rows = hs[:, lane, :]
                                transpose(t_ps[lane], rows, S).then_inc(et_done, 1)
                                continue
                            m += 1
                            e = es[group * 3 + lane]
                            ready = it * (3 * U) + (nt + m)
                            pe.wait_ge(eh_done, ready)
                            at = e * EW + (layer - 1) * LW
                            add = (sel_hl[:, :], b3_hl[:, bass.ds(e * D, D)]) if layer == 3 else None
                            product(l_ps[lane][:, 0:F], lane,
                                    lambda c, at=at: we_h[:, bass.ds(at + c * F, F)],
                                    lambda c, at=at: we_l[:, bass.ds(at + c * F, F)],
                                    el_done, ready, add).then_inc(l_done, 1)


def kernel(**inputs):
    import numpy as np
    import concourse.bacc as bacc
    from concourse.bass_utils import run_bass_kernel_spmd as run

    wqkv = np.asarray(inputs["L0_mix_w_qkv"])
    given = {
        "x": inputs["x"], "src": inputs["src"], "dst": inputs["dst"],
        "w_kv": wqkv[MI:].T, "w_q": wqkv[:MI], "w_oT": np.asarray(inputs["L0_mix_w_out"]).T,
        "b_out": inputs["L0_mix_b_out"], "w_g": inputs["L0_gnn_weight"],
        "a_l": inputs["L0_gnn_attn_l"], "a_r": inputs["L0_gnn_attn_r"],
        "rw1": inputs["L0_ffn_router_w1"], "rb1": inputs["L0_ffn_router_b1"],
        "rw2": inputs["L0_ffn_router_w2"], "rb2": inputs["L0_ffn_router_b2"],
        "ew1": inputs["L0_ffn_expert_w1"], "eb1": inputs["L0_ffn_expert_b1"],
        "ew2": inputs["L0_ffn_expert_w2"], "eb2": inputs["L0_ffn_expert_b2"],
        "ew3": inputs["L0_ffn_expert_w3"], "eb3": inputs["L0_ffn_expert_b3"],
    }
    nc = bacc.Bacc("TRN2", target_bir_lowering=False, num_devices=1)
    arrays, aps = {}, []
    for name, a in given.items():
        a = np.ascontiguousarray(a)
        arrays[f"in_{name}"] = a
        aps.append(nc.dram_tensor(f"in_{name}", a.shape, mybir.dt.from_np(a.dtype), kind="ExternalInput").ap())
    out = nc.dram_tensor("out_x", (N, D), FP32, kind="ExternalOutput").ap()
    gps_layer(nc, *aps, out)
    r = run(nc, [arrays], core_ids=[0])
    return r.results[0]["out_x"]
```

```python
import concourse.bass as bass
from concourse import mybir
from contextlib import ExitStack

FP32 = mybir.dt.float32
FP32R = mybir.dt.float32r
I32 = mybir.dt.int32
ALU = mybir.AluOpType
ACT = mybir.ActivationFunctionType
AX = mybir.AxisListType

N, D = 6250, 256
GH, GC = 4, 64
MH, MC = 8, 64
MI = MH * MC
E, F, RH = 6, 256, 128
EPS = 1e-5

P = 125
T = N // P
G = 10
ITERS = T // G
KC = D // 128
AHEAD = 7
HALF = G // 2
Q = 5
GROUPS = T // Q
IN_G = 16 * 2 * Q
OUT_G = 16 * Q
XTW = D + GH
GW = D + 2 * GH

S = 128
REG = N + S
EP = 8
NT = (N + E * (S - 1)) // S
LEAD = 3
U = 9
ROW = D + 6
C_NMR, C_R, C_W, C_TOK, C_POS = D, D + 1, D + 2, D + 4, D + 5
ROW1 = D + ROW
SKIP = 1 << 20
LW = KC * F
EW = 3 * LW

ORDER = [("product", 1, 0), ("transpose", 0, 2), ("product", 1, 1), ("transpose", 1, 0),
         ("product", 1, 2), ("transpose", 1, 1), ("product", 2, 0), ("transpose", 1, 2),
         ("product", 2, 1), ("transpose", 2, 0), ("product", 2, 2), ("transpose", 2, 1),
         ("product", 3, 0), ("transpose", 2, 2), ("product", 3, 1), ("transpose", 0, 0),
         ("product", 3, 2), ("transpose", 0, 1)]

B_TILES = [(0, 1), (2, 3), (4,), (), ()]
AL_STEPS, R_STEPS = 6, 20

PREP_EPS, PREP_X, PREP_ALL = 1, 3, 27


class Group:

    def __init__(self, it, p):
        self.it, self.p = it, p

    def __mul__(self, n):
        return self.it * (2 * n) + (2 + self.p) * n

    def __add__(self, n):
        return self.it * 2 + (2 + self.p + n)

    def __floordiv__(self, n):
        assert n == 2
        return self.it + (2 + self.p) // 2


def gps_layer(nc, x, src, dst, w_kv, w_q, w_oT, b_out, w_g, a_l, a_r, rw1, rb1, rw2, rb2,
              ew1, eb1, ew2, eb2, ew3, eb3, out):
    ctx = ExitStack()
    with ctx:
        def sb(name, shape, dt=FP32):
            return ctx.enter_context(nc.sbuf_tensor(name, shape, dt))

        def sem(name):
            return ctx.enter_context(nc.semaphore(name))

        xt_tab = nc.dram_tensor("xt_tab", (N, XTW), FP32, kind="Internal").ap()
        al_tab = nc.dram_tensor("al_tab", (N, GH), FP32, kind="Internal").ap()
        tab0 = nc.dram_tensor("tab0", (E * REG + S, ROW), FP32, kind="Internal").ap()
        tab1 = nc.dram_tensor("tab1", (E * REG + S, ROW1), FP32, kind="Internal").ap()

        ident = sb("ident", [128, 128])
        tri = sb("tri", [P, P])
        ones = sb("ones", [P, P])
        ebase = sb("ebase", [P, 2, EP])
        desc = sb("desc", [P, EP])
        tok_all = sb("tok_all", [P, T], I32)
        wkv_h, wkv_l = sb("wkv_h", [128, KC, 2 * MI], FP32R), sb("wkv_l", [128, KC, 2 * MI], FP32R)
        wg_h, wg_l = sb("wg_h", [128, KC, GW], FP32R), sb("wg_l", [128, KC, GW], FP32R)
        wq_sb = sb("wq_sb", [128, MI // 128, D])
        woT_sb = sb("woT_sb", [128, MI // 128, D])
        mix_w = sb("mix_w", [128, KC, D])
        bo_sb = sb("bo_sb", [33, D])
        rw1_sb = sb("rw1_sb", [128, KC, RH])
        rb1_sb = sb("rb1_sb", [RH, 1])
        rw2_sb = sb("rw2_sb", [RH, EP])
        rb2_sb = sb("rb2_sb", [P, EP])
        we_h, we_l = sb("we_h", [128, E * EW], FP32R), sb("we_l", [128, E * EW], FP32R)
        be_sb = sb("be_sb", [128, E * 2 * F])
        b3_hl = sb("b3_hl", [128, E * D], FP32R)
        bo_hl = sb("bo_hl", [128, D], FP32R)
        sel_hl = sb("sel_hl", [128, S], FP32R)
        src_all, dst_all = sb("src_all", [P, T], I32), sb("dst_all", [P, T], I32)
        raw_e = sb("raw_e", [128, EW])
        skip_rows = sb("skip_rows", [S, ROW1])
        eps_sb = sb("eps_sb", [128, 1])

        arena = sb("arena", [128, U * ROW1])
        xring = sb("xring", [P, G, D])
        xn = sb("xn", [P, 2, D])
        x_h, x_l = sb("x_h", [128, 3, KC, 128], FP32R), sb("x_l", [128, 3, KC, 128], FP32R)
        st = sb("st", [P, G, 6])
        mv = sb("mv", [P, G, 2])
        sd = sb("sd", [P, G])
        rs = sb("rs", [P, G])
        nmr = sb("nmr", [P, G])
        rs_all, nmr_all = sb("rs_all", [P, T + G]), sb("nmr_all", [P, T + G])
        work = sb("work", [128, 6 * MI])

        kv_raw = arena[:, 0:KC * 2 * MI].rearrange("p (c n) -> p c n", c=KC)
        g_at = KC * 2 * MI
        wg_raw = arena[:, g_at:g_at + KC * GW].rearrange("p (c n) -> p c n", c=KC)
        att_bc = arena[:, g_at + KC * GW:g_at + KC * GW + 2 * D].rearrange("p (s n) -> p s n", s=2)
        att_pr = work[:, 0:KC * D].rearrange("p (c n) -> p c n", c=KC)
        kv_mean = work[:, 2 * MI:2 * MI + KC * 2 * MH].rearrange("p (c h) -> p c h", c=KC)
        b3_raw = work[:, 2 * MI + 64:2 * MI + 64 + E * D]
        xts = arena[0:P, 0:G * GW].rearrange("p (g n) -> p g n", g=G)
        sq = work[0:P, 0:2 * MI]
        ks = work[0:P, 2 * MI:4 * MI].rearrange("p (b n) -> p b n", b=2)
        vs = work[0:P, 4 * MI:6 * MI].rearrange("p (b n) -> p b n", b=2)
        ss = sb("ss", [P, 2 * MH])
        sse = sb("sse", [P, 2 * MH])
        pr = sb("pr", [P, MH])
        sr = sb("sr", [P, MH])
        rkv = sb("rkv", [P, MH])

        dotsT = sb("dotsT", [128, MI // 128, 128])
        a_sb = work[:, 0:(MI // 128) * D].rearrange("p (b n) -> p b n", b=MI // 128)

        xtg = arena[0:P, 0:2 * Q * XTW].rearrange("p (b g n) -> p b g n", b=2, g=Q)
        gp = arena[0:P, 2 * Q * XTW:2 * Q * XTW + 2 * D].rearrange("p (b n) -> p b n", b=2)
        gt = arena[0:P, 2 * Q * XTW + 2 * D:2 * Q * XTW + 2 * D + 2 * GC].rearrange("p (b n) -> p b n", b=2)
        y2 = arena[0:P, 2 * Q * XTW + 3 * D:2 * Q * XTW + 5 * D].rearrange("p (b n) -> p b n", b=2)
        xr = work[0:P, 0:2 * Q * ROW].rearrange("p (b g n) -> p b g n", b=2, g=Q)
        xT = sb("xT", [128, 2, KC, 128])
        rhT = sb("rhT", [RH, 2, P])
        alg = sb("alg", [P, 2, Q, GH])
        al = sb("al", [P, 4, Q, GH])
        am = sb("am", [P, 3, Q])
        idx_s, idx_d = sb("idx_s", [P, 2, Q], I32), sb("idx_d", [P, 2, Q], I32)
        lg = sb("lg", [P, 4, Q, EP])
        oh = sb("oh", [P, Q, 2, EP])
        rk = sb("rk", [P, Q, 2, EP])
        tw = sb("tw", [P, 8, Q])
        posf = sb("posf", [P, Q, 2])
        pos0 = sb("pos0", [P, 2, Q], I32)
        base = sb("base", [P, 2, EP])
        bsum = sb("bsum", [P, 2, EP])

        NTT = NT + LEAD
        NM = -(-N // S)
        cnt = sb("cnt", [1, 2, EP])
        nmul = sb("nmul", [1, NM])
        ntl = sb("ntl", [1, 2, EP])
        ncmp = arena[0:1, 0:2 * EP * NM].rearrange("p (k e m) -> p k e m", k=2, e=EP)
        ends = sb("ends", [1, 2, EP])
        jj = sb("jj", [1, NTT])
        ge = arena[0:1, 1024:1024 + 2 * NTT * E].rearrange("p (k j e) -> p k j e", k=2, j=NTT)
        gn = arena[0:1, 2048:2048 + 2 * NTT * E].rearrange("p (k j e) -> p k j e", k=2, j=NTT)
        tf = sb("tf", [1, 8, 2, NTT])
        tab_row = sb("tab_row", [1, 2, NTT], I32)
        tab_e = sb("tab_e", [1, 2, NTT // 3, 4], I32)
        fill = sb("fill", [1, 2, EP], I32)

        rb = arena[:, :].rearrange("p (u n) -> p u n", u=U)
        xe = sb("xe", [S, 3, D])
        hs = sb("hs", [S, 3, D])

        xnr = xe[0:P, :, :]
        xTr = hs[:, :, :].rearrange("p b (c n) -> p b c n", c=KC)

        kv_ps = [ctx.enter_context(nc.psum_tensor(f"kv_ps{b}", [128, 2 * MI], FP32)) for b in range(2)]
        pt = [ctx.enter_context(nc.psum_tensor(f"pt{b}", [128, 512], FP32)) for b in range(2)]
        xt_ps = ctx.enter_context(nc.psum_tensor("xt_ps", [128, 512], FP32))
        d_ps = ctx.enter_context(nc.psum_tensor("d_ps", [128, 512], FP32))

        def half_t(bank):
            return bank[:, 0:KC * 128].rearrange("p (c n) -> p c n", c=KC)

        ma_ps = [kv_ps[0][:, 0:512], kv_ps[0][:, 512:1024]]
        rh_ps = [kv_ps[1][:, 0:512], kv_ps[1][:, 512:1024]]
        lg_ps = xt_ps[0:P, 0:Q * EP].rearrange("p (g e) -> p g e", g=Q)
        rk_ps = d_ps[0:P, 0:Q * 2 * EP].rearrange("p (g k e) -> p g k e", g=Q, k=2)
        t_ps = [pt[0], pt[1], xt_ps]
        l_ps = [kv_ps[0][:, 0:512], kv_ps[0][:, 512:1024], kv_ps[1][:, 0:512]]

        x_in = [sem(f"x_in{g}") for g in range(G)]
        w1_in, w2_in, b3_in, raw_in = sem("w1_in"), sem("w2_in"), sem("b3_in"), sem("raw_in")
        pool_c, prep = sem("pool_c"), sem("prep")
        split_h, split_l = sem("split_h"), sem("split_l")
        bs_done, ag_done, sd_done, fin_done = sem("bs_done"), sem("ag_done"), sem("sd_done"), sem("fin_done")
        xn_ready, pt_ready, xh_ready, xl_ready = sem("xn_ready"), sem("pt_ready"), sem("xh_ready"), sem("xl_ready")
        k_ready, v_ready, xt_ready = sem("k_ready"), sem("v_ready"), sem("xt_ready")
        sqk_done, sqv_done, red_done, sse_done = sem("sqk_done"), sem("sqv_done"), sem("red_done"), sem("sse_done")
        pr_done, sr_done, rc_done = sem("pr_done"), sem("sr_done"), sem("rc_done")
        ks_ready, xts_done, dots_done = sem("ks_ready"), sem("xts_done"), sem("dots_done")
        xt_out = [sem(f"xt_out{h}") for h in range(2)]
        dT_done, a_done, as_done, m_done, mw_done = (sem("dT_done"), sem("a_done"), sem("as_done"),
                                                     sem("m_done"), sem("mw_done"))
        idx_done = sem("idx_done")
        bo_done = sem("bo_done")
        g_in = [sem(f"g_in{b}") for b in range(2)]
        rs2_done, al_step, al_ready, ex_done = sem("rs2_done"), sem("al_step"), sem("al_ready"), sem("ex_done")
        xn1_done, t1_done, xT1_done, ma_done = sem("xn1_done"), sem("t1_done"), sem("xT1_done"), sem("ma_done")
        gp_done, gt_done, y2_done, x2_done = sem("gp_done"), sem("gt_done"), sem("y2_done"), sem("x2_done")
        bs2_done, ag2_done, sd2_done, fin2_done = sem("bs2_done"), sem("ag2_done"), sem("sd2_done"), sem("fin2_done")
        xn2_done, t2_done, xT2_done = sem("xn2_done"), sem("t2_done"), sem("xT2_done")
        rh_done, rhT_done, lg_done = sem("rh_done"), sem("rhT_done"), sem("lg_done")
        step_done, lgx_ready, ex2_done, d_ready, ex3_done = (sem("step_done"), sem("lgx_ready"), sem("ex2_done"),
                                                        sem("d_ready"), sem("ex3_done"))
        oh_ready, rk_done, row_ready = sem("oh_ready"), sem("rk_done"), sem("row_ready")
        sc_out = [sem(f"sc_out{b}") for b in range(2)]
        cnt_done, tstep, tab_done, fill_out = sem("cnt_done"), sem("tstep"), sem("tab_done"), sem("fill_out")
        r_in = [sem(f"r_in{u}") for u in range(U)]
        xe_done, et_done, eh_done, el_done = sem("xe_done"), sem("et_done"), sem("eh_done"), sem("el_done")
        l_done, hs_done, z_done = sem("l_done"), sem("hs_done"), sem("z_done")
        z_out = [sem(f"z_out{u}") for u in range(U)]

        x_t = x.rearrange("(p t) n -> p t n", t=T)
        xt_t = xt_tab.rearrange("(p t) n -> p t n", t=T)
        al_t = al_tab.rearrange("(p t) n -> p t n", t=T)
        W1, W2, RAW = 16 * 4, 16 * 11, 16 * 3

        def groups(engine, step):
            step(0, None, 0)
            step(1, 0, 1)
            with engine.Fori(0, GROUPS // 2 - 1) as it:
                for p in range(2):
                    step(Group(it, p), Group(it, p - 1), p)
            step(None, GROUPS - 1, 0)

        def experts(engine, regs, k, at):
            engine.load(regs, tab_e[0:1, k, bass.ds(at, 1), 0:3].rearrange("p a l -> p (a l)"))
            return [engine.snap(reg, min_val=0, max_val=E - 1) for reg in regs]

        block = ctx.enter_context(nc.Block())

        @block.sync
        def _(sp):
            def chunks(w):
                return w.rearrange("(c p) n -> p c n", p=128)

            def row(w):
                return w.rearrange("(a n) -> a n", a=1)

            ev = [w.rearrange("e (c p) n -> e p c n", p=128) for w in (ew1, ew2, ew3)]

            def expert(at):
                for layer in range(3):
                    wide = raw_e[:, layer * LW:(layer + 1) * LW].rearrange("p (c n) -> p c n", c=KC)
                    sp.dma_start(wide, ev[layer][at, :, :, :].rearrange("a p c n -> (a p) c n")).then_inc(raw_in, 16)

            for g in range(G):
                if g == 2:
                    sp.dma_start(kv_raw, chunks(w_kv)).then_inc(w1_in, 16)
                    sp.dma_start(wg_raw[:, :, 0:D], chunks(w_g)).then_inc(w1_in, 16)
                    for s, a in enumerate((a_r, a_l)):
                        sp.dma_start(att_bc[:, s, :], a.rearrange("h c -> (h c)").partition_broadcast(128)).then_inc(w1_in, 16)
                    for q in (0, 32):
                        sp.dma_start(b3_raw[q:q + 1, :], row(eb3.rearrange("e n -> (e n)"))).then_inc(b3_in, 16)
                sp.dma_start(xring[:, g, :], x_t[:, g, :]).then_inc(x_in[g], 16)
            expert(slice(0, 1))
            sp.dma_start(src_all[:, :], src[0:N].rearrange("(p t) -> p t", t=T)).then_inc(w2_in, 16)
            sp.dma_start(dst_all[:, :], dst[0:N].rearrange("(p t) -> p t", t=T)).then_inc(w2_in, 16)
            sp.dma_start(wq_sb[:, :, :], chunks(w_q)).then_inc(w2_in, 16)
            sp.dma_start(woT_sb[:, :, :], chunks(w_oT)).then_inc(w2_in, 16)
            sp.dma_start(bo_sb[:, :], b_out.partition_broadcast(33)).then_inc(w2_in, 16)
            sp.dma_start(rw1_sb[:, :, :], chunks(rw1)).then_inc(w2_in, 16)
            sp.dma_start(rb1_sb[:, :], rb1.rearrange("(p a) -> p a", a=1)).then_inc(w2_in, 16)
            sp.dma_start(rw2_sb[:, 0:E], rw2).then_inc(w2_in, 16)
            sp.dma_start(rb2_sb[:, 0:E], rb2.partition_broadcast(P)).then_inc(w2_in, 16)
            be_v = be_sb[:, :].rearrange("p (e l n) -> p e l n", e=E, l=2)
            for layer, b in enumerate((eb1, eb2)):
                sp.dma_start(be_v[:, :, layer, :], b.partition_broadcast(128)).then_inc(w2_in, 16)

            def reload(it, at, expert_at):
                for g in range(G):
                    sp.wait_ge(xn_ready, it * G + (g + 1))
                    sp.dma_start(xring[:, g, :], x_t[:, at(g), :].rearrange("p a n -> p (a n)")).then_inc(x_in[g], 16)
                    if g == 3:
                        sp.wait_ge(split_l, it + 1)
                        expert(expert_at)
                    if g == 6:
                        store(it, 0)
                store(it, 1)

            def store(it, h):
                lo = HALF * h
                sp.wait_ge(xts_done, it * G + (1 + lo + HALF))
                sp.dma_start(xt_t[:, bass.ds(it * G + lo, HALF), :], xts[:, lo:lo + HALF, 0:XTW]).then_inc(xt_out[h], 16)
                sp.dma_start(al_t[:, bass.ds(it * G + lo, HALF), :], xts[:, lo:lo + HALF, XTW:GW]).then_inc(xt_out[h], 16)

            with sp.Fori(0, ITERS - 1) as it:
                reload(it, lambda g: bass.ds(it * G + (G + g), 1), bass.ds(it + 1, 1))
            reload(ITERS - 1, lambda g: slice(g, g + 1), slice(E - 1, E))

            with sp.Fori(0, GROUPS // 2 - 1) as it:
                for j in range(G):
                    sp.wait_ge(xn1_done, it * G + (j + 1))
                    sp.wait_ge(y2_done, it * G + (j + 1))
                    sp.dma_start(xring[:, j, :], x_t[:, bass.ds(it * G + (G + j), 1), :].rearrange("p a n -> p (a n)")).then_inc(x_in[j], 16)

            sp.wait_ge(tab_done, 1)
            sp.wait_ge(pool_c, 12)
            for b in range(2):
                sp.wait_ge(sc_out[b], OUT_G * (GROUPS // 2))
            sp.dma_start(tab0[E * REG:E * REG + S, :], skip_rows[:, D:ROW1]).then_inc(fill_out, 16)
            sp.dma_start(tab1[E * REG:E * REG + S, :], skip_rows[:, :]).then_inc(fill_out, 16)
            for k, tab in enumerate((tab0, tab1)):
                for e in range(E):
                    end = sp.value_load(fill[0:1, k, e:e + 1], min_val=0, max_val=(E - 1) * REG + N)
                    sp.dma_start(tab[bass.ds(end, S), :], skip_rows[:, ROW1 - tab.shape[1]:ROW1]).then_inc(fill_out, 16)
            sp.wait_ge(fill_out, 16 * (2 * E + 2))

            def load(k, u, at, turn=None):
                tab = (tab0, tab1)[k]
                first = sp.value_load(tab_row[0:1, k, at], min_val=0, max_val=E * REG)
                if turn is not None:
                    sp.wait_ge(z_out[u], turn * 16 + 16 * (k * (NT // U) + 1))
                sp.dma_start(rb[:, u, ROW1 - tab.shape[1]:ROW1], tab[bass.ds(first, S), :]).then_inc(r_in[u], 16)

            for k in range(2):
                if k == 1:
                    for u in range(U):
                        sp.wait_ge(z_out[u], 16 * (NT // U))
                    sp.wait_ge(xe_done, NT + LEAD)
                for u in range(U):
                    load(k, u, slice(u, u + 1))
                with sp.Fori(0, NT // U - 1) as it:
                    for u in range(U):
                        load(k, u, bass.ds(it * U + (U + u), 1), it)
                for u in range(LEAD):
                    load(k, u, slice(NT + u, NT + u + 1), NT // U - 1)
            for u in range(U):
                sp.wait_ge(z_out[u], 16 * 2 * (NT // U))

        @block.gpsimd
        def _(pool):
            pool.memset(ident[:, :], 0.0).then_inc(pool_c, 1)
            pool.memset(tri[:, :], 0.0).then_inc(pool_c, 1)
            pool.memset(ones[:, :], 1.0).then_inc(pool_c, 1)
            pool.wait_ge(pool_c, 3)
            pool.affine_select(out=ident[:, :], in_=ident[:, :], compare_op=ALU.not_equal, fill=1.0, base=0,
                               pattern=[[-1, 128]], channel_multiplier=1).then_inc(pool_c, 1)
            pool.affine_select(out=tri[:, :], in_=tri[:, :], compare_op=ALU.is_ge, fill=1.0, base=0,
                               pattern=[[-1, P]], channel_multiplier=1).then_inc(pool_c, 1)
            pool.iota(ebase[:, :, :], pattern=[[0, 2], [REG, EP]], base=0, channel_multiplier=0,
                      allow_small_or_imprecise_dtypes=True).then_inc(pool_c, 1)
            pool.iota(desc[:, :], pattern=[[-1, EP]], base=EP, channel_multiplier=0,
                      allow_small_or_imprecise_dtypes=True).then_inc(pool_c, 1)
            pool.iota(tok_all[:, :], pattern=[[1, T]], base=0, channel_multiplier=T).then_inc(pool_c, 1)
            pool.iota(nmul[:, :], pattern=[[S, NM]], base=0, channel_multiplier=0,
                      allow_small_or_imprecise_dtypes=True).then_inc(pool_c, 1)
            pool.iota(jj[:, :], pattern=[[1, NTT]], base=0, channel_multiplier=0,
                      allow_small_or_imprecise_dtypes=True).then_inc(pool_c, 1)
            pool.memset(skip_rows[:, 0:D + C_TOK], 0.0).then_inc(pool_c, 1)
            pool.iota(skip_rows[:, D + C_TOK:ROW1].bitcast(I32), pattern=[[0, 2]], base=SKIP,
                      channel_multiplier=0).then_inc(pool_c, 1)
            def wait_alone(semaphore, value):
                value = pool.to_reg(value)
                pool.wait_ge(pool_c, 1)
                pool.wait_ge(semaphore, value)

            with pool.Fori(0, E) as e:
                wait_alone(raw_in, e * RAW + RAW)
                pool.tensor_copy(we_h[:, bass.ds(e * EW, EW)], raw_e[:, :]).then_inc(split_h, 1)
                wait_alone(split_h, e + 1)
                pool.tensor_tensor(we_l[:, bass.ds(e * EW, EW)], raw_e[:, :],
                                   we_h[:, bass.ds(e * EW, EW)].bitcast(FP32), ALU.subtract).then_inc(split_l, 1)

            def gathers(n, b, at, turn):
                if turn is not None:
                    pool.wait_ge(g_in[b], turn * IN_G + IN_G)
                pool.tensor_copy(idx_s[:, b, :], src_all[:, at]).then_inc(idx_done, 1)
                pool.tensor_copy(idx_d[:, b, :], dst_all[:, at]).then_inc(idx_done, 1)
                wait_alone(idx_done, n * 2 + 2)
                if turn is not None:
                    wait_alone(gp_done, n * Q - Q)
                for g in range(Q):
                    pool.indirect_dma_start(out=alg[:, b, g, :], out_offset=None, in_=al_tab,
                                            in_offset=bass.IndirectOffsetOnAxis(ap=idx_s[:, b, g:g + 1], axis=0)
                                            ).then_inc(g_in[b], 16)
                    pool.indirect_dma_start(out=xtg[:, b, g, :], out_offset=None, in_=xt_tab,
                                            in_offset=bass.IndirectOffsetOnAxis(ap=idx_d[:, b, g:g + 1], axis=0)
                                            ).then_inc(g_in[b], 16)

            def scatters(n, b):
                wait_alone(row_ready, n + 1)
                for g in range(Q):
                    pool.indirect_dma_start(out=tab0, out_offset=bass.IndirectOffsetOnAxis(ap=pos0[:, b, g:g + 1], axis=0),
                                            in_=xr[:, b, g, :], in_offset=None).then_inc(sc_out[b], 16)

            for h in range(2):
                pool.wait_ge(xt_out[h], 16 + 32 * ITERS)
            pool.wait_ge(w2_in, W2)
            for b in range(2):
                gathers(b, b, slice(b * Q, b * Q + Q), None)
            with pool.Fori(0, GROUPS // 2 - 1) as it:
                for b in range(2):
                    gathers(it * 2 + (2 + b), b, bass.ds(it * G + (2 + b) * Q, Q), it)
                    scatters(it * 2 + b, b)
            for b in range(2):
                scatters(GROUPS - 2 + b, b)

            for k in range(2):
                with pool.Fori(0, NT // U) as it:
                    for u in range(U):
                        wait_alone(z_done, it * U + (k * NT + u + 1))
                        if k == 0:
                            pool.indirect_dma_start(
                                out=tab1, out_offset=bass.IndirectOffsetOnAxis(
                                    ap=rb[:, u, D + C_POS:D + C_POS + 1].bitcast(I32), axis=0),
                                in_=rb[:, u, :], in_offset=None, bounds_check=E * REG - 1, oob_is_err=False
                            ).then_inc(z_out[u], 16)
                        else:
                            pool.indirect_dma_start(
                                out=out, out_offset=bass.IndirectOffsetOnAxis(
                                    ap=rb[:, u, D + C_TOK:D + C_TOK + 1].bitcast(I32), axis=0),
                                in_=rb[:, u, 0:D], in_offset=None, bounds_check=N - 1, oob_is_err=False
                            ).then_inc(z_out[u], 16)

        @block.scalar
        def _(act):
            def stdev(h, value):
                lo = HALF * h
                act.wait_ge(ag_done, value)
                act.activation(sd[:, lo:lo + HALF], mv[:, lo:lo + HALF, 1], ACT.Sqrt, bias=eps_sb[0:P, 0:1]).then_inc(sd_done, 1)

            def upper(b):
                act.activation(x_h[:, b, :, 0:P], half_t(pt[b])[:, :, 0:P], ACT.Copy).then_inc(xh_ready, 1)

            act.sem_inc(xts_done, 1)
            for h in range(2):
                act.sem_inc(xt_out[h], 16)
            act.wait_ge(prep, PREP_EPS)
            stdev(0, AHEAD)
            act.wait_ge(prep, PREP_X)
            act.wait_ge(pt_ready, 1)
            upper(0)
            with act.Fori(0, ITERS) as it:
                for g in range(G):
                    b = g % 2
                    t = it * G + g
                    act.wait_ge(k_ready, t + 1)
                    act.activation(sq[:, 0:MI], kv_ps[b][0:P, 0:MI], ACT.Square).then_inc(sqk_done, 1)
                    act.wait_ge(pt_ready, t + 2)
                    upper(1 - b)
                    act.wait_ge(v_ready, t + 1)
                    act.activation(sq[:, MI:2 * MI], kv_ps[b][0:P, MI:2 * MI], ACT.Square).then_inc(sqv_done, 1)
                    act.activation(vs[:, b, :], kv_ps[b][0:P, MI:2 * MI], ACT.Copy)
                    if g % HALF == 0:
                        act.wait_ge(xt_out[g // HALF], it * 32 + 16)
                    act.wait_ge(xt_ready, t + 1)
                    act.activation(xts[:, g, :], xt_ps[0:P, 0:GW], ACT.Copy).then_inc(xts_done, 1)
                    act.wait_ge(pr_done, t + 1)
                    act.activation(sr[:, :], pr[:, :], ACT.Sqrt).then_inc(sr_done, 1)
                    if g in (2, 7):
                        stdev(1 if g == 2 else 0, it * G + (AHEAD + g + 1))

            act.wait_ge(a_done, 1)
            act.activation(a_sb, kv_ps[0][:, :].rearrange("p (b n) -> p b n", b=MI // 128), ACT.Copy,
                           scale=1.0 / N).then_inc(as_done, 1)
            act.wait_ge(m_done, 1)
            act.activation(mix_w[:, :, :], pt[0][:, :].rearrange("p (c n) -> p c n", c=KC), ACT.Copy).then_inc(mw_done, 1)

            def step(a, b, p):
                if b is not None:
                    o = slice((1 - p) * Q, (2 - p) * Q)
                    act.wait_ge(ag2_done, b * Q + Q)
                    act.activation(sd[:, o], mv[:, o, 1], ACT.Sqrt, bias=eps_sb[0:P, 0:1]).then_inc(sd2_done, 1)
                if a is not None:
                    act.wait_ge(al_ready, a + 1)
                    act.activation(al[:, 2, :, :], al[:, 1, :, :], ACT.Exp).then_inc(ex_done, 1)

                def normal1(g):
                    j = p * Q + g
                    act.wait_ge(x_in[j], a // 2 * 16 + 16 * (ITERS + 1))
                    if g >= 2:
                        act.wait_ge(t1_done, a * Q + (g - 1))
                    act.activation(xn[:, g % 2, :], xring[:, j, :], ACT.Identity, bias=nmr[:, j:j + 1],
                                   scale=rs[:, j:j + 1]).then_inc(xn1_done, 1)

                def normal2(g):
                    if g >= 2:
                        act.wait_ge(t2_done, b * Q + (g - 1))
                    act.activation(xnr[:, g % 2, :], xr[:, 1 - p, g, 0:D], ACT.Identity,
                                   bias=xr[:, 1 - p, g, C_NMR:C_NMR + 1],
                                   scale=xr[:, 1 - p, g, C_R:C_R + 1]).then_inc(xn2_done, 1)

                def hidden(g):
                    act.wait_ge(rh_done, b * Q + (g + 1))
                    act.activation(rhT[:, g % 2, :], rh_ps[g % 2][:, 0:P], ACT.Relu, bias=rb1_sb[:, 0:1]).then_inc(rhT_done, 1)

                if a is not None:
                    act.wait_ge(rs2_done, a * 2 + 2)
                    normal1(0)
                if b is not None:
                    act.wait_ge(fin2_done, b * 2 + 2)
                    normal2(0)
                for g in range(Q):
                    if a is not None:
                        if g + 1 < Q:
                            normal1(g + 1)
                        act.wait_ge(t1_done, a * Q + (g + 1))
                        act.activation(xT[:, g % 2, :, 0:P], half_t(pt[0])[:, :, 0:P], ACT.Copy).then_inc(xT1_done, 1)
                    if b is not None:
                        for q in B_TILES[g]:
                            if q + 1 < Q:
                                normal2(q + 1)
                            act.wait_ge(t2_done, b * Q + (q + 1))
                            act.activation(xTr[:, q % 2, :, 0:P], half_t(pt[1])[:, :, 0:P], ACT.Copy).then_inc(xT2_done, 1)
                            if q > 0:
                                hidden(q - 1)
                        if g == 2:
                            hidden(Q - 1)
                            act.wait_ge(lgx_ready, b + 1)
                            act.activation(lg[:, 2, :, :], lg[:, 1, :, :], ACT.Exp).then_inc(ex2_done, 1)
                if b is not None:
                    act.wait_ge(d_ready, b + 1)
                    act.activation(tw[:, 5, :], tw[:, 4, :], ACT.Exp).then_inc(ex3_done, 1)

            groups(act, step)

            def normal(k, j, it):
                u, turn = j % U, j // U
                loads = NT // U + (1 if u < LEAD else 0)
                act.wait_ge(r_in[u], it * 16 + 16 * (k * loads + turn + 1))
                act.activation(xe[:, j % 3, :], rb[:, u, D:2 * D], ACT.Identity,
                               bias=rb[:, u, D + C_NMR:D + C_NMR + 1],
                               scale=rb[:, u, D + C_R:D + C_R + 1]).then_inc(xe_done, 1)

            def upper3(layer, lane, n):
                act.wait_ge(et_done, n)
                act.activation(x_h[:, lane, :, :], half_t(t_ps[lane]), ACT.Relu if layer else ACT.Copy).then_inc(eh_done, 1)

            for k in range(2):
                nt = k * (NT * 3 + 2)
                for j in range(LEAD):
                    normal(k, j, 0)
                for j in range(2):
                    upper3(0, j, nt + j + 1)
                with act.Fori(0, NT // U) as it:
                    n, j = 2, 3
                    for _ in range(U // 3):
                        for kind, layer, lane in ORDER:
                            if kind == "transpose":
                                if layer == 0:
                                    normal(k, j, it)
                                    j += 1
                                n += 1
                                upper3(layer, lane, it * (3 * U) + (nt + n))

        @block.vector
        def _(dve):
            done = [0]

            def link(ins):
                done[0] += 1
                ins.then_inc(prep, 1)
                dve.wait_ge(prep, done[0])

            def stats(j, value):
                dve.wait_ge(x_in[j], value)
                dve.bn_stats(st[:, j, :], xring[:, j, :]).then_inc(bs_done, 1)

            def wait_alone(semaphore, value):
                value = dve.to_reg(value)
                dve.wait_ge(prep, 1)
                dve.wait_ge(semaphore, value)

            def aggregate(j, value):
                wait_alone(bs_done, value)
                dve.bn_aggr(mv[:, j, :], st[:, j, :]).then_inc(ag_done, 1)

            def finish(h, n, at):
                lo = HALF * h
                part = slice(lo, lo + HALF)
                dve.wait_ge(sd_done, n + 1)
                dve.reciprocal(rs[:, part], sd[:, part]).then_inc(fin_done, 1)
                dve.wait_ge(fin_done, n * 4 + 1)
                dve.scalar_tensor_tensor(nmr[:, part], mv[:, part, 0], -1.0, rs[:, part], ALU.mult, ALU.mult).then_inc(fin_done, 1)
                dve.wait_ge(fin_done, n * 4 + 2)
                dve.tensor_copy(rs_all[:, at], rs[:, part]).then_inc(fin_done, 1)
                dve.tensor_copy(nmr_all[:, at], nmr[:, part]).then_inc(fin_done, 1)

            def normal(j, b):
                dve.tensor_scalar(xn[:, b, :], xring[:, j, :], rs[:, j:j + 1], nmr[:, j:j + 1],
                                  ALU.mult, ALU.add).then_inc(xn_ready, 1)

            def lower(b):
                dve.tensor_tensor(x_l[:, b, :, 0:P], half_t(pt[b])[:, :, 0:P], x_h[:, b, :, 0:P].bitcast(FP32),
                                  ALU.subtract).then_inc(xl_ready, 1)

            link(dve.memset(eps_sb[:, :], EPS))
            assert done[0] == PREP_EPS
            for j in range(AHEAD):
                stats(j, 16)
            for j in range(AHEAD):
                aggregate(j, j + 1)
            for buf in (x_h, x_l):
                dve.memset(buf[:, :, :, :].bitcast(FP32), 0.0).then_inc(prep, 1)
                done[0] += 1
            assert done[0] == PREP_X
            dve.wait_ge(prep, PREP_X)
            finish(0, 0, slice(0, HALF))
            for j in range(2):
                normal(j, j)

            dve.wait_ge(w1_in, W1)
            kv_v = kv_raw.rearrange("p c (h n) -> p (c h) n", n=MC)
            mean_v = kv_mean.rearrange("p c h -> p (c h)")
            link(dve.reduce_sum(mean_v, kv_v, axis=AX.X))
            link(dve.tensor_scalar(mean_v, mean_v, -1.0 / MC, None, ALU.mult))
            link(dve.tensor_tensor(kv_v, kv_v, mean_v.unsqueeze(2).to_broadcast([128, KC * 2 * MH, MC]), ALU.add))
            link(dve.tensor_copy(wkv_h[:, :, :], kv_raw))
            dve.tensor_tensor(wkv_l[:, :, :], kv_raw, wkv_h[:, :, :].bitcast(FP32), ALU.subtract).then_inc(prep, 1)
            done[0] += 1
            for s in range(2):
                link(dve.tensor_tensor(att_pr, wg_raw[:, :, 0:D], att_bc[:, s, :].unsqueeze(1).to_broadcast([128, KC, D]), ALU.mult))
                link(dve.reduce_sum(wg_raw[:, :, D + GH * s:D + GH * (s + 1)], att_pr.rearrange("p c (h n) -> p c h n", n=GC), axis=AX.X))
            link(dve.tensor_copy(wg_h[:, :, :], wg_raw))
            link(dve.tensor_tensor(wg_l[:, :, :], wg_raw, wg_h[:, :, :].bitcast(FP32), ALU.subtract))
            dve.wait_ge(b3_in, 32)
            link(dve.memset(b3_hl[:, :].bitcast(FP32), 0.0))
            link(dve.memset(sel_hl[:, :].bitcast(FP32), 0.0))
            link(dve.tensor_copy(b3_hl[0:1, :], b3_raw[0:1, :]))
            link(dve.tensor_copy(b3_hl[32:33, :], b3_raw[32:33, :]))
            link(dve.tensor_tensor(b3_hl[32:33, :], b3_raw[32:33, :], b3_hl[32:33, :].bitcast(FP32), ALU.subtract))
            for q in (0, 32):
                link(dve.memset(sel_hl[q:q + 1, :].bitcast(FP32), 1.0))
            link(dve.memset(rw2_sb[:, E:EP], 0.0))
            link(dve.memset(rb2_sb[:, E:EP], -1e30))
            link(dve.memset(base[:, :, :], 0.0))
            dve.wait_ge(pool_c, 12)
            link(dve.tensor_copy(base[0:1, :, :], ebase[0:1, :, :]))
            link(dve.memset(dotsT[:, :, :], 0.0))
            link(dve.memset(vs[:, 1, :], 0.0))
            dve.memset(ks[:, 1, :], 0.0).then_inc(ks_ready, 1)
            assert done[0] == PREP_ALL, done[0]
            dve.wait_ge(xh_ready, 1)
            lower(0)

            with dve.Fori(0, ITERS) as it:
                for g in range(G):
                    b = g % 2
                    t = it * G + g
                    j = (g + AHEAD) % G
                    stats(j, it * 16 + 16 * (1 + (g + AHEAD) // G))
                    dve.wait_ge(sqk_done, t + 1)
                    dve.reduce_sum(ss[:, 0:MH], sq[:, 0:MI].rearrange("p (h n) -> p h n", n=MC), axis=AX.X).then_inc(red_done, 1)
                    aggregate(j, t + (AHEAD + 1))
                    dve.wait_ge(xh_ready, t + 2)
                    lower(1 - b)
                    dve.wait_ge(sqv_done, t + 1)
                    dve.reduce_sum(ss[:, MH:2 * MH], sq[:, MI:2 * MI].rearrange("p (h n) -> p h n", n=MC), axis=AX.X).then_inc(red_done, 1)
                    dve.wait_ge(red_done, t * 2 + 2)
                    dve.tensor_scalar(sse[:, :], ss[:, :], 1.0 / MC, EPS, ALU.mult, ALU.add).then_inc(sse_done, 1)
                    dve.wait_ge(sse_done, t + 1)
                    dve.tensor_tensor(pr[:, :], sse[:, 0:MH], sse[:, MH:2 * MH], ALU.mult).then_inc(pr_done, 1)
                    if g in (3, 8):
                        h = 1 if g == 3 else 0
                        finish(h, it * 2 + (1 if g == 3 else 2), bass.ds(it * G + (HALF if g == 3 else G), HALF))
                        dve.wait_ge(fin_done, it * 8 + (8 if g == 3 else 12))
                    dve.wait_ge(pt_ready, t + 1)
                    normal((g + 2) % G, b)
                    dve.wait_ge(sr_done, t + 1)
                    dve.reciprocal(rkv[:, :], sr[:, :]).then_inc(rc_done, 1)
                    dve.wait_ge(rc_done, t + 1)
                    dve.tensor_tensor(ks[:, b, :].rearrange("p (h n) -> p h n", n=MC),
                                      kv_ps[b][0:P, 0:MI].rearrange("p (h n) -> p h n", n=MC),
                                      rkv[:, :].unsqueeze(2).to_broadcast([P, MH, MC]), ALU.mult).then_inc(ks_ready, 1)

            def mlink(ins):
                mix_steps[0] += 1
                ins.then_inc(bo_done, 1)
                dve.wait_ge(bo_done, mix_steps[0])

            mix_steps = [0]
            dve.wait_ge(w2_in, W2)
            mlink(dve.memset(bo_hl[:, :].bitcast(FP32), 0.0))
            mlink(dve.tensor_copy(bo_hl[0:1, :], bo_sb[0:1, :]))
            mlink(dve.tensor_copy(bo_hl[32:33, :], bo_sb[32:33, :]))
            mlink(dve.tensor_tensor(bo_hl[32:33, :], bo_sb[32:33, :], bo_hl[32:33, :].bitcast(FP32), ALU.subtract))

            dve.wait_ge(dots_done, 1)
            d_v = d_ps[:, :].rearrange("p (b n) -> p b n", b=MI // 128)
            for q in range(2):
                dve.tensor_copy(dotsT[MC * q:MC * (q + 1), :, MC * q:MC * (q + 1)],
                                d_v[MC * q:MC * (q + 1), :, MC * q:MC * (q + 1)]).then_inc(dT_done, 1)

            def bc(ap, n):
                return ap.unsqueeze(len(ap.shape)).to_broadcast([*ap.shape, n])

            for h in range(2):
                dve.wait_ge(xt_out[h], 16 + 32 * ITERS)

            def step(a, b, p):
                if b is not None:
                    o = slice((1 - p) * Q, (2 - p) * Q)
                    row = xr[:, 1 - p, :, :]
                    dve.wait_ge(sd2_done, b + 1)
                    dve.reciprocal(row[:, :, C_R], sd[:, o]).then_inc(fin2_done, 1)
                    dve.wait_ge(fin2_done, b * 2 + 1)
                    dve.scalar_tensor_tensor(row[:, :, C_NMR], mv[:, o, 0], -1.0, row[:, :, C_R], ALU.mult, ALU.mult).then_inc(fin2_done, 1)
                parts = {} if b is None else route(b, 1 - p)
                if a is not None:
                    sums(a, p, parts)
                else:
                    for g in (2, 3, 4):
                        parts[g]()
                if b is not None:
                    parts["end"]()

            def sums(a, p, parts):
                n = [0]

                def al_link(ins):
                    n[0] += 1
                    ins.then_inc(al_step, 1)
                    dve.wait_ge(al_step, a * AL_STEPS + n[0])

                own = slice(p * Q, p * Q + Q)
                at = bass.ds(a * Q, Q)
                dve.tensor_copy(rs[:, own], rs_all[:, at]).then_inc(rs2_done, 1)
                dve.tensor_copy(nmr[:, own], nmr_all[:, at]).then_inc(rs2_done, 1)
                dve.wait_ge(g_in[p], a // 2 * IN_G + IN_G)
                al_link(dve.tensor_tensor(al[:, 0, :, :], alg[:, p, :, :], xtg[:, p, :, D:XTW], ALU.add))
                al_link(dve.scalar_tensor_tensor(al[:, 1, :, :], al[:, 0, :, :], 0.01, al[:, 0, :, :], ALU.mult, ALU.max))
                al_link(dve.reduce_max(am[:, 0, :], al[:, 1, :, :], axis=AX.X))
                dve.tensor_tensor(al[:, 1, :, :], al[:, 1, :, :], bc(am[:, 0, :], GH), ALU.subtract).then_inc(al_ready, 1)
                dve.wait_ge(ex_done, a + 1)
                al_link(dve.reduce_sum(am[:, 1, :], al[:, 2, :, :], axis=AX.X))
                al_link(dve.reciprocal(am[:, 2, :], am[:, 1, :]))
                al_link(dve.tensor_tensor(al[:, 3, :, :], al[:, 2, :, :], bc(am[:, 2, :], GH), ALU.mult))
                assert n[0] == AL_STEPS

                def graph(g):
                    dve.tensor_tensor(gp[:, g % 2, :].rearrange("p (h n) -> p h n", n=GC),
                                      xtg[:, p, g, 0:D].rearrange("p (h n) -> p h n", n=GC),
                                      bc(al[:, 3, g, :], GC), ALU.mult).then_inc(gp_done, 1)

                def graph_sum(g):
                    dve.wait_ge(gp_done, a * Q + (g + 1))
                    dve.reduce_sum(gt[:, g % 2, :], gp[:, g % 2, :].rearrange("p (h n) -> p n h", n=GC), axis=AX.X).then_inc(gt_done, 1)

                def plus_graph(g):
                    dve.wait_ge(gt_done, a * Q + (g + 1))
                    dve.wait_ge(x_in[p * Q + g], a // 2 * 16 + 16 * (ITERS + 1))
                    dve.tensor_tensor(y2[:, g % 2, :].rearrange("p (h n) -> p h n", n=GC),
                                      xring[:, p * Q + g, :].rearrange("p (h n) -> p h n", n=GC),
                                      gt[:, g % 2, :].unsqueeze(1).to_broadcast([P, GH, GC]), ALU.add).then_inc(y2_done, 1)

                def plus_mix(g):
                    dve.wait_ge(y2_done, a * Q + (g + 1))
                    dve.wait_ge(ma_done, a * Q + (g + 1))
                    dve.tensor_tensor(xr[:, p, g, 0:D], ma_ps[g % 2][0:P, 0:D], y2[:, g % 2, :], ALU.add).then_inc(x2_done, 1)

                def stats2(g):
                    dve.wait_ge(x2_done, a * Q + (g + 1))
                    dve.bn_stats(st[:, p * Q + g, :], xr[:, p, g, 0:D]).then_inc(bs2_done, 1)

                def aggregate2(g):
                    wait_alone(bs2_done, a * Q + (g + 1))
                    dve.bn_aggr(mv[:, p * Q + g, :], st[:, p * Q + g, :]).then_inc(ag2_done, 1)

                for g in range(Q + 1):
                    if g < Q:
                        graph(g)
                    if g > 0:
                        if g == 1 and not (isinstance(a, int) and a < 2):
                            dve.wait_ge(sc_out[p], a // 2 * OUT_G)
                        plus_mix(g - 1)
                    if g < Q:
                        graph_sum(g)
                    if g > 0:
                        stats2(g - 1)
                    if g < Q:
                        plus_graph(g)
                    if g > 0:
                        aggregate2(g - 1)
                    if parts and g in (2, 3, 4):
                        parts[g]()

            def route(b, p):
                row = xr[:, p, :, :]
                n = [0]

                def link(ins):
                    n[0] += 1
                    ins.then_inc(step_done, 1)
                    dve.wait_ge(step_done, b * R_STEPS + n[0])

                def probabilities():
                    dve.wait_ge(lg_done, b * Q + Q)
                    link(dve.reduce_max(tw[:, 0, :], lg_ps, axis=AX.X))
                    dve.tensor_tensor(lg[:, 1, :, :], lg_ps, bc(tw[:, 0, :], EP), ALU.subtract).then_inc(lgx_ready, 1)
                    dve.tensor_copy(row[:, :, C_TOK].bitcast(I32), tok_all[:, bass.ds(b * Q, Q)])
                    dve.wait_ge(ex2_done, b + 1)
                    link(dve.reduce_sum(tw[:, 1, :], lg[:, 2, :, :], axis=AX.X))
                    link(dve.reciprocal(tw[:, 1, :], tw[:, 1, :]))
                    link(dve.tensor_tensor(lg[:, 3, :, :], lg[:, 2, :, :], bc(tw[:, 1, :], EP), ALU.mult))

                def choose(k, prob):
                    link(dve.reduce_max(tw[:, 2 + k, :], prob, axis=AX.X))
                    link(dve.tensor_tensor(lg[:, 0, :, :], prob, bc(tw[:, 2 + k, :], EP), ALU.is_equal))
                    link(dve.tensor_tensor(lg[:, 1, :, :], lg[:, 0, :, :], desc[:, :].unsqueeze(1).to_broadcast([P, Q, EP]), ALU.mult))
                    link(dve.reduce_max(tw[:, 6, :], lg[:, 1, :, :], axis=AX.X))
                    return dve.tensor_tensor(oh[:, :, k, :], lg[:, 1, :, :], bc(tw[:, 6, :], EP), ALU.is_equal)

                def first_choice():
                    link(choose(0, lg[:, 3, :, :]))

                def second_choice():
                    link(dve.scalar_tensor_tensor(lg[:, 2, :, :], oh[:, :, 0, :], -4.0, lg[:, 3, :, :], ALU.mult, ALU.add))
                    choose(1, lg[:, 2, :, :]).then_inc(oh_ready, 1)
                    dve.tensor_tensor(tw[:, 4, :], tw[:, 3, :], tw[:, 2, :], ALU.subtract).then_inc(d_ready, 1)

                def slots():
                    dve.wait_ge(ex3_done, b + 1)
                    link(dve.tensor_scalar(tw[:, 7, :], tw[:, 5, :], 1.0, None, ALU.add))
                    link(dve.reciprocal(row[:, :, C_W], tw[:, 7, :]))
                    dve.tensor_tensor(row[:, :, C_W + 1], tw[:, 5, :], row[:, :, C_W], ALU.mult)
                    link(dve.reduce_sum(bsum[:, :, :], oh[:, :, :, :].rearrange("p g k e -> p k e g"), axis=AX.X))
                    dve.wait_ge(rk_done, b + 1)
                    link(dve.tensor_tensor(rk[:, :, :, :], rk_ps, oh[:, :, :, :], ALU.mult))
                    link(dve.reduce_sum(posf[:, :, :], rk[:, :, :, :], axis=AX.X))
                    dve.tensor_copy(pos0[:, p, :], posf[:, :, 0])
                    dve.tensor_copy(row[:, :, C_POS].bitcast(I32), posf[:, :, 1]).then_inc(row_ready, 1)
                    link(dve.tensor_tensor(base[:, :, :], base[:, :, :], bsum[:, :, :], ALU.add))
                    assert n[0] == R_STEPS, n[0]

                return {2: probabilities, 3: first_choice, 4: second_choice, "end": slots}

            groups(dve, step)

            tn = [0]

            def tlink(ins):
                tn[0] += 1
                ins.then_inc(tstep, 1)
                dve.wait_ge(tstep, tn[0])

            dve.wait_ge(cnt_done, 1)
            ends_ps = d_ps[0:1, 0:2 * EP].rearrange("p (k e) -> p k e", k=2)
            tlink(dve.tensor_tensor(cnt[:, :, :], ends_ps, ebase[0:1, :, :], ALU.subtract))
            dve.tensor_copy(fill[:, :, :], ends_ps)
            ce = cnt[:, :, :].rearrange("p k e -> p (k e)")
            nc_v = ncmp.rearrange("p k e m -> p (k e) m")
            tlink(dve.tensor_tensor(nc_v, bc(ce, NM), nmul[:, :].unsqueeze(1).to_broadcast([1, 2 * EP, NM]), ALU.is_gt))
            tlink(dve.reduce_sum(ntl[:, :, :].rearrange("p k e -> p (k e)"), nc_v, axis=AX.X))
            tlink(dve.tensor_copy(ends[:, :, 0:1], ntl[:, :, 0:1]))
            for e in range(1, E):
                tlink(dve.tensor_tensor(ends[:, :, e:e + 1], ends[:, :, e - 1:e], ntl[:, :, e:e + 1], ALU.add))
            for k in range(2):
                tlink(dve.tensor_tensor(ge[:, k, :, :], bc(jj[:, :], E), ends[:, k, 0:E].unsqueeze(1).to_broadcast([1, NTT, E]), ALU.is_ge))
                tlink(dve.reduce_sum(tf[:, 0, k, :], ge[:, k, :, :], axis=AX.X))
                tlink(dve.tensor_tensor(gn[:, k, :, :], ge[:, k, :, :], ntl[:, k, 0:E].unsqueeze(1).to_broadcast([1, NTT, E]), ALU.mult))
                tlink(dve.reduce_sum(tf[:, 1, k, :], gn[:, k, :, :], axis=AX.X))
                tlink(dve.tensor_tensor(tf[:, 2, k, :], jj[:, :], tf[:, 1, k, :], ALU.subtract))
                tlink(dve.tensor_scalar(tf[:, 3, k, :], ge[:, k, :, E - 1], -1.0, 1.0, ALU.mult, ALU.add))
                tlink(dve.tensor_tensor(tf[:, 4, k, :], tf[:, 2, k, :], tf[:, 3, k, :], ALU.mult))
                tlink(dve.tensor_scalar(tf[:, 5, k, :], tf[:, 4, k, :], float(S), None, ALU.mult))
                tlink(dve.scalar_tensor_tensor(tf[:, 6, k, :], tf[:, 0, k, :], float(REG), tf[:, 5, k, :], ALU.mult, ALU.add))
                tlink(dve.tensor_scalar(tf[:, 7, k, :], tf[:, 0, k, :], float(E - 1), None, ALU.min))
                tlink(dve.tensor_copy(tab_row[:, k, :], tf[:, 6, k, :]))
                tlink(dve.tensor_copy(tab_e[:, k, :, 0:3], tf[:, 7, k, :].rearrange("p (j l) -> p j l", l=3)))
            dve.sem_inc(tab_done, 1)

            e_regs = [dve.alloc_register(f"dve_e{i}") for i in range(3)]

            def lower3(layer, lane, n):
                dve.wait_ge(eh_done, n)
                hi = x_h[:, lane, :, :].bitcast(FP32)
                if layer:
                    ins = dve.scalar_tensor_tensor(x_l[:, lane, :, :], half_t(t_ps[lane]), 0.0, hi, ALU.max, ALU.subtract)
                else:
                    ins = dve.tensor_tensor(x_l[:, lane, :, :], half_t(t_ps[lane]), hi, ALU.subtract)
                ins.then_inc(el_done, 1)

            for k in range(2):
                nt, nl = k * (NT * 3 + 2), k * NT * 3
                for j in range(2):
                    lower3(0, j, nt + j + 1)
                with dve.Fori(0, NT // U) as it:
                    n, m, j, i = 2, 0, 0, 0
                    for group in range(U // 3):
                        es = experts(dve, e_regs, k, it * (U // 3) + group)
                        for kind, layer, lane in ORDER:
                            if kind == "transpose":
                                n += 1
                                lower3(layer, lane, it * (3 * U) + (nt + n))
                                continue
                            m += 1
                            u = group * 3 + lane
                            dve.wait_ge(l_done, it * (3 * U) + (nl + m))
                            if layer < 3:
                                at = es[lane] * (2 * F) + (layer - 1) * F
                                dve.tensor_tensor(hs[:, lane, :], l_ps[lane][:, 0:F], be_sb[:, bass.ds(at, F)], ALU.add).then_inc(hs_done, 1)
                            else:
                                before = rb[:, u, D:2 * D] if k == 0 else rb[:, u, 0:D]
                                dve.scalar_tensor_tensor(rb[:, u, 0:D], l_ps[lane][:, 0:D],
                                                         rb[:, u, D + C_W + k:D + C_W + k + 1], before,
                                                         ALU.mult, ALU.add).then_inc(z_done, 1)

        @block.tensor
        def _(pe):
            def transpose(bank, rows, p):
                for c in range(KC):
                    last = pe.transpose(half_t(bank)[:, c, 0:p], rows[:, c * 128:(c + 1) * 128], ident[0:p, 0:p])
                return last

            def product(outp, lane, w_h, w_l, xl, ready, add=None):
                first = True
                if add is not None:
                    pe.matmul(outp, add[0], add[1], start=True, stop=False)
                    first = False
                for c in range(KC):
                    pe.matmul(outp, x_h[:, lane, c, :], w_h(c), start=first, stop=False)
                    first = False
                    pe.matmul(outp, x_h[:, lane, c, :], w_l(c), start=False, stop=False)
                if ready is not None:
                    pe.wait_ge(xl, ready)
                for c in range(KC):
                    last = pe.matmul(outp, x_l[:, lane, c, :], w_h(c), start=False, stop=c == KC - 1)
                return last

            pe.wait_ge(pool_c, 5)
            pe.wait_ge(xn_ready, 1)
            transpose(pt[0], xn[:, 0, :], P).then_inc(pt_ready, 1)
            pe.wait_ge(ks_ready, 1)
            pe.wait_ge(prep, PREP_ALL)
            pe.matmul(d_ps[:, :], vs[:, 1, 0:128], ks[:, 1, :], start=True, stop=False, skip_group_check=True)

            def dots(b):
                for q in range(MI // 128):
                    at = slice(q * 128, (q + 1) * 128)
                    last = pe.matmul(d_ps[:, at], vs[:, b, at], ks[:, b, at], start=False, stop=False, skip_group_check=True)
                return last

            with pe.Fori(0, ITERS) as it:
                for g in range(G):
                    b = g % 2
                    t = it * G + g
                    pe.wait_ge(xh_ready, t + 1)
                    product(kv_ps[b][:, 0:MI], b, lambda c: wkv_h[:, c, 0:MI], lambda c: wkv_l[:, c, 0:MI],
                            xl_ready, t + 1).then_inc(k_ready, 1)
                    product(kv_ps[b][:, MI:2 * MI], b, lambda c: wkv_h[:, c, MI:2 * MI], lambda c: wkv_l[:, c, MI:2 * MI],
                            None, None).then_inc(v_ready, 1)
                    pe.wait_ge(xn_ready, t + 2)
                    transpose(pt[1 - b], xn[:, 1 - b, :], P).then_inc(pt_ready, 1)
                    pe.wait_ge(xts_done, t + 1)
                    product(xt_ps[:, 0:GW], b, lambda c: wg_h[:, c, :], lambda c: wg_l[:, c, :],
                            None, None).then_inc(xt_ready, 1)
                    pe.wait_ge(ks_ready, t + 1)
                    dots(1 - b)
            pe.wait_ge(ks_ready, T + 1)
            dots((T - 1) % 2).then_inc(dots_done, 1)

            pe.wait_ge(w2_in, W2)
            pe.wait_ge(dT_done, 2)
            for q in range(MI // 128):
                last = pe.matmul(kv_ps[0][:, q * D:(q + 1) * D], dotsT[:, q, :], woT_sb[:, q, :], start=True, stop=True)
            last.then_inc(a_done, 1)
            pe.wait_ge(as_done, 1)
            pe.wait_ge(xl_ready, T + 1)
            for c in range(KC):
                for q in range(MI // 128):
                    last = pe.matmul(pt[0][:, c * D:(c + 1) * D], wq_sb[:, q, c * 128:(c + 1) * 128], a_sb[:, q, :],
                                     start=q == 0, stop=q == MI // 128 - 1)
            last.then_inc(m_done, 1)
            pe.wait_ge(mw_done, 1)
            pe.wait_ge(bo_done, 4)

            def step(a, b, p):
                def t1(g):
                    pe.wait_ge(xn1_done, a * Q + (g + 1))
                    if not (g == 0 and isinstance(a, int) and a == 0):
                        pe.wait_ge(xT1_done, a * Q + g)
                    transpose(pt[0], xn[:, g % 2, :], P).then_inc(t1_done, 1)

                def mix(g):
                    out_ps = ma_ps[g % 2][0:P, 0:D]
                    pe.wait_ge(xT1_done, a * Q + (g + 1))
                    if not (g < 2 and isinstance(a, int) and a == 0):
                        pe.wait_ge(x2_done, a * Q + (g - 1))
                    pe.matmul(out_ps, sel_hl[:, 0:P], bo_hl[:, :], start=True, stop=False)
                    for c in range(KC):
                        last = pe.matmul(out_ps, xT[:, g % 2, c, 0:P], mix_w[:, c, :], start=False, stop=c == KC - 1)
                    last.then_inc(ma_done, 1)

                def t2(g):
                    pe.wait_ge(xn2_done, b * Q + (g + 1))
                    if not (g == 0 and isinstance(b, int) and b == 0):
                        pe.wait_ge(xT2_done, b * Q + g)
                    transpose(pt[1], xnr[:, g % 2, :], P).then_inc(t2_done, 1)

                def hidden(g):
                    pe.wait_ge(xT2_done, b * Q + (g + 1))
                    for c in range(KC):
                        last = pe.matmul(rh_ps[g % 2][:, 0:P], rw1_sb[:, c, :], xTr[:, g % 2, c, 0:P], start=c == 0, stop=c == KC - 1)
                    last.then_inc(rh_done, 1)

                def logits(g):
                    pe.wait_ge(rhT_done, b * Q + (g + 1))
                    pe.matmul(lg_ps[:, g, :], rhT[:, g % 2, :], rw2_sb[:, :], start=False, stop=g == Q - 1,
                              skip_group_check=True).then_inc(lg_done, 1)

                if a is not None:
                    t1(0)
                if b is not None:
                    t2(0)
                    pe.matmul(lg_ps, ones[0:1, 0:P], rb2_sb[0:1, :].unsqueeze(1).to_broadcast([1, Q, EP]), start=True, stop=False,
                              skip_group_check=True)
                for g in range(Q):
                    if a is not None:
                        if g + 1 < Q:
                            t1(g + 1)
                        mix(g)
                    if b is not None:
                        for q in B_TILES[g]:
                            if q + 1 < Q:
                                t2(q + 1)
                            hidden(q)
                            if q > 0:
                                logits(q - 1)
                        if g == 2:
                            logits(Q - 1)
                if b is not None:
                    pe.wait_ge(oh_ready, b + 1)
                    pe.matmul(rk_ps, tri[:, :], oh[:, :, :, :], start=True, stop=False, skip_group_check=True)
                    pe.matmul(rk_ps, ones[:, :], base[:, :, :].unsqueeze(1).to_broadcast([P, Q, 2, EP]), start=False, stop=False,
                              skip_group_check=True)
                    for g in range(Q - 1):
                        last = pe.matmul(rk_ps[:, g + 1:Q, :, :], ones[:, :],
                                         oh[:, g, :, :].unsqueeze(1).to_broadcast([P, Q - 1 - g, 2, EP]),
                                         start=False, stop=g == Q - 2, skip_group_check=True)
                    last.then_inc(rk_done, 1)

            groups(pe, step)
            pe.wait_ge(step_done, GROUPS * R_STEPS)
            pe.matmul(d_ps[0:P, 0:2 * EP], ones[:, :], base[:, :, :].rearrange("p k e -> p (k e)"), start=True, stop=True).then_inc(cnt_done, 1)

            pe.wait_ge(split_l, E)
            pe.wait_ge(tab_done, 1)
            e_regs = [pe.alloc_register(f"pe_e{i}") for i in range(3)]
            for k in range(2):
                nt, nx, nh = k * (NT * 3 + 2), k * (NT + LEAD), k * NT * 2
                if k == 1:
                    pe.wait_ge(el_done, nt)
                for j in range(2):
                    pe.wait_ge(xe_done, nx + j + 1)
                    transpose(t_ps[j], xe[:, j, :], S).then_inc(et_done, 1)
                with pe.Fori(0, NT // U) as it:
                    x_n, h_n, m = 2, 0, 0
                    for group in range(U // 3):
                        es = experts(pe, e_regs, k, it * (U // 3) + group)
                        for kind, layer, lane in ORDER:
                            if kind == "transpose":
                                if layer == 0:
                                    x_n += 1
                                    pe.wait_ge(xe_done, it * U + (nx + x_n))
                                    rows = xe[:, lane, :]
                                else:
                                    h_n += 1
                                    pe.wait_ge(hs_done, it * (2 * U) + (nh + h_n))
                                    rows = hs[:, lane, :]
                                transpose(t_ps[lane], rows, S).then_inc(et_done, 1)
                                continue
                            m += 1
                            e = es[lane]
                            ready = it * (3 * U) + (nt + m)
                            pe.wait_ge(eh_done, ready)
                            at = e * EW + (layer - 1) * LW
                            add = (sel_hl[:, :], b3_hl[:, bass.ds(e * D, D)]) if layer == 3 else None
                            product(l_ps[lane][:, 0:F], lane,
                                    lambda c, at=at: we_h[:, bass.ds(at + c * F, F)],
                                    lambda c, at=at: we_l[:, bass.ds(at + c * F, F)],
                                    el_done, ready, add).then_inc(l_done, 1)


def kernel(**inputs):
    import numpy as np
    import concourse.bacc as bacc
    from concourse.bass_utils import run_bass_kernel_spmd as run

    wqkv = np.asarray(inputs["L0_mix_w_qkv"])
    given = {
        "x": inputs["x"], "src": inputs["src"], "dst": inputs["dst"],
        "w_kv": wqkv[MI:].T, "w_q": wqkv[:MI], "w_oT": np.asarray(inputs["L0_mix_w_out"]).T,
        "b_out": inputs["L0_mix_b_out"], "w_g": inputs["L0_gnn_weight"],
        "a_l": inputs["L0_gnn_attn_l"], "a_r": inputs["L0_gnn_attn_r"],
        "rw1": inputs["L0_ffn_router_w1"], "rb1": inputs["L0_ffn_router_b1"],
        "rw2": inputs["L0_ffn_router_w2"], "rb2": inputs["L0_ffn_router_b2"],
        "ew1": inputs["L0_ffn_expert_w1"], "eb1": inputs["L0_ffn_expert_b1"],
        "ew2": inputs["L0_ffn_expert_w2"], "eb2": inputs["L0_ffn_expert_b2"],
        "ew3": inputs["L0_ffn_expert_w3"], "eb3": inputs["L0_ffn_expert_b3"],
    }
    nc = bacc.Bacc("TRN2", target_bir_lowering=False, num_devices=1)
    arrays, aps = {}, []
    for name, a in given.items():
        a = np.ascontiguousarray(a)
        arrays[f"in_{name}"] = a
        aps.append(nc.dram_tensor(f"in_{name}", a.shape, mybir.dt.from_np(a.dtype), kind="ExternalInput").ap())
    out = nc.dram_tensor("out_x", (N, D), FP32, kind="ExternalOutput").ap()
    gps_layer(nc, *aps, out)
    r = run(nc, [arrays], core_ids=[0])
    return r.results[0]["out_x"]
```

```python
import concourse.bass as bass
from concourse import mybir
from contextlib import ExitStack

FP32 = mybir.dt.float32
FP32R = mybir.dt.float32r
I32 = mybir.dt.int32
ALU = mybir.AluOpType
ACT = mybir.ActivationFunctionType
AX = mybir.AxisListType

N, D = 6250, 256
GH, GC = 4, 64
MH, MC = 8, 64
MI = MH * MC
E, F, RH = 6, 256, 128
EPS = 1e-5

P = 125
T = N // P
G = 10
ITERS = T // G
KC = D // 128
AHEAD = 7
HALF = G // 2
Q = 10
GROUPS = T // Q
H = Q // 2
IN_G = 16 * 2 * H
XTW = D + GH
GW = D + 2 * GH

S = 128
REG = N + S
EP = 8
NT = (N + E * (S - 1)) // S
LEAD = 3
U = 9
ROW = D + 6
C_NMR, C_R, C_W, C_TOK, C_POS = D, D + 1, D + 2, D + 4, D + 5
ROW1 = D + ROW
SKIP = 1 << 20
LW = KC * F
EW = 3 * LW

ORDER = [("product", 1, 0), ("transpose", 0, 2), ("product", 1, 1), ("transpose", 1, 0),
         ("product", 1, 2), ("transpose", 1, 1), ("product", 2, 0), ("transpose", 1, 2),
         ("product", 2, 1), ("transpose", 2, 0), ("product", 2, 2), ("transpose", 2, 1),
         ("product", 3, 0), ("transpose", 2, 2), ("product", 3, 1), ("transpose", 0, 0),
         ("product", 3, 2), ("transpose", 0, 1)]

NORMAL_AFTER = [(1, 0), (1, 2), (2, 1)]
WEIGHT_AFTER = [(2, 2), (0, 0), (0, 1)]

B_TILES = [(0, 1)] + [(g + 1,) for g in range(1, Q - 1)] + [()]
AL_STEPS, R_STEPS = 6, 20

PREP_EPS, PREP_W, PREP_2 = 1, 12, 23


def gps_layer(nc, x, src, dst, w_kv, w_q, w_oT, b_out, w_g, a_l, a_r, rw1, rb1, rw2, rb2,
              ew1, eb1, ew2, eb2, ew3, eb3, out):
    ctx = ExitStack()
    with ctx:
        def sb(name, shape, dt=FP32):
            return ctx.enter_context(nc.sbuf_tensor(name, shape, dt))

        def sem(name):
            return ctx.enter_context(nc.semaphore(name))

        xt_tab = nc.dram_tensor("xt_tab", (N, XTW), FP32, kind="Internal").ap()
        al_tab = nc.dram_tensor("al_tab", (N, GH), FP32, kind="Internal").ap()
        tab0 = nc.dram_tensor("tab0", (E * REG + S, ROW), FP32, kind="Internal").ap()
        tab1 = nc.dram_tensor("tab1", (E * REG + S, ROW1), FP32, kind="Internal").ap()

        ident = sb("ident", [128, 128])
        tri = sb("tri", [P, P], FP32R)
        ones = sb("ones", [P, P], FP32R)
        ebase = sb("ebase", [P, 2, EP])
        desc = sb("desc", [P, EP])
        tok_all = sb("tok_all", [P, T], I32)
        wkv_h, wkv_l = sb("wkv_h", [128, KC, 2 * MI], FP32R), sb("wkv_l", [128, KC, 2 * MI], FP32R)
        wg_h, wg_l = sb("wg_h", [128, KC, GW], FP32R), sb("wg_l", [128, KC, GW], FP32R)
        wq_sb = sb("wq_sb", [128, MI // 128, D])
        woT_sb = sb("woT_sb", [128, MI // 128, D])
        mix_w = sb("mix_w", [128, KC, D])
        rw1_sb = sb("rw1_sb", [128, KC, RH])
        rb1_sb = sb("rb1_sb", [RH, 1])
        rw2_sb = sb("rw2_sb", [RH, EP])
        rb2_sb = sb("rb2_sb", [P, EP])
        we_h, we_l = sb("we_h", [128, E * EW], FP32R), sb("we_l", [128, E * EW], FP32R)
        be_sb = sb("be_sb", [128, E * 3 * F])
        bo_hl = sb("bo_hl", [128, D], FP32R)
        sel_hl = sb("sel_hl", [128, S], FP32R)
        src_all, dst_all = sb("src_all", [P, T], I32), sb("dst_all", [P, T], I32)
        weight_in = sb("weight_in", [128, Q * ROW])
        raw_e = weight_in[:, 0:EW]
        bo_sb = weight_in[0:33, EW:EW + D]
        skip_rows = sb("skip_rows", [S, ROW1])
        eps_sb = sb("eps_sb", [128, 1])

        arena = sb("arena", [128, U * ROW1])
        xring = sb("xring", [P, G, D])
        xn = sb("xn", [P, 2, D])
        x_h, x_l = sb("x_h", [128, 3, KC, 128], FP32R), sb("x_l", [128, 3, KC, 128], FP32R)
        st = sb("st", [P, G, 6])
        mv = sb("mv", [P, G, 2])
        sd = sb("sd", [P, G])
        rs = sb("rs", [P, G])
        nmr = sb("nmr", [P, G])
        rs_all, nmr_all = sb("rs_all", [P, T + G]), sb("nmr_all", [P, T + G])
        work = sb("work", [128, 6 * MI])

        kv_raw = arena[:, 0:KC * 2 * MI].rearrange("p (c n) -> p c n", c=KC)
        g_at = KC * 2 * MI
        wg_raw = arena[:, g_at:g_at + KC * GW].rearrange("p (c n) -> p c n", c=KC)
        att_bc = arena[:, g_at + KC * GW:g_at + KC * GW + 2 * D].rearrange("p (s n) -> p s n", s=2)
        att_pr = work[:, 0:KC * D].rearrange("p (c n) -> p c n", c=KC)
        kv_mean = work[:, 2 * MI:2 * MI + KC * 2 * MH].rearrange("p (c h) -> p c h", c=KC)
        xts = arena[0:P, 0:G * GW].rearrange("p (g n) -> p g n", g=G)
        sq = work[0:P, 0:2 * MI]
        ks = work[0:P, 2 * MI:4 * MI].rearrange("p (b n) -> p b n", b=2)
        vs = work[0:P, 4 * MI:6 * MI].rearrange("p (b n) -> p b n", b=2)
        ss = sb("ss", [P, 2 * MH])
        sse = sb("sse", [P, 2 * MH])
        pr = sb("pr", [P, MH])
        sr = sb("sr", [P, MH])
        rkv = sb("rkv", [P, MH])

        dotsT = sb("dotsT", [128, MI // 128, 128])
        a_sb = work[:, 0:(MI // 128) * D].rearrange("p (b n) -> p b n", b=MI // 128)

        xtg = arena[0:P, 0:2 * H * XTW].rearrange("p (b g n) -> p b g n", b=2, g=H)
        gp = arena[0:P, 2 * H * XTW:2 * H * XTW + 2 * D].rearrange("p (b n) -> p b n", b=2)
        gt = arena[0:P, 2 * H * XTW + 2 * D:2 * H * XTW + 2 * D + 2 * GC].rearrange("p (b n) -> p b n", b=2)
        y2 = arena[0:P, 2 * H * XTW + 3 * D:2 * H * XTW + 5 * D].rearrange("p (b n) -> p b n", b=2)
        xr = [rows[0:P, 0:Q * ROW].rearrange("p (g n) -> p g n", g=Q) for rows in (work, weight_in)]
        xT = sb("xT", [128, 2, KC, 128])
        rhT = sb("rhT", [RH, 2, P])
        alg = sb("alg", [P, 2, H, GH])
        al = sb("al", [P, 4, H, GH])
        am = sb("am", [P, 3, H])
        idx_s, idx_d = sb("idx_s", [P, 2, H], I32), sb("idx_d", [P, 2, H], I32)
        lg = sb("lg", [P, 4, Q, EP])
        oh = sb("oh", [P, Q, 2, EP], FP32R)
        rk = sb("rk", [P, Q, 2, EP])
        tw = sb("tw", [P, 8, Q])
        posf = sb("posf", [P, Q, 2])
        pos0 = sb("pos0", [P, 2, Q], I32)
        base = sb("base", [P, 2, EP])
        bsum = sb("bsum", [P, 2, EP])

        NTT = NT + LEAD
        NM = -(-N // S)
        cnt = sb("cnt", [1, 2, EP])
        nmul = sb("nmul", [1, NM])
        ntl = sb("ntl", [1, 2, EP])
        free = xring[:, :, :].rearrange("p g n -> p (g n)")
        ge_at = 2 * EP * NM
        gn_at = ge_at + 2 * NTT * E
        ncmp = free[0:1, 0:ge_at].rearrange("p (k e m) -> p k e m", k=2, e=EP)
        ends = sb("ends", [1, 2, EP])
        jj = sb("jj", [1, NTT])
        ge = free[0:1, ge_at:gn_at].rearrange("p (k j e) -> p k j e", k=2, j=NTT)
        gn = free[0:1, gn_at:gn_at + 2 * NTT * E].rearrange("p (k j e) -> p k j e", k=2, j=NTT)
        tf = sb("tf", [1, 8, 2, NTT])
        tab_row = sb("tab_row", [1, 2, NTT], I32)
        tab_e = sb("tab_e", [1, 2, NTT // 3, 4], I32)
        fill = sb("fill", [1, 2, EP], I32)

        rb = arena[:, :].rearrange("p (u n) -> p u n", u=U)
        xe = sb("xe", [S, 3, D])
        hs = sb("hs", [S, 3, D])

        xnr = xe[0:P, :, :]
        xTr = hs[:, :, :].rearrange("p b (c n) -> p b c n", c=KC)

        kv_ps = [ctx.enter_context(nc.psum_tensor(f"kv_ps{b}", [128, 2 * MI], FP32)) for b in range(2)]
        pt = [ctx.enter_context(nc.psum_tensor(f"pt{b}", [128, 512], FP32)) for b in range(2)]
        xt_ps = ctx.enter_context(nc.psum_tensor("xt_ps", [128, 512], FP32))
        d_ps = ctx.enter_context(nc.psum_tensor("d_ps", [128, 512], FP32))

        def half_t(bank):
            return bank[:, 0:KC * 128].rearrange("p (c n) -> p c n", c=KC)

        ma_ps = [kv_ps[0][:, 0:512], kv_ps[0][:, 512:1024]]
        rh_ps = [kv_ps[1][:, 0:512], kv_ps[1][:, 512:1024]]
        lg_ps = xt_ps[0:P, 0:Q * EP].rearrange("p (g e) -> p g e", g=Q)
        rk_ps = d_ps[0:P, 0:Q * 2 * EP].rearrange("p (g k e) -> p g k e", g=Q, k=2)
        t_ps = [pt[0], pt[1], xt_ps]
        l_ps = [kv_ps[0][:, 0:512], kv_ps[0][:, 512:1024], kv_ps[1][:, 0:512]]

        x_in = [sem(f"x_in{g}") for g in range(G)]
        w1_in, w2_in, raw_in = sem("w1_in"), sem("w2_in"), sem("raw_in")
        pool_c, prep, x_zero = sem("pool_c"), sem("prep"), sem("x_zero")
        centred, kvh_done = sem("centred"), sem("kvh_done")
        split_h, split_l = sem("split_h"), sem("split_l")
        bs_done, ag_done, sd_done, fin_done = sem("bs_done"), sem("ag_done"), sem("sd_done"), sem("fin_done")
        xn_ready, pt_ready, xh_ready, xl_ready = sem("xn_ready"), sem("pt_ready"), sem("xh_ready"), sem("xl_ready")
        k_ready, v_ready, xt_ready = sem("k_ready"), sem("v_ready"), sem("xt_ready")
        sqk_done, sqv_done, red_done, sse_done = sem("sqk_done"), sem("sqv_done"), sem("red_done"), sem("sse_done")
        pr_done, sr_done, rc_done = sem("pr_done"), sem("sr_done"), sem("rc_done")
        ks_ready, xts_done, dots_done = sem("ks_ready"), sem("xts_done"), sem("dots_done")
        xt_out = [sem(f"xt_out{h}") for h in range(2)]
        dT_done, a_done, as_done, m_done, mw_done = (sem("dT_done"), sem("a_done"), sem("as_done"),
                                                     sem("m_done"), sem("mw_done"))
        idx_done = sem("idx_done")
        g_in = [sem(f"g_in{b}") for b in range(2)]
        al_step, al_ready, ex_done = sem("al_step"), sem("al_ready"), sem("ex_done")
        xn1_done, t1_done, xT1_done, ma_done = sem("xn1_done"), sem("t1_done"), sem("xT1_done"), sem("ma_done")
        gp_done, gt_done, y2_done, x2_done = sem("gp_done"), sem("gt_done"), sem("y2_done"), sem("x2_done")
        bs2_done, ag2_done, sd2_done, fin2_done = sem("bs2_done"), sem("ag2_done"), sem("sd2_done"), sem("fin2_done")
        xn2_done, t2_done, xT2_done = sem("xn2_done"), sem("t2_done"), sem("xT2_done")
        rh_done, rhT_done, lg_done = sem("rh_done"), sem("rhT_done"), sem("lg_done")
        step_done, lgx_ready, ex2_done, d_ready, ex3_done = (sem("step_done"), sem("lgx_ready"), sem("ex2_done"),
                                                        sem("d_ready"), sem("ex3_done"))
        oh_ready, rk_done, row_ready = sem("oh_ready"), sem("rk_done"), sem("row_ready")
        sc_out = [sem(f"sc_out{g}") for g in range(Q)]
        cnt_done, tstep, tab_done, fill_out = sem("cnt_done"), sem("tstep"), sem("tab_done"), [sem(f"fill_out{k}") for k in range(2)]
        fill_ready = sem("fill_ready")
        r_in = [sem(f"r_in{u}") for u in range(U)]
        xe_done, et_done, eh_done, el_done = sem("xe_done"), sem("et_done"), sem("eh_done"), sem("el_done")
        l_done, hs_done = sem("l_done"), sem("hs_done")
        o_done, w_done, z_done = sem("o_done"), sem("w_done"), sem("z_done")
        z_out = [sem(f"z_out{u}") for u in range(U)]

        x_t = x.rearrange("(p t) n -> p t n", t=T)
        xt_t = xt_tab.rearrange("(p t) n -> p t n", t=T)
        al_t = al_tab.rearrange("(p t) n -> p t n", t=T)
        W1, W2, RAW = 16 * 4, 16 * 12, 16 * 3

        def groups(engine, step):
            step(0, None, 0)
            with engine.Fori(0, GROUPS // 2) as it:
                step(it * 2 + 1, it * 2, 1)
                step(it * 2 + 2, it * 2 + 1, 0)
            step(None, GROUPS - 1, 1)

        def first(n, count=1):
            return isinstance(n, int) and n < count

        def experts(engine, regs, k, at):
            engine.load(regs, tab_e[0:1, k, bass.ds(at, 1), 0:3].rearrange("p a l -> p (a l)"))
            return [engine.snap(reg, min_val=0, max_val=E - 1) for reg in regs]

        def output(k, u):
            return rb[:, u, 0:D] if k == 0 else rb[:, u, D:2 * D]

        block = ctx.enter_context(nc.Block())

        @block.sync
        def _(sp):
            def chunks(w):
                return w.rearrange("(c p) n -> p c n", p=128)

            ev = [w.rearrange("e (c p) n -> e p c n", p=128) for w in (ew1, ew2, ew3)]

            def expert(at):
                for layer in range(3):
                    wide = weight_in[:, layer * LW:(layer + 1) * LW].rearrange("p (c n) -> p c n", c=KC)
                    sp.dma_start(wide, ev[layer][at, :, :, :].rearrange("a p c n -> (a p) c n")).then_inc(raw_in, 16)

            for g in range(G):
                if g == 2:
                    sp.dma_start(kv_raw, chunks(w_kv)).then_inc(w1_in, 16)
                    sp.dma_start(wg_raw[:, :, 0:D], chunks(w_g)).then_inc(w1_in, 16)
                    for s, a in enumerate((a_r, a_l)):
                        sp.dma_start(att_bc[:, s, :], a.rearrange("h c -> (h c)").partition_broadcast(128)).then_inc(w1_in, 16)
                sp.dma_start(xring[:, g, :], x_t[:, g, :]).then_inc(x_in[g], 16)
            expert(slice(0, 1))
            sp.dma_start(src_all[:, :], src[0:N].rearrange("(p t) -> p t", t=T)).then_inc(w2_in, 16)
            sp.dma_start(dst_all[:, :], dst[0:N].rearrange("(p t) -> p t", t=T)).then_inc(w2_in, 16)
            sp.dma_start(wq_sb[:, :, :], chunks(w_q)).then_inc(w2_in, 16)
            sp.dma_start(woT_sb[:, :, :], chunks(w_oT)).then_inc(w2_in, 16)
            sp.dma_start(bo_sb, b_out.partition_broadcast(33)).then_inc(w2_in, 16)
            sp.dma_start(rw1_sb[:, :, :], chunks(rw1)).then_inc(w2_in, 16)
            sp.dma_start(rb1_sb[:, :], rb1.rearrange("(p a) -> p a", a=1)).then_inc(w2_in, 16)
            sp.dma_start(rw2_sb[:, 0:E], rw2).then_inc(w2_in, 16)
            sp.dma_start(rb2_sb[:, 0:E], rb2.partition_broadcast(P)).then_inc(w2_in, 16)
            be_v = be_sb[:, :].rearrange("p (e l n) -> p e l n", e=E, l=3)
            for layer, b in enumerate((eb1, eb2, eb3)):
                sp.dma_start(be_v[:, :, layer, :], b.partition_broadcast(128)).then_inc(w2_in, 16)

            def reload(it, at, expert_at):
                for g in range(G):
                    sp.wait_ge(xn_ready, it * G + (g + 1))
                    sp.dma_start(xring[:, g, :], x_t[:, at(g), :].rearrange("p a n -> p (a n)")).then_inc(x_in[g], 16)
                    if g == 3:
                        sp.wait_ge(split_l, it + 1)
                        expert(expert_at)
                    if g == 6:
                        store(it, 0)
                store(it, 1)

            def store(it, h):
                lo = HALF * h
                sp.wait_ge(xts_done, it * G + (1 + lo + HALF))
                sp.dma_start(xt_t[:, bass.ds(it * G + lo, HALF), :], xts[:, lo:lo + HALF, 0:XTW]).then_inc(xt_out[h], 16)
                sp.dma_start(al_t[:, bass.ds(it * G + lo, HALF), :], xts[:, lo:lo + HALF, XTW:GW]).then_inc(xt_out[h], 16)

            with sp.Fori(0, ITERS - 1) as it:
                reload(it, lambda g: bass.ds(it * G + (G + g), 1), bass.ds(it + 1, 1))
            reload(ITERS - 1, lambda g: slice(g, g + 1), slice(E - 1, E))

            def again(it, j, at):
                sp.wait_ge(xn1_done, it * G + (j + 1))
                sp.wait_ge(y2_done, it * G + (j + 1))
                sp.dma_start(xring[:, j, :], x_t[:, at, :].rearrange("p a n -> p (a n)")).then_inc(x_in[j], 16)

            with sp.Fori(0, GROUPS - 1) as it:
                for j in range(G):
                    again(it, j, bass.ds(it * G + (G + j), 1))
            for j in range(2):
                again(GROUPS - 1, j, slice(j, j + 1))

            sp.wait_ge(fill_ready, 1)
            end_regs = [sp.alloc_register(f"end{e}") for e in range(E)]

            def fill_up(k):
                tab = (tab0, tab1)[k]
                rows = skip_rows[:, ROW1 - tab.shape[1]:ROW1]
                if k == 1:
                    sp.dma_start(tab[E * REG:E * REG + S, :], rows).then_inc(fill_out[k], 16)
                sp.load(end_regs, fill[0:1, k, 0:E])
                for reg in end_regs:
                    end = sp.snap(reg, min_val=0, max_val=(E - 1) * REG + N)
                    sp.dma_start(tab[bass.ds(end, S), :], rows).then_inc(fill_out[k], 16)

            fill_up(0)
            sp.wait_ge(tab_done, 1)
            sp.wait_ge(fill_out[0], 16 * E)
            for g in range(Q):
                sp.wait_ge(sc_out[g], 16 * (GROUPS + 1))

            def load(k, u, at, turn=None):
                tab = (tab0, tab1)[k]
                first = sp.value_load(tab_row[0:1, k, at], min_val=0, max_val=E * REG)
                if turn is not None:
                    sp.wait_ge(z_out[u], turn * 16 + 16 * (k * (NT // U) + 1))
                sp.dma_start(rb[:, u, ROW1 - tab.shape[1]:ROW1], tab[bass.ds(first, S), :]).then_inc(r_in[u], 16)

            for k in range(2):
                if k == 1:
                    sp.wait_ge(tab_done, 2)
                    for u in range(U):
                        sp.wait_ge(z_out[u], 16 * (NT // U))
                    sp.wait_ge(xe_done, NT + LEAD)
                    sp.wait_ge(fill_out[1], 16 * (E + 1))
                for u in range(U):
                    load(k, u, slice(u, u + 1))
                if k == 0:
                    fill_up(1)
                with sp.Fori(0, NT // U - 1) as it:
                    for u in range(U):
                        load(k, u, bass.ds(it * U + (U + u), 1), it)
                for u in range(LEAD):
                    load(k, u, slice(NT + u, NT + u + 1), NT // U - 1)
            for u in range(U):
                sp.wait_ge(z_out[u], 16 * 2 * (NT // U))

        @block.gpsimd
        def _(pool):
            for buf in (x_h, x_l):
                pool.memset(buf[:, :, :, :].bitcast(FP32), 0.0).then_inc(x_zero, 1)
            pool.memset(ident[:, :], 0.0).then_inc(pool_c, 1)
            pool.memset(tri[:, :].bitcast(FP32), 0.0).then_inc(pool_c, 1)
            pool.memset(ones[:, :].bitcast(FP32), 1.0).then_inc(pool_c, 1)
            pool.wait_ge(pool_c, 3)
            pool.affine_select(out=ident[:, :], in_=ident[:, :], compare_op=ALU.not_equal, fill=1.0, base=0,
                               pattern=[[-1, 128]], channel_multiplier=1).then_inc(pool_c, 1)
            pool.affine_select(out=tri[:, :], in_=tri[:, :].bitcast(FP32), compare_op=ALU.is_ge, fill=1.0, base=0,
                               pattern=[[-1, P]], channel_multiplier=1).then_inc(pool_c, 1)
            pool.iota(ebase[:, :, :], pattern=[[0, 2], [REG, EP]], base=0, channel_multiplier=0,
                      allow_small_or_imprecise_dtypes=True).then_inc(pool_c, 1)
            pool.iota(desc[:, :], pattern=[[-1, EP]], base=EP, channel_multiplier=0,
                      allow_small_or_imprecise_dtypes=True).then_inc(pool_c, 1)
            pool.iota(tok_all[:, :], pattern=[[1, T]], base=0, channel_multiplier=T).then_inc(pool_c, 1)
            pool.iota(nmul[:, :], pattern=[[S, NM]], base=0, channel_multiplier=0,
                      allow_small_or_imprecise_dtypes=True).then_inc(pool_c, 1)
            pool.iota(jj[:, :], pattern=[[1, NTT]], base=0, channel_multiplier=0,
                      allow_small_or_imprecise_dtypes=True).then_inc(pool_c, 1)
            pool.memset(skip_rows[:, 0:D + C_TOK], 0.0).then_inc(pool_c, 1)
            pool.iota(skip_rows[:, D + C_TOK:ROW1].bitcast(I32), pattern=[[0, 2]], base=SKIP,
                      channel_multiplier=0).then_inc(pool_c, 1)
            part = -(-S // Q)
            pool.wait_ge(pool_c, 12)
            for g in range(Q):
                lo, hi = g * part, min(g * part + part, S)
                pool.dma_start(tab0[E * REG + lo:E * REG + hi, :], skip_rows[lo:hi, D:ROW1]).then_inc(sc_out[g], 16)

            def wait_alone(semaphore, value):
                value = pool.to_reg(value)
                pool.wait_ge(pool_c, 1)
                pool.wait_ge(semaphore, value)

            with pool.Fori(0, E) as e:
                wait_alone(raw_in, e * RAW + RAW)
                pool.tensor_copy(we_h[:, bass.ds(e * EW, EW)], raw_e).then_inc(split_h, 1)
                wait_alone(split_h, e + 1)
                pool.tensor_tensor(we_l[:, bass.ds(e * EW, EW)], raw_e,
                                   we_h[:, bass.ds(e * EW, EW)].bitcast(FP32), ALU.subtract).then_inc(split_l, 1)

            def gathers(n, b, at, turn):
                if turn is not None:
                    pool.wait_ge(g_in[b], turn * IN_G + IN_G)
                pool.tensor_copy(idx_s[:, b, :], src_all[:, at]).then_inc(idx_done, 1)
                pool.tensor_copy(idx_d[:, b, :], dst_all[:, at]).then_inc(idx_done, 1)
                wait_alone(idx_done, n * 2 + 2)
                if turn is not None:
                    wait_alone(gp_done, n * H - H)
                for g in range(H):
                    pool.indirect_dma_start(out=alg[:, b, g, :], out_offset=None, in_=al_tab,
                                            in_offset=bass.IndirectOffsetOnAxis(ap=idx_s[:, b, g:g + 1], axis=0)
                                            ).then_inc(g_in[b], 16)
                    pool.indirect_dma_start(out=xtg[:, b, g, :], out_offset=None, in_=xt_tab,
                                            in_offset=bass.IndirectOffsetOnAxis(ap=idx_d[:, b, g:g + 1], axis=0)
                                            ).then_inc(g_in[b], 16)

            def scatters(n, b):
                wait_alone(row_ready, n + 1)
                for g in range(Q):
                    pool.indirect_dma_start(out=tab0, out_offset=bass.IndirectOffsetOnAxis(ap=pos0[:, b, g:g + 1], axis=0),
                                            in_=xr[b][:, g, :], in_offset=None).then_inc(sc_out[g], 16)

            for h in range(2):
                pool.wait_ge(xt_out[h], 16 + 32 * ITERS)
            pool.wait_ge(w2_in, W2)
            for b in range(2):
                gathers(b, b, slice(b * H, b * H + H), None)
            with pool.Fori(0, 2) as it:
                for b in range(2):
                    gathers(it * 2 + (2 + b), b, bass.ds(it * Q + (2 + b) * H, H), it)
            for n in range(GROUPS):
                scatters(n, n % 2)
                if n + 3 < GROUPS:
                    for b in range(2):
                        gathers(n * 2 + (6 + b), b, slice(n * Q + (6 + b) * H, n * Q + (7 + b) * H), n + 2)

            for k in range(2):
                with pool.Fori(0, NT // U) as it:
                    for u in range(U):
                        wait_alone(w_done, it * U + (k * NT + u + 1))
                        pool.tensor_tensor(rb[:, u, 0:D], rb[:, u, 0:D], rb[:, u, D:2 * D], ALU.add).then_inc(z_done, 1)
                        wait_alone(z_done, it * U + (k * NT + u + 1))
                        if k == 0:
                            pool.indirect_dma_start(
                                out=tab1, out_offset=bass.IndirectOffsetOnAxis(
                                    ap=rb[:, u, D + C_POS:D + C_POS + 1].bitcast(I32), axis=0),
                                in_=rb[:, u, :], in_offset=None, bounds_check=E * REG - 1, oob_is_err=False
                            ).then_inc(z_out[u], 16)
                        else:
                            pool.indirect_dma_start(
                                out=out, out_offset=bass.IndirectOffsetOnAxis(
                                    ap=rb[:, u, D + C_TOK:D + C_TOK + 1].bitcast(I32), axis=0),
                                in_=rb[:, u, 0:D], in_offset=None, bounds_check=N - 1, oob_is_err=False
                            ).then_inc(z_out[u], 16)

        @block.scalar
        def _(act):
            def stdev(h, value):
                lo = HALF * h
                act.wait_ge(ag_done, value)
                act.activation(sd[:, lo:lo + HALF], mv[:, lo:lo + HALF, 1], ACT.Sqrt, bias=eps_sb[0:P, 0:1]).then_inc(sd_done, 1)

            def upper(b):
                act.activation(x_h[:, b, :, 0:P], half_t(pt[b])[:, :, 0:P], ACT.Copy).then_inc(xh_ready, 1)

            act.sem_inc(xts_done, 1)
            for h in range(2):
                act.sem_inc(xt_out[h], 16)
            act.wait_ge(prep, PREP_EPS)
            stdev(0, AHEAD)
            act.wait_ge(x_zero, 2)
            act.wait_ge(pt_ready, 1)
            upper(0)
            for half in range(2):
                cols = slice(half * MI, half * MI + MI)
                act.wait_ge(centred, half + 1)
                act.activation(wkv_h[:, :, cols], kv_raw[:, :, cols], ACT.Copy).then_inc(kvh_done, 1)
            act.wait_ge(centred, 3)
            act.activation(wg_h[:, :, :], wg_raw, ACT.Copy).then_inc(kvh_done, 1)
            with act.Fori(0, ITERS) as it:
                for g in range(G):
                    b = g % 2
                    t = it * G + g
                    act.wait_ge(k_ready, t + 1)
                    act.activation(sq[:, 0:MI], kv_ps[b][0:P, 0:MI], ACT.Square).then_inc(sqk_done, 1)
                    act.wait_ge(pt_ready, t + 2)
                    upper(1 - b)
                    act.wait_ge(v_ready, t + 1)
                    act.activation(sq[:, MI:2 * MI], kv_ps[b][0:P, MI:2 * MI], ACT.Square).then_inc(sqv_done, 1)
                    act.activation(vs[:, b, :], kv_ps[b][0:P, MI:2 * MI], ACT.Copy)
                    if g % HALF == 0:
                        act.wait_ge(xt_out[g // HALF], it * 32 + 16)
                    act.wait_ge(xt_ready, t + 1)
                    act.activation(xts[:, g, :], xt_ps[0:P, 0:GW], ACT.Copy).then_inc(xts_done, 1)
                    act.wait_ge(pr_done, t + 1)
                    act.activation(sr[:, :], pr[:, :], ACT.Sqrt).then_inc(sr_done, 1)
                    if g in (2, 7):
                        stdev(1 if g == 2 else 0, it * G + (AHEAD + g + 1))

            act.wait_ge(a_done, 1)
            act.activation(a_sb, kv_ps[0][:, :].rearrange("p (b n) -> p b n", b=MI // 128), ACT.Copy,
                           scale=1.0 / N).then_inc(as_done, 1)
            act.wait_ge(m_done, 1)
            act.activation(mix_w[:, :, :], pt[0][:, :].rearrange("p (c n) -> p c n", c=KC), ACT.Copy).then_inc(mw_done, 1)

            def normal1(a, g):
                n, j = a * Q + g, g % Q
                act.wait_ge(x_in[j], a * 16 + 16 * (ITERS + 1 + g // Q))
                if not first(n, 2):
                    act.wait_ge(t1_done, n - 1)
                act.activation(xn[:, g % 2, :], xring[:, j, :], ACT.Identity, bias=nmr_all[:, bass.ds(n, 1)],
                               scale=rs_all[:, bass.ds(n, 1)]).then_inc(xn1_done, 1)

            def upper1(a, g):
                act.wait_ge(t1_done, a * Q + (g + 1))
                act.activation(xT[:, g % 2, :, 0:P], half_t(pt[0])[:, :, 0:P], ACT.Copy).then_inc(xT1_done, 1)

            act.wait_ge(xn_ready, T + 2)
            normal1(0, 0)
            normal1(0, 1)
            upper1(0, 0)

            def step(a, b, p):
                def softmax(h):
                    act.wait_ge(al_ready, a * 2 + (h + 1))
                    act.activation(al[:, 2, :, :], al[:, 1, :, :], ACT.Exp).then_inc(ex_done, 1)

                if b is not None:
                    act.wait_ge(ag2_done, b * Q + Q)
                    act.activation(sd[:, :], mv[:, :, 1], ACT.Sqrt, bias=eps_sb[0:P, 0:1]).then_inc(sd2_done, 1)
                if a is not None:
                    softmax(0)

                def normal2(g):
                    if g >= 2:
                        act.wait_ge(t2_done, b * Q + (g - 1))
                    act.activation(xnr[:, g % 2, :], xr[1 - p][:, g, 0:D], ACT.Identity,
                                   bias=xr[1 - p][:, g, C_NMR:C_NMR + 1],
                                   scale=xr[1 - p][:, g, C_R:C_R + 1]).then_inc(xn2_done, 1)

                def hidden(g):
                    act.wait_ge(rh_done, b * Q + (g + 1))
                    act.activation(rhT[:, g % 2, :], rh_ps[g % 2][:, 0:P], ACT.Relu, bias=rb1_sb[:, 0:1]).then_inc(rhT_done, 1)

                if b is not None:
                    act.wait_ge(fin2_done, b * 2 + 2)
                    normal2(0)
                for g in range(Q):
                    if a is not None:
                        upper1(a, g + 1)
                        normal1(a, g + 2)
                        if g == H - 1:
                            softmax(1)
                    if b is not None:
                        for q in B_TILES[g]:
                            if q + 1 < Q:
                                normal2(q + 1)
                            act.wait_ge(t2_done, b * Q + (q + 1))
                            act.activation(xTr[:, q % 2, :, 0:P], half_t(pt[1])[:, :, 0:P], ACT.Copy).then_inc(xT2_done, 1)
                            if q > 0:
                                hidden(q - 1)
                if b is not None:
                    hidden(Q - 1)
                    act.wait_ge(lgx_ready, b + 1)
                    act.activation(lg[:, 2, :, :], lg[:, 1, :, :], ACT.Exp).then_inc(ex2_done, 1)
                    act.wait_ge(d_ready, b + 1)
                    act.activation(tw[:, 5, :], tw[:, 4, :], ACT.Exp).then_inc(ex3_done, 1)

            groups(act, step)

            def normal(k, j, it):
                u, turn = j % U, j // U
                loads = NT // U + (1 if u < LEAD else 0)
                act.wait_ge(r_in[u], it * 16 + 16 * (k * loads + turn + 1))
                act.activation(xe[:, j % 3, :], rb[:, u, D:2 * D], ACT.Identity,
                               bias=rb[:, u, D + C_NMR:D + C_NMR + 1],
                               scale=rb[:, u, D + C_R:D + C_R + 1]).then_inc(xe_done, 1)

            def upper3(layer, lane, n):
                act.wait_ge(et_done, n)
                act.activation(x_h[:, lane, :, :], half_t(t_ps[lane]), ACT.Relu if layer else ACT.Copy).then_inc(eh_done, 1)

            for k in range(2):
                nt = k * (NT * 3 + 2)
                for j in range(LEAD):
                    normal(k, j, 0)
                for j in range(2):
                    upper3(0, j, nt + j + 1)
                with act.Fori(0, NT // U) as it:
                    n, j = 2, LEAD
                    for group in range(U // 3):
                        for kind, layer, lane in ORDER:
                            if kind == "product":
                                continue
                            n += 1
                            upper3(layer, lane, it * (3 * U) + (nt + n))
                            if (layer, lane) in NORMAL_AFTER:
                                normal(k, j, it)
                                j += 1
                            if (layer, lane) in WEIGHT_AFTER:
                                u = group * 3 + WEIGHT_AFTER.index((layer, lane))
                                act.wait_ge(o_done, it * U + (k * NT + u + 1))
                                act.activation(output(k, u), output(k, u), ACT.Copy,
                                               scale=rb[:, u, D + C_W + k:D + C_W + k + 1]).then_inc(w_done, 1)

        @block.vector
        def _(dve):
            done = [0]

            def link(ins):
                done[0] += 1
                ins.then_inc(prep, 1)
                dve.wait_ge(prep, done[0])

            def stats(j, value):
                dve.wait_ge(x_in[j], value)
                dve.bn_stats(st[:, j, :], xring[:, j, :]).then_inc(bs_done, 1)

            def wait_alone(semaphore, value):
                value = dve.to_reg(value)
                dve.wait_ge(prep, 1)
                dve.wait_ge(semaphore, value)

            def aggregate(j, value):
                wait_alone(bs_done, value)
                dve.bn_aggr(mv[:, j, :], st[:, j, :]).then_inc(ag_done, 1)

            def finish(h, n, at):
                lo = HALF * h
                part = slice(lo, lo + HALF)
                dve.wait_ge(sd_done, n + 1)
                dve.reciprocal(rs[:, part], sd[:, part]).then_inc(fin_done, 1)
                dve.wait_ge(fin_done, n * 4 + 1)
                dve.scalar_tensor_tensor(nmr[:, part], mv[:, part, 0], -1.0, rs[:, part], ALU.mult, ALU.mult).then_inc(fin_done, 1)
                dve.wait_ge(fin_done, n * 4 + 2)
                dve.tensor_copy(rs_all[:, at], rs[:, part]).then_inc(fin_done, 1)
                dve.tensor_copy(nmr_all[:, at], nmr[:, part]).then_inc(fin_done, 1)

            def normal(j, b):
                dve.tensor_scalar(xn[:, b, :], xring[:, j, :], rs[:, j:j + 1], nmr[:, j:j + 1],
                                  ALU.mult, ALU.add).then_inc(xn_ready, 1)

            def lower(b):
                dve.tensor_tensor(x_l[:, b, :, 0:P], half_t(pt[b])[:, :, 0:P], x_h[:, b, :, 0:P].bitcast(FP32),
                                  ALU.subtract).then_inc(xl_ready, 1)

            link(dve.memset(eps_sb[:, :], EPS))
            assert done[0] == PREP_EPS
            for j in range(AHEAD):
                stats(j, 16)
            for j in range(AHEAD):
                aggregate(j, j + 1)
            finish(0, 0, slice(0, HALF))
            for j in range(2):
                normal(j, j)

            dve.wait_ge(w1_in, W1)
            for half in range(2):
                cols = slice(half * MI, half * MI + MI)
                kv_v = kv_raw[:, :, cols].rearrange("p c (h n) -> p c h n", n=MC)
                mean_v = kv_mean[:, :, half * MH:half * MH + MH]
                link(dve.reduce_sum(mean_v, kv_v, axis=AX.X))
                link(dve.tensor_scalar(mean_v, mean_v, -1.0 / MC, None, ALU.mult))
                for c in range(KC):
                    last = dve.tensor_tensor(kv_v[:, c, :, :], kv_v[:, c, :, :], mean_v[:, c, :].unsqueeze(2).to_broadcast([128, MH, MC]), ALU.add)
                last.then_inc(centred, 1)
            dve.wait_ge(xh_ready, 1)
            lower(0)
            for s in range(2):
                link(dve.tensor_tensor(att_pr, wg_raw[:, :, 0:D], att_bc[:, s, :].unsqueeze(1).to_broadcast([128, KC, D]), ALU.mult))
                last = dve.reduce_sum(wg_raw[:, :, D + GH * s:D + GH * (s + 1)], att_pr.rearrange("p c (h n) -> p c h n", n=GC), axis=AX.X)
                if s == 0:
                    link(last)
                else:
                    last.then_inc(centred, 1)
            link(dve.memset(vs[:, 1, :], 0.0))
            dve.memset(ks[:, 1, :], 0.0).then_inc(ks_ready, 1)
            for half in range(2):
                cols = slice(half * MI, half * MI + MI)
                dve.wait_ge(kvh_done, half + 1)
                link(dve.tensor_tensor(wkv_l[:, :, cols], kv_raw[:, :, cols], wkv_h[:, :, cols].bitcast(FP32), ALU.subtract))
            dve.wait_ge(kvh_done, 3)
            link(dve.tensor_tensor(wg_l[:, :, :], wg_raw, wg_h[:, :, :].bitcast(FP32), ALU.subtract))
            assert done[0] == PREP_W, done[0]

            def prepare():
                dve.wait_ge(split_l, E)
                link(dve.memset(bo_hl[:, :].bitcast(FP32), 0.0))
                link(dve.memset(sel_hl[:, :].bitcast(FP32), 0.0))
                for q in (0, 32):
                    link(dve.memset(sel_hl[q:q + 1, :].bitcast(FP32), 1.0))
                dve.wait_ge(w2_in, W2)
                link(dve.tensor_copy(bo_hl[0:1, :], bo_sb[0:1, :]))
                link(dve.tensor_copy(bo_hl[32:33, :], bo_sb[32:33, :]))
                link(dve.tensor_tensor(bo_hl[32:33, :], bo_sb[32:33, :], bo_hl[32:33, :].bitcast(FP32), ALU.subtract))
                link(dve.memset(rw2_sb[:, E:EP], 0.0))
                link(dve.memset(rb2_sb[:, E:EP], -1e30))
                link(dve.memset(base[:, :, :], 0.0))
                dve.wait_ge(pool_c, 12)
                link(dve.tensor_copy(base[0:1, :, :], ebase[0:1, :, :]))
                assert done[0] == PREP_2, done[0]

            with dve.Fori(0, ITERS) as it:
                for g in range(G):
                    b = g % 2
                    t = it * G + g
                    j = (g + AHEAD) % G
                    stats(j, it * 16 + 16 * (1 + (g + AHEAD) // G))
                    dve.wait_ge(sqk_done, t + 1)
                    dve.reduce_sum(ss[:, 0:MH], sq[:, 0:MI].rearrange("p (h n) -> p h n", n=MC), axis=AX.X).then_inc(red_done, 1)
                    aggregate(j, t + (AHEAD + 1))
                    dve.wait_ge(xh_ready, t + 2)
                    lower(1 - b)
                    dve.wait_ge(sqv_done, t + 1)
                    dve.reduce_sum(ss[:, MH:2 * MH], sq[:, MI:2 * MI].rearrange("p (h n) -> p h n", n=MC), axis=AX.X).then_inc(red_done, 1)
                    dve.wait_ge(red_done, t * 2 + 2)
                    dve.tensor_scalar(sse[:, :], ss[:, :], 1.0 / MC, EPS, ALU.mult, ALU.add).then_inc(sse_done, 1)
                    dve.wait_ge(sse_done, t + 1)
                    dve.tensor_tensor(pr[:, :], sse[:, 0:MH], sse[:, MH:2 * MH], ALU.mult).then_inc(pr_done, 1)
                    if g in (3, 8):
                        h = 1 if g == 3 else 0
                        finish(h, it * 2 + (1 if g == 3 else 2), bass.ds(it * G + (HALF if g == 3 else G), HALF))
                        dve.wait_ge(fin_done, it * 8 + (8 if g == 3 else 12))
                    dve.wait_ge(pt_ready, t + 1)
                    normal((g + 2) % G, b)
                    dve.wait_ge(sr_done, t + 1)
                    dve.reciprocal(rkv[:, :], sr[:, :]).then_inc(rc_done, 1)
                    dve.wait_ge(rc_done, t + 1)
                    dve.tensor_tensor(ks[:, b, :].rearrange("p (h n) -> p h n", n=MC),
                                      kv_ps[b][0:P, 0:MI].rearrange("p (h n) -> p h n", n=MC),
                                      rkv[:, :].unsqueeze(2).to_broadcast([P, MH, MC]), ALU.mult).then_inc(ks_ready, 1)

            dve.memset(dotsT[:, :, :], 0.0).then_inc(dT_done, 1)
            dve.wait_ge(dT_done, 1)
            dve.wait_ge(dots_done, 1)
            d_v = d_ps[:, :].rearrange("p (b n) -> p b n", b=MI // 128)
            for q in range(2):
                dve.tensor_copy(dotsT[MC * q:MC * (q + 1), :, MC * q:MC * (q + 1)],
                                d_v[MC * q:MC * (q + 1), :, MC * q:MC * (q + 1)]).then_inc(dT_done, 1)
            prepare()

            def bc(ap, n):
                return ap.unsqueeze(len(ap.shape)).to_broadcast([*ap.shape, n])

            for h in range(2):
                dve.wait_ge(xt_out[h], 16 + 32 * ITERS)

            def step(a, b, p):
                if b is not None:
                    row = xr[1 - p]
                    dve.wait_ge(sd2_done, b + 1)
                    dve.reciprocal(row[:, :, C_R], sd[:, :]).then_inc(fin2_done, 1)
                    dve.wait_ge(fin2_done, b * 2 + 1)
                    dve.scalar_tensor_tensor(row[:, :, C_NMR], mv[:, :, 0], -1.0, row[:, :, C_R], ALU.mult, ALU.mult).then_inc(fin2_done, 1)
                if a is not None:
                    sums(a, p)
                if b is not None:
                    route(b, 1 - p)

            def sums(a, p):
                def weights(h):
                    n = [0]

                    def al_link(ins):
                        n[0] += 1
                        ins.then_inc(al_step, 1)
                        dve.wait_ge(al_step, a * (2 * AL_STEPS) + (h * AL_STEPS + n[0]))

                    dve.wait_ge(g_in[h], a * IN_G + IN_G)
                    al_link(dve.tensor_tensor(al[:, 0, :, :], alg[:, h, :, :], xtg[:, h, :, D:XTW], ALU.add))
                    al_link(dve.scalar_tensor_tensor(al[:, 1, :, :], al[:, 0, :, :], 0.01, al[:, 0, :, :], ALU.mult, ALU.max))
                    al_link(dve.reduce_max(am[:, 0, :], al[:, 1, :, :], axis=AX.X))
                    dve.tensor_tensor(al[:, 1, :, :], al[:, 1, :, :], bc(am[:, 0, :], GH), ALU.subtract).then_inc(al_ready, 1)
                    dve.wait_ge(ex_done, a * 2 + (h + 1))
                    al_link(dve.reduce_sum(am[:, 1, :], al[:, 2, :, :], axis=AX.X))
                    al_link(dve.reciprocal(am[:, 2, :], am[:, 1, :]))
                    al_link(dve.tensor_tensor(al[:, 3, :, :], al[:, 2, :, :], bc(am[:, 2, :], GH), ALU.mult))
                    assert n[0] == AL_STEPS

                def graph(g):
                    dve.tensor_tensor(gp[:, g % 2, :].rearrange("p (h n) -> p h n", n=GC),
                                      xtg[:, g // H, g % H, 0:D].rearrange("p (h n) -> p h n", n=GC),
                                      bc(al[:, 3, g % H, :], GC), ALU.mult).then_inc(gp_done, 1)

                def graph_sum(g):
                    dve.wait_ge(gp_done, a * Q + (g + 1))
                    dve.reduce_sum(gt[:, g % 2, :], gp[:, g % 2, :].rearrange("p (h n) -> p n h", n=GC), axis=AX.X).then_inc(gt_done, 1)

                def plus_graph(g):
                    dve.wait_ge(gt_done, a * Q + (g + 1))
                    dve.wait_ge(x_in[g], a * 16 + 16 * (ITERS + 1))
                    dve.tensor_tensor(y2[:, g % 2, :].rearrange("p (h n) -> p h n", n=GC),
                                      xring[:, g, :].rearrange("p (h n) -> p h n", n=GC),
                                      gt[:, g % 2, :].unsqueeze(1).to_broadcast([P, GH, GC]), ALU.add).then_inc(y2_done, 1)

                def plus_mix(g):
                    dve.wait_ge(y2_done, a * Q + (g + 1))
                    dve.wait_ge(ma_done, a * Q + (g + 1))
                    dve.tensor_tensor(xr[p][:, g, 0:D], ma_ps[g % 2][0:P, 0:D], y2[:, g % 2, :], ALU.add).then_inc(x2_done, 1)

                def stats2(g):
                    dve.wait_ge(x2_done, a * Q + (g + 1))
                    dve.bn_stats(st[:, g, :], xr[p][:, g, 0:D]).then_inc(bs2_done, 1)

                def aggregate2(g):
                    wait_alone(bs2_done, a * Q + (g + 1))
                    dve.bn_aggr(mv[:, g, :], st[:, g, :]).then_inc(ag2_done, 1)

                for g in range(Q + 1):
                    if g in (0, H):
                        weights(g // H)
                    if g < Q:
                        graph(g)
                    if g > 0:
                        if not first(a):
                            dve.wait_ge(sc_out[g - 1], a * 16)
                        plus_mix(g - 1)
                    if g < Q:
                        graph_sum(g)
                    if g > 0:
                        stats2(g - 1)
                    if g < Q:
                        plus_graph(g)
                    if g > 0:
                        aggregate2(g - 1)

            def route(b, p):
                row = xr[p]
                n = [0]

                def link(ins):
                    n[0] += 1
                    ins.then_inc(step_done, 1)
                    dve.wait_ge(step_done, b * R_STEPS + n[0])

                def probabilities():
                    dve.wait_ge(lg_done, b * Q + Q)
                    link(dve.reduce_max(tw[:, 0, :], lg_ps, axis=AX.X))
                    dve.tensor_tensor(lg[:, 1, :, :], lg_ps, bc(tw[:, 0, :], EP), ALU.subtract).then_inc(lgx_ready, 1)
                    dve.tensor_copy(row[:, :, C_TOK].bitcast(I32), tok_all[:, bass.ds(b * Q, Q)])
                    dve.wait_ge(ex2_done, b + 1)
                    link(dve.reduce_sum(tw[:, 1, :], lg[:, 2, :, :], axis=AX.X))
                    link(dve.reciprocal(tw[:, 1, :], tw[:, 1, :]))
                    link(dve.tensor_tensor(lg[:, 3, :, :], lg[:, 2, :, :], bc(tw[:, 1, :], EP), ALU.mult))

                def choose(k, prob):
                    link(dve.reduce_max(tw[:, 2 + k, :], prob, axis=AX.X))
                    link(dve.tensor_tensor(lg[:, 0, :, :], prob, bc(tw[:, 2 + k, :], EP), ALU.is_equal))
                    link(dve.tensor_tensor(lg[:, 1, :, :], lg[:, 0, :, :], desc[:, :].unsqueeze(1).to_broadcast([P, Q, EP]), ALU.mult))
                    link(dve.reduce_max(tw[:, 6, :], lg[:, 1, :, :], axis=AX.X))
                    return dve.tensor_tensor(oh[:, :, k, :], lg[:, 1, :, :], bc(tw[:, 6, :], EP), ALU.is_equal)

                def first_choice():
                    link(choose(0, lg[:, 3, :, :]))

                def second_choice():
                    link(dve.scalar_tensor_tensor(lg[:, 2, :, :], oh[:, :, 0, :].bitcast(FP32), -4.0, lg[:, 3, :, :], ALU.mult, ALU.add))
                    choose(1, lg[:, 2, :, :]).then_inc(oh_ready, 1)
                    dve.tensor_tensor(tw[:, 4, :], tw[:, 3, :], tw[:, 2, :], ALU.subtract).then_inc(d_ready, 1)

                def slots():
                    dve.wait_ge(ex3_done, b + 1)
                    link(dve.tensor_scalar(tw[:, 7, :], tw[:, 5, :], 1.0, None, ALU.add))
                    link(dve.reciprocal(row[:, :, C_W], tw[:, 7, :]))
                    dve.tensor_tensor(row[:, :, C_W + 1], tw[:, 5, :], row[:, :, C_W], ALU.mult)
                    link(dve.reduce_sum(bsum[:, :, :], oh[:, :, :, :].bitcast(FP32).rearrange("p g k e -> p k e g"), axis=AX.X))
                    dve.wait_ge(rk_done, b + 1)
                    link(dve.tensor_tensor(rk[:, :, :, :], rk_ps, oh[:, :, :, :].bitcast(FP32), ALU.mult))
                    link(dve.reduce_sum(posf[:, :, :], rk[:, :, :, :], axis=AX.X))
                    dve.tensor_copy(pos0[:, p, :], posf[:, :, 0])
                    dve.tensor_copy(row[:, :, C_POS].bitcast(I32), posf[:, :, 1]).then_inc(row_ready, 1)
                    link(dve.tensor_tensor(base[:, :, :], base[:, :, :], bsum[:, :, :], ALU.add))
                    assert n[0] == R_STEPS, n[0]

                probabilities()
                first_choice()
                second_choice()
                slots()

            groups(dve, step)

            tn = [0]

            def tlink(ins):
                tn[0] += 1
                ins.then_inc(tstep, 1)
                dve.wait_ge(tstep, tn[0])

            dve.wait_ge(cnt_done, 1)
            ends_ps = d_ps[0:1, 0:2 * EP].rearrange("p (k e) -> p k e", k=2)
            tlink(dve.tensor_tensor(cnt[:, :, :], ends_ps, ebase[0:1, :, :], ALU.subtract))
            dve.tensor_copy(fill[:, :, :], ends_ps).then_inc(fill_ready, 1)
            ce = cnt[:, :, :].rearrange("p k e -> p (k e)")
            nc_v = ncmp.rearrange("p k e m -> p (k e) m")
            tlink(dve.tensor_tensor(nc_v, bc(ce, NM), nmul[:, :].unsqueeze(1).to_broadcast([1, 2 * EP, NM]), ALU.is_gt))
            tlink(dve.reduce_sum(ntl[:, :, :].rearrange("p k e -> p (k e)"), nc_v, axis=AX.X))
            tlink(dve.tensor_copy(ends[:, :, 0:1], ntl[:, :, 0:1]))
            for e in range(1, E):
                tlink(dve.tensor_tensor(ends[:, :, e:e + 1], ends[:, :, e - 1:e], ntl[:, :, e:e + 1], ALU.add))
            for k in range(2):
                tlink(dve.tensor_tensor(ge[:, k, :, :], bc(jj[:, :], E), ends[:, k, 0:E].unsqueeze(1).to_broadcast([1, NTT, E]), ALU.is_ge))
                tlink(dve.reduce_sum(tf[:, 0, k, :], ge[:, k, :, :], axis=AX.X))
                tlink(dve.tensor_tensor(gn[:, k, :, :], ge[:, k, :, :], ntl[:, k, 0:E].unsqueeze(1).to_broadcast([1, NTT, E]), ALU.mult))
                tlink(dve.reduce_sum(tf[:, 1, k, :], gn[:, k, :, :], axis=AX.X))
                tlink(dve.tensor_tensor(tf[:, 2, k, :], jj[:, :], tf[:, 1, k, :], ALU.subtract))
                tlink(dve.tensor_scalar(tf[:, 3, k, :], ge[:, k, :, E - 1], -1.0, 1.0, ALU.mult, ALU.add))
                tlink(dve.tensor_tensor(tf[:, 4, k, :], tf[:, 2, k, :], tf[:, 3, k, :], ALU.mult))
                tlink(dve.tensor_scalar(tf[:, 5, k, :], tf[:, 4, k, :], float(S), None, ALU.mult))
                tlink(dve.scalar_tensor_tensor(tf[:, 6, k, :], tf[:, 0, k, :], float(REG), tf[:, 5, k, :], ALU.mult, ALU.add))
                tlink(dve.tensor_scalar(tf[:, 7, k, :], tf[:, 0, k, :], float(E - 1), None, ALU.min))
                tlink(dve.tensor_copy(tab_row[:, k, :], tf[:, 6, k, :]))
                dve.tensor_copy(tab_e[:, k, :, 0:3], tf[:, 7, k, :].rearrange("p (j l) -> p j l", l=3)).then_inc(tab_done, 1)

            dve.wait_ge(tab_done, 2)

            e_regs = [dve.alloc_register(f"dve_e{i}") for i in range(3)]

            def lower3(layer, lane, n):
                dve.wait_ge(eh_done, n)
                hi = x_h[:, lane, :, :].bitcast(FP32)
                if layer:
                    ins = dve.scalar_tensor_tensor(x_l[:, lane, :, :], half_t(t_ps[lane]), 0.0, hi, ALU.max, ALU.subtract)
                else:
                    ins = dve.tensor_tensor(x_l[:, lane, :, :], half_t(t_ps[lane]), hi, ALU.subtract)
                ins.then_inc(el_done, 1)

            for k in range(2):
                nt, nl = k * (NT * 3 + 2), k * NT * 3
                for j in range(2):
                    lower3(0, j, nt + j + 1)
                with dve.Fori(0, NT // U) as it:
                    n, m, j, i = 2, 0, 0, 0
                    for group in range(U // 3):
                        es = experts(dve, e_regs, k, it * (U // 3) + group)
                        for kind, layer, lane in ORDER:
                            if kind == "transpose":
                                n += 1
                                lower3(layer, lane, it * (3 * U) + (nt + n))
                                continue
                            m += 1
                            u = group * 3 + lane
                            dve.wait_ge(l_done, it * (3 * U) + (nl + m))
                            at = es[lane] * (3 * F) + (layer - 1) * F
                            rows = output(k, u) if layer == 3 else hs[:, lane, :]
                            dve.tensor_tensor(rows, l_ps[lane][:, 0:F], be_sb[:, bass.ds(at, F)],
                                              ALU.add).then_inc(o_done if layer == 3 else hs_done, 1)

        @block.tensor
        def _(pe):
            def transpose(bank, rows, p):
                for c in range(KC):
                    last = pe.transpose(half_t(bank)[:, c, 0:p], rows[:, c * 128:(c + 1) * 128], ident[0:p, 0:p])
                return last

            def product(outp, lane, w_h, w_l, xl, ready):
                for c in range(KC):
                    pe.matmul(outp, x_h[:, lane, c, :], w_h(c), start=c == 0, stop=False)
                    pe.matmul(outp, x_h[:, lane, c, :], w_l(c), start=False, stop=False)
                if ready is not None:
                    pe.wait_ge(xl, ready)
                for c in range(KC):
                    last = pe.matmul(outp, x_l[:, lane, c, :], w_h(c), start=False, stop=c == KC - 1)
                return last

            pe.wait_ge(pool_c, 5)
            pe.wait_ge(xn_ready, 1)
            transpose(pt[0], xn[:, 0, :], P).then_inc(pt_ready, 1)
            pe.wait_ge(ks_ready, 1)
            pe.wait_ge(prep, PREP_W)
            pe.matmul(d_ps[:, :], vs[:, 1, 0:128], ks[:, 1, :], start=True, stop=False, skip_group_check=True)

            def dots(b):
                for q in range(MI // 128):
                    at = slice(q * 128, (q + 1) * 128)
                    last = pe.matmul(d_ps[:, at], vs[:, b, at], ks[:, b, at], start=False, stop=False, skip_group_check=True)
                return last

            with pe.Fori(0, ITERS) as it:
                for g in range(G):
                    b = g % 2
                    t = it * G + g
                    pe.wait_ge(xh_ready, t + 1)
                    product(kv_ps[b][:, 0:MI], b, lambda c: wkv_h[:, c, 0:MI], lambda c: wkv_l[:, c, 0:MI],
                            xl_ready, t + 1).then_inc(k_ready, 1)
                    product(kv_ps[b][:, MI:2 * MI], b, lambda c: wkv_h[:, c, MI:2 * MI], lambda c: wkv_l[:, c, MI:2 * MI],
                            None, None).then_inc(v_ready, 1)
                    pe.wait_ge(xn_ready, t + 2)
                    transpose(pt[1 - b], xn[:, 1 - b, :], P).then_inc(pt_ready, 1)
                    pe.wait_ge(xts_done, t + 1)
                    product(xt_ps[:, 0:GW], b, lambda c: wg_h[:, c, :], lambda c: wg_l[:, c, :],
                            None, None).then_inc(xt_ready, 1)
                    pe.wait_ge(ks_ready, t + 1)
                    dots(1 - b)
            pe.wait_ge(ks_ready, T + 1)
            dots((T - 1) % 2).then_inc(dots_done, 1)

            pe.wait_ge(w2_in, W2)
            pe.wait_ge(dT_done, 3)
            for q in range(MI // 128):
                last = pe.matmul(kv_ps[0][:, q * D:(q + 1) * D], dotsT[:, q, :], woT_sb[:, q, :], start=True, stop=True)
            last.then_inc(a_done, 1)
            pe.wait_ge(as_done, 1)
            pe.wait_ge(xl_ready, T + 1)
            for c in range(KC):
                for q in range(MI // 128):
                    last = pe.matmul(pt[0][:, c * D:(c + 1) * D], wq_sb[:, q, c * 128:(c + 1) * 128], a_sb[:, q, :],
                                     start=q == 0, stop=q == MI // 128 - 1)
            last.then_inc(m_done, 1)
            pe.wait_ge(mw_done, 1)
            pe.wait_ge(prep, PREP_2)

            def t1(a, g):
                n = a * Q + g
                pe.wait_ge(xn1_done, n + 1)
                if not first(n):
                    pe.wait_ge(xT1_done, n)
                transpose(pt[0], xn[:, g % 2, :], P).then_inc(t1_done, 1)

            def mix(a, g):
                n, b = a * Q + g, g % 2
                out_ps = ma_ps[b][0:P, 0:D]
                pe.wait_ge(xT1_done, n + 1)
                if not first(n, 2):
                    pe.wait_ge(x2_done, n - 1)
                pe.matmul(out_ps, sel_hl[:, 0:P], bo_hl[:, :], start=True, stop=False)
                for c in range(KC):
                    last = pe.matmul(out_ps, xT[:, b, c, 0:P], mix_w[:, c, :], start=False, stop=c == KC - 1)
                last.then_inc(ma_done, 1)

            t1(0, 0)
            mix(0, 0)
            t1(0, 1)

            def step(a, b, p):
                def t2(g):
                    pe.wait_ge(xn2_done, b * Q + (g + 1))
                    if g > 0:
                        pe.wait_ge(xT2_done, b * Q + g)
                    transpose(pt[1], xnr[:, g % 2, :], P).then_inc(t2_done, 1)

                def hidden(g):
                    pe.wait_ge(xT2_done, b * Q + (g + 1))
                    for c in range(KC):
                        last = pe.matmul(rh_ps[g % 2][:, 0:P], rw1_sb[:, c, :], xTr[:, g % 2, c, 0:P], start=c == 0, stop=c == KC - 1)
                    last.then_inc(rh_done, 1)

                def logits(g):
                    pe.wait_ge(rhT_done, b * Q + (g + 1))
                    pe.matmul(lg_ps[:, g, :], rhT[:, g % 2, :], rw2_sb[:, :], start=False, stop=g == Q - 1,
                              skip_group_check=True).then_inc(lg_done, 1)

                if b is not None:
                    t2(0)
                    pe.matmul(lg_ps, ones[0:1, 0:P].bitcast(FP32), rb2_sb[0:1, :].unsqueeze(1).to_broadcast([1, Q, EP]), start=True, stop=False,
                              skip_group_check=True)
                for g in range(Q):
                    if a is not None:
                        mix(a, g + 1)
                        t1(a, g + 2)
                    if b is not None:
                        for q in B_TILES[g]:
                            if q + 1 < Q:
                                t2(q + 1)
                            hidden(q)
                            if q > 0:
                                logits(q - 1)
                if b is not None:
                    logits(Q - 1)
                    pe.wait_ge(oh_ready, b + 1)
                    pe.matmul(rk_ps, tri[:, :], oh[:, :, :, :], start=True, stop=False, skip_group_check=True)
                    pe.matmul(rk_ps, ones[:, :].bitcast(FP32), base[:, :, :].unsqueeze(1).to_broadcast([P, Q, 2, EP]), start=False, stop=False,
                              skip_group_check=True)
                    for g in range(Q - 1):
                        last = pe.matmul(rk_ps[:, g + 1:Q, :, :], ones[:, :],
                                         oh[:, g, :, :].unsqueeze(1).to_broadcast([P, Q - 1 - g, 2, EP]),
                                         start=False, stop=g == Q - 2, skip_group_check=True)
                    last.then_inc(rk_done, 1)

            groups(pe, step)
            pe.wait_ge(step_done, GROUPS * R_STEPS)
            pe.matmul(d_ps[0:P, 0:2 * EP], ones[:, :].bitcast(FP32), base[:, :, :].rearrange("p k e -> p (k e)"), start=True, stop=True).then_inc(cnt_done, 1)

            pe.wait_ge(split_l, E)
            pe.wait_ge(tab_done, 2)
            e_regs = [pe.alloc_register(f"pe_e{i}") for i in range(3)]
            for k in range(2):
                nt, nx, nh = k * (NT * 3 + 2), k * (NT + LEAD), k * NT * 2
                if k == 1:
                    pe.wait_ge(el_done, nt)
                for j in range(2):
                    pe.wait_ge(xe_done, nx + j + 1)
                    transpose(t_ps[j], xe[:, j, :], S).then_inc(et_done, 1)
                with pe.Fori(0, NT // U) as it:
                    x_n, h_n, m = 2, 0, 0
                    for group in range(U // 3):
                        es = experts(pe, e_regs, k, it * (U // 3) + group)
                        for kind, layer, lane in ORDER:
                            if kind == "transpose":
                                if layer == 0:
                                    x_n += 1
                                    pe.wait_ge(xe_done, it * U + (nx + x_n))
                                    rows = xe[:, lane, :]
                                else:
                                    h_n += 1
                                    pe.wait_ge(hs_done, it * (2 * U) + (nh + h_n))
                                    rows = hs[:, lane, :]
                                transpose(t_ps[lane], rows, S).then_inc(et_done, 1)
                                continue
                            m += 1
                            e = es[lane]
                            ready = it * (3 * U) + (nt + m)
                            pe.wait_ge(eh_done, ready)
                            at = e * EW + (layer - 1) * LW
                            product(l_ps[lane][:, 0:F], lane,
                                    lambda c, at=at: we_h[:, bass.ds(at + c * F, F)],
                                    lambda c, at=at: we_l[:, bass.ds(at + c * F, F)],
                                    el_done, ready).then_inc(l_done, 1)


def kernel(**inputs):
    import numpy as np
    import concourse.bacc as bacc
    from concourse.bass_utils import run_bass_kernel_spmd as run

    wqkv = np.asarray(inputs["L0_mix_w_qkv"])
    given = {
        "x": inputs["x"], "src": inputs["src"], "dst": inputs["dst"],
        "w_kv": wqkv[MI:].T, "w_q": wqkv[:MI], "w_oT": np.asarray(inputs["L0_mix_w_out"]).T,
        "b_out": inputs["L0_mix_b_out"], "w_g": inputs["L0_gnn_weight"],
        "a_l": inputs["L0_gnn_attn_l"], "a_r": inputs["L0_gnn_attn_r"],
        "rw1": inputs["L0_ffn_router_w1"], "rb1": inputs["L0_ffn_router_b1"],
        "rw2": inputs["L0_ffn_router_w2"], "rb2": inputs["L0_ffn_router_b2"],
        "ew1": inputs["L0_ffn_expert_w1"], "eb1": inputs["L0_ffn_expert_b1"],
        "ew2": inputs["L0_ffn_expert_w2"], "eb2": inputs["L0_ffn_expert_b2"],
        "ew3": inputs["L0_ffn_expert_w3"], "eb3": inputs["L0_ffn_expert_b3"],
    }
    nc = bacc.Bacc("TRN2", target_bir_lowering=False, num_devices=1)
    arrays, aps = {}, []
    for name, a in given.items():
        a = np.ascontiguousarray(a)
        arrays[f"in_{name}"] = a
        aps.append(nc.dram_tensor(f"in_{name}", a.shape, mybir.dt.from_np(a.dtype), kind="ExternalInput").ap())
    out = nc.dram_tensor("out_x", (N, D), FP32, kind="ExternalOutput").ap()
    gps_layer(nc, *aps, out)
    r = run(nc, [arrays], core_ids=[0])
    return r.results[0]["out_x"]
```
